# Optimizing a Trainium2 kernel written in Bass

```python
import numpy as np
import jax
import jax.numpy as jnp

def _softmax(x, axis=-1):
    return jax.nn.softmax(x, axis=axis)

def _gelu(x):
    return jax.nn.gelu(x, approximate=True)

def _silu(x):
    return jax.nn.silu(x)

def _sigmoid(x):
    return jax.nn.sigmoid(x)

def _layernorm(x, axis=-1, eps=1e-05):
    m = jnp.mean(x, axis=axis, keepdims=True)
    v = jnp.var(x, axis=axis, keepdims=True)
    return (x - m) / jnp.sqrt(v + eps)

def _scatter_add(tgt, idx, src, axis=0):
    return tgt.at[idx].add(src)

def _segment_sum(src, seg, n):
    return jax.ops.segment_sum(src, seg, n)
kernel_name = 'mk_gnn_ffn_d2_gnn_r8_084e46'

def setup_inputs(seed: int=0):
    np.random.seed(seed)
    _w = jnp.asarray

    def _rec_inputs():
        import jax
        import jax.numpy as jnp
        _gk = jax.random.key(seed)
        x = -0.0003713 + 1 * jax.random.normal(jax.random.fold_in(_gk, 1), (6250, 256), jnp.float32)
        _s = jax.random.randint(jax.random.fold_in(_gk, 2), (50000,), 0, 6250, jnp.int32)
        _d = jax.random.randint(jax.random.fold_in(_gk, 3), (50000,), 0, 6250, jnp.int32)
        _loop = jnp.arange(6250, dtype=jnp.int32)
        src = jnp.concatenate([_s, _d, _loop])
        dst = jnp.concatenate([_d, _s, _loop])
        _o = jnp.argsort(dst, stable=True)
        src = src[_o]
        dst = dst[_o]
        edge_type_64 = jax.random.randint(jax.random.fold_in(_gk, 12), (106250,), 0, 64, jnp.int32)
        return (x, src, dst, edge_type_64)
    x, src, dst, edge_type_64 = _rec_inputs()

    def _L0_gnn_setup():
        import jax, jax.numpy as jnp
        import numpy as np
        N, IN_CH, HEADS, OUT_CH, E = (6250, 256, 4, 64, 100000)
        key = jax.random.key(seed)
        k1, k2, k3, k4, k5 = jax.random.split(key, 5)
        x = jax.random.normal(k1, (N, IN_CH), dtype=jnp.float32)
        edge_index = jax.random.randint(k2, (2, E), 0, N, dtype=jnp.int64)
        bw = float(np.sqrt(6.0 / (IN_CH + HEADS * OUT_CH)))
        ba = float(np.sqrt(6.0 / (HEADS + OUT_CH)))
        weight = jax.random.uniform(k3, (IN_CH, HEADS * OUT_CH), jnp.float32, -bw, bw)
        attn_l = jax.random.uniform(k4, (HEADS, OUT_CH), jnp.float32, -ba, ba)
        attn_r = jax.random.uniform(k5, (HEADS, OUT_CH), jnp.float32, -ba, ba)
        return {'x': x, 'edge_index': edge_index, 'weight': weight, 'attn_l': attn_l, 'attn_r': attn_r}
    _L0_gnn_all = _L0_gnn_setup()
    _L0_gnn_in = {k: v for k, v in _L0_gnn_all.items() if k in ('weight', 'attn_l', 'attn_r')}
    del _L0_gnn_all

    def _L0_ffn_setup():
        import jax, jax.numpy as jnp
        import numpy as np
        D_MODEL = 256
        EXPERT_DIM = 512
        NUM_EXPERTS = 8
        TOP_K = 2
        SEQ_LEN = 256
        BATCH = 2
        key = jax.random.key(seed)
        ks = jax.random.split(key, 8)
        s = 0.02
        x = jax.random.normal(ks[0], (SEQ_LEN, BATCH, D_MODEL), dtype=jnp.float32)
        Wg = jax.random.normal(ks[1], (D_MODEL, NUM_EXPERTS), dtype=jnp.float32) * s
        bg = jax.random.normal(ks[2], (NUM_EXPERTS,), dtype=jnp.float32) * s
        bias = jnp.zeros((NUM_EXPERTS,), dtype=jnp.float32)
        W1 = jax.random.normal(ks[3], (NUM_EXPERTS, D_MODEL, EXPERT_DIM), dtype=jnp.float32) * s
        b1 = jax.random.normal(ks[4], (NUM_EXPERTS, EXPERT_DIM), dtype=jnp.float32) * s
        W2 = jax.random.normal(ks[5], (NUM_EXPERTS, EXPERT_DIM, D_MODEL), dtype=jnp.float32) * s
        b2 = jax.random.normal(ks[6], (NUM_EXPERTS, D_MODEL), dtype=jnp.float32) * s
        return {'x': x, 'Wg': Wg, 'bg': bg, 'bias': bias, 'W1': W1, 'b1': b1, 'W2': W2, 'b2': b2}
    _L0_ffn_all = _L0_ffn_setup()
    _L0_ffn_in = {k: v for k, v in _L0_ffn_all.items() if k in ('Wg', 'bg', 'bias', 'W1', 'b1', 'W2', 'b2')}
    del _L0_ffn_all

    def _L1_gnn_setup():
        import jax, jax.numpy as jnp
        import numpy as np
        N_NODES = 6250
        N_EDGES = 62500
        IN_DIM = 256
        HID = 64
        HEADS = 4
        N_REL = 64
        key = jax.random.key(seed)
        ks = jax.random.split(key, 16)
        s = 0.02
        return {'node_features': jax.random.normal(ks[0], (N_NODES, IN_DIM), jnp.float32), 'edge_index': jax.random.randint(ks[1], (2, N_EDGES), 0, N_NODES, jnp.int32), 'edge_relations': jax.random.randint(ks[2], (N_EDGES,), 0, N_REL, jnp.int32), 'query_emb': jax.random.normal(ks[3], (IN_DIM,), jnp.float32), 'Wq': jax.random.normal(ks[4], (IN_DIM, HID * HEADS), jnp.float32) * s, 'bq': jnp.zeros((HID * HEADS,), jnp.float32), 'Wk': jax.random.normal(ks[5], (IN_DIM, HID * HEADS), jnp.float32) * s, 'bk': jnp.zeros((HID * HEADS,), jnp.float32), 'Wv': jax.random.normal(ks[6], (IN_DIM, HID * HEADS), jnp.float32) * s, 'bv': jnp.zeros((HID * HEADS,), jnp.float32), 'rel_w': jax.random.normal(ks[7], (N_REL, HID), jnp.float32) * s, 'Wo': jax.random.normal(ks[8], (HID * HEADS, IN_DIM), jnp.float32) * s, 'bo': jnp.zeros((IN_DIM,), jnp.float32), 'gamma': jnp.ones((IN_DIM,), jnp.float32), 'beta': jnp.zeros((IN_DIM,), jnp.float32)}
    _L1_gnn_all = _L1_gnn_setup()
    _L1_gnn_in = {k: v for k, v in _L1_gnn_all.items() if k in ('query_emb', 'Wq', 'bq', 'Wk', 'bk', 'Wv', 'bv', 'rel_w', 'Wo', 'bo', 'gamma', 'beta')}
    del _L1_gnn_all

    def _L1_ffn_setup():
        import math
        import jax, jax.numpy as jnp
        import numpy as np
        CAPACITY_FACTOR = 1.25
        key = jax.random.key(seed)
        ks = jax.random.split(key, 5)
        B, L, D, F, E = (8, 1024, 256, 1024, 8)
        h = jax.random.normal(ks[0], (B, L, D), dtype=jnp.float32)
        gate_w = jax.random.normal(ks[1], (D, E), dtype=jnp.float32) * 0.02
        gate_b = jnp.zeros((E,), dtype=jnp.float32)
        w1 = jax.random.normal(ks[2], (E, D, F), dtype=jnp.float32) * (1.0 / math.sqrt(D))
        b1 = jnp.zeros((E, F), dtype=jnp.float32)
        w2 = jax.random.normal(ks[3], (E, F, D), dtype=jnp.float32) * (1.0 / math.sqrt(F))
        b2 = jnp.zeros((E, D), dtype=jnp.float32)
        return {'h': h, 'gate_w': gate_w, 'gate_b': gate_b, 'w1': w1, 'b1': b1, 'w2': w2, 'b2': b2}
    _L1_ffn_all = _L1_ffn_setup()
    _L1_ffn_in = {k: v for k, v in _L1_ffn_all.items() if k in ('gate_w', 'gate_b', 'w1', 'b1', 'w2', 'b2')}
    del _L1_ffn_all
    return {'x': x, 'src': src, 'dst': dst, 'edge_type_64': edge_type_64, 'L0_gnn_weight': _L0_gnn_in['weight'], 'L0_gnn_attn_l': _L0_gnn_in['attn_l'], 'L0_gnn_attn_r': _L0_gnn_in['attn_r'], 'L0_ffn_Wg': _L0_ffn_in['Wg'], 'L0_ffn_bg': _L0_ffn_in['bg'], 'L0_ffn_bias': _L0_ffn_in['bias'], 'L0_ffn_W1': _L0_ffn_in['W1'], 'L0_ffn_b1': _L0_ffn_in['b1'], 'L0_ffn_W2': _L0_ffn_in['W2'], 'L0_ffn_b2': _L0_ffn_in['b2'], 'L1_gnn_query_emb': _L1_gnn_in['query_emb'], 'L1_gnn_Wq': _L1_gnn_in['Wq'], 'L1_gnn_bq': _L1_gnn_in['bq'], 'L1_gnn_Wk': _L1_gnn_in['Wk'], 'L1_gnn_bk': _L1_gnn_in['bk'], 'L1_gnn_Wv': _L1_gnn_in['Wv'], 'L1_gnn_bv': _L1_gnn_in['bv'], 'L1_gnn_rel_w': _L1_gnn_in['rel_w'], 'L1_gnn_Wo': _L1_gnn_in['Wo'], 'L1_gnn_bo': _L1_gnn_in['bo'], 'L1_gnn_gamma': _L1_gnn_in['gamma'], 'L1_gnn_beta': _L1_gnn_in['beta'], 'L1_ffn_gate_w': _L1_ffn_in['gate_w'], 'L1_ffn_gate_b': _L1_ffn_in['gate_b'], 'L1_ffn_w1': _L1_ffn_in['w1'], 'L1_ffn_b1': _L1_ffn_in['b1'], 'L1_ffn_w2': _L1_ffn_in['w2'], 'L1_ffn_b2': _L1_ffn_in['b2']}

def reference(x, src, dst, edge_type_64, L0_gnn_weight, L0_gnn_attn_l, L0_gnn_attn_r, L0_ffn_Wg, L0_ffn_bg, L0_ffn_bias, L0_ffn_W1, L0_ffn_b1, L0_ffn_W2, L0_ffn_b2, L1_gnn_query_emb, L1_gnn_Wq, L1_gnn_bq, L1_gnn_Wk, L1_gnn_bk, L1_gnn_Wv, L1_gnn_bv, L1_gnn_rel_w, L1_gnn_Wo, L1_gnn_bo, L1_gnn_gamma, L1_gnn_beta, L1_ffn_gate_w, L1_ffn_gate_b, L1_ffn_w1, L1_ffn_b1, L1_ffn_w2, L1_ffn_b2):
    import jax
    import jax.numpy as jnp

    def _L0_gnn_ref(x, edge_index, weight, attn_l, attn_r):
        import jax, jax.numpy as jnp
        import numpy as np
        N, IN_CH, HEADS, OUT_CH, E = (6250, 256, 4, 64, 100000)
        heads, out_ch = attn_l.shape
        n = x.shape[0]
        xt = jnp.matmul(x, weight).reshape(-1, heads, out_ch)
        row, col = (edge_index[0], edge_index[1])
        alpha_l = jnp.einsum('ehd,hd->eh', xt[row], attn_l)
        alpha_r = jnp.einsum('ehd,hd->eh', xt[col], attn_r)
        alpha = jax.nn.softmax(jax.nn.leaky_relu(alpha_l + alpha_r, 0.01), axis=1)
        tmp = jnp.einsum('nh,nhd->nd', alpha[:n], xt[col[:n]])
        out = jnp.broadcast_to(tmp[:, None, :], (n, heads, out_ch))
        return out.reshape(n, heads * out_ch)

    def _L0_ffn_ref(x, Wg, bg, bias, W1, b1, W2, b2):
        import jax, jax.numpy as jnp
        import numpy as np
        D_MODEL = 256
        EXPERT_DIM = 512
        NUM_EXPERTS = 8
        TOP_K = 2
        SEQ_LEN = 256
        BATCH = 2
        x_flat = x.reshape(-1, D_MODEL)
        gate_logits = x_flat @ Wg + bg + bias
        topk_vals, topk_idx = jax.lax.top_k(gate_logits, TOP_K)
        topk_w = jax.nn.softmax(topk_vals, axis=-1)
        combine = (jax.nn.one_hot(topk_idx, NUM_EXPERTS, dtype=x.dtype) * topk_w[..., None]).sum(axis=1)
        h = jax.nn.relu(jnp.einsum('td,edh->teh', x_flat, W1) + b1)
        y = jnp.einsum('teh,ehd->ted', h, W2) + b2
        out = jnp.einsum('ted,te->td', y, combine)
        return out.reshape(x.shape)

    def _L1_gnn_ref(node_features, edge_index, edge_relations, query_emb, Wq, bq, Wk, bk, Wv, bv, rel_w, Wo, bo, gamma, beta):
        import jax, jax.numpy as jnp
        import numpy as np
        N_NODES = 6250
        N_EDGES = 62500
        IN_DIM = 256
        HID = 64
        HEADS = 4
        N_REL = 64
        N = node_features.shape[0]
        D = rel_w.shape[1]
        H = Wq.shape[1] // D
        enh = node_features + 0.1 * query_emb[None, :]
        Q = (enh @ Wq + bq).reshape(N, H, D)
        K = (enh @ Wk + bk).reshape(N, H, D)
        V = (enh @ Wv + bv).reshape(N, H, D)
        src, dst = (edge_index[0], edge_index[1])
        rel = rel_w[edge_relations]
        mod_k = K[src] + 0.2 * rel[:, None, :]
        scores = jnp.einsum('ehd,ehd->eh', Q[dst], mod_k) / D ** 0.5
        seg_max = jax.ops.segment_max(scores, dst, num_segments=N)
        ex = jnp.exp(scores - seg_max[dst])
        denom = jax.ops.segment_sum(ex, dst, num_segments=N)
        w = ex / denom[dst]
        agg = jax.ops.segment_sum(w[:, :, None] * V[src], dst, num_segments=N)
        deg = jax.ops.segment_sum(jnp.ones((src.shape[0],), jnp.float32), dst, num_segments=N)
        msgs = jnp.where(deg[:, None, None] > 0, agg, V)
        out = msgs.reshape(N, H * D) @ Wo + bo
        x = out + node_features
        mu = jnp.mean(x, axis=-1, keepdims=True)
        var = jnp.var(x, axis=-1, keepdims=True)
        return (x - mu) / jnp.sqrt(var + 1e-05) * gamma + beta

    def _L1_ffn_ref(h, gate_w, gate_b, w1, b1, w2, b2):
        import math
        import jax, jax.numpy as jnp
        import numpy as np
        CAPACITY_FACTOR = 1.25
        B, L, D = h.shape
        E = gate_w.shape[1]
        T = B * L
        C = max(1, math.ceil(CAPACITY_FACTOR * T / E))
        x = h.reshape(T, D)
        logits = x @ gate_w + gate_b
        probs = jax.nn.softmax(logits, axis=-1)
        idx = jnp.argmax(probs, axis=-1)
        prb = jnp.take_along_axis(probs, idx[:, None], axis=1)[:, 0]
        one_hot = jax.nn.one_hot(idx, E, dtype=jnp.float32)
        pos = (jnp.cumsum(one_hot, axis=0) * one_hot).sum(-1).astype(jnp.int32) - 1
        kept = pos < C
        pos_safe = jnp.where(kept, pos, C)
        buf = jnp.zeros((E, C, D), dtype=h.dtype).at[idx, pos_safe].set(x, mode='drop')
        hmid = jax.nn.relu(jnp.einsum('ecd,edf->ecf', buf, w1) + b1[:, None, :])
        ybuf = jnp.einsum('ecf,efd->ecd', hmid, w2) + b2[:, None, :]
        pos_g = jnp.minimum(pos, C - 1)
        y_tok = ybuf[idx, pos_g] * (prb * kept)[:, None]
        y = y_tok.reshape(B, L, D)
        y = jnp.nan_to_num(y, nan=0.0, posinf=10000.0, neginf=-10000.0)
        return y
    edge_index = jnp.stack([src, dst])
    x = x + _L0_gnn_ref(_layernorm(x, axis=-1), edge_index, L0_gnn_weight, L0_gnn_attn_l, L0_gnn_attn_r)
    x = x + _L0_ffn_ref(_layernorm(x, axis=-1)[None], L0_ffn_Wg, L0_ffn_bg, L0_ffn_bias, L0_ffn_W1, L0_ffn_b1, L0_ffn_W2, L0_ffn_b2)[0]
    x = x + _L1_gnn_ref(_layernorm(x, axis=-1), edge_index, edge_type_64, L1_gnn_query_emb, L1_gnn_Wq, L1_gnn_bq, L1_gnn_Wk, L1_gnn_bk, L1_gnn_Wv, L1_gnn_bv, L1_gnn_rel_w, L1_gnn_Wo, L1_gnn_bo, L1_gnn_gamma, L1_gnn_beta)
    x = x + _L1_ffn_ref(_layernorm(x, axis=-1)[None], L1_ffn_gate_w, L1_ffn_gate_b, L1_ffn_w1, L1_ffn_b1, L1_ffn_w2, L1_ffn_b2)[0]
    return x

_drawn_inputs = setup_inputs


def setup_inputs(seed=0):
    import zlib

    import numpy as np

    out = dict(_drawn_inputs(seed))
    spreads = {'L0_ffn_bias': (0.0, 0.1),
     'L1_gnn_bq': (0.0, 0.8),
     'L1_gnn_bk': (0.0, 2.0),
     'L1_gnn_bv': (0.0, 0.446),
     'L1_gnn_bo': (0.0, 0.1),
     'L1_gnn_gamma': (1.0, 0.2),
     'L1_gnn_beta': (0.0, 0.1),
     'L1_ffn_gate_b': (0.0, 0.1),
     'L1_ffn_b1': (0.0, 0.8),
     'L1_ffn_b2': (0.0, 0.8)}
    factors = {'L0_ffn_bg': 4.909,
     'L0_ffn_b1': 8.0,
     'L0_ffn_b2': 4.101,
     'L1_gnn_query_emb': 8.0,
     'L1_gnn_Wq': 8.0,
     'L1_gnn_Wk': 8.0,
     'L1_gnn_Wv': 3.951,
     'L1_gnn_rel_w': 39.973,
     'L1_gnn_Wo': 2.711}
    for name, (base, spread) in spreads.items():
        noise = np.random.default_rng([zlib.crc32(name.encode()), seed]).standard_normal(out[name].shape)
        drawn = base * np.exp(spread * noise) if base else spread * noise
        out[name] = jnp.asarray(drawn.astype(out[name].dtype))
    for name, factor in factors.items():
        out[name] = (out[name] * factor).astype(out[name].dtype)
    return out
```

```python
from contextlib import ExitStack

import concourse.bass as bass
from concourse import mybir

ALU = mybir.AluOpType
ACT = mybir.ActivationFunctionType
AX = mybir.AxisListType
F32 = mybir.dt.float32
BF16 = mybir.dt.bfloat16
I32 = mybir.dt.int32
U32 = mybir.dt.uint32

P = 128
SKIP = 1 << 20


class Shapes:

    def __init__(self, x, dst, rel_w, attn, W1a, W1b):
        self.N, self.D = x.shape
        self.E = dst.shape[0]
        self.RELS, self.HD = rel_w.shape
        self.H = attn.shape[0]
        self.NT = -(-self.N // P)
        self.NP = self.NT * P
        self.U = 7
        self.IT = self.NT // self.U
        self.LAST = self.N - (self.NT - 1) * P
        self.B = 4
        self.GR = 4
        per = self.B * self.GR * P
        self.EC = -(-self.E // per) * self.B * self.GR
        self.EP = self.EC * P
        self.NB = self.EP // self.B
        self.DK = self.D // P
        self.X = W1a.shape[0]
        self.GT = 256
        self.FA = W1a.shape[2]
        self.FB = W1b.shape[2]
        most = (2 * self.N + self.X * (self.GT - 1)) // self.GT
        self.GA = most + most % 2
        self.CAP = -(-5 * self.N // (4 * self.X))
        self.GPE = -(-self.CAP // self.GT)
        self.GB = self.X * self.GPE
        assert self.NT == self.U * self.IT and self.D == self.H * self.HD


def columns(col, n):
    return col[:, :].unsqueeze(2).to_broadcast(n)


class Program:
    def __init__(self, nc, ins, out, stop=None):
        self.nc, self.ins, self.out, self.stop = nc, ins, out, stop
        self.s = Shapes(ins["x"], ins["dst"], ins["L1_gnn_rel_w"], ins["L0_gnn_attn_l"], ins["L0_ffn_W1"], ins["L1_ffn_w1"])
        self.n_sem = 0

    def dram(self, name, shape, dt=F32):
        return self.nc.dram_tensor(name, shape, dt, kind="Internal").ap()


class Stage(ExitStack):

    def __init__(self):
        super().__init__()
        self.semaphores = []


def in_scope(nc, ctx):
    def sb(name, shape, dt=F32):
        return ctx.enter_context(nc.sbuf_tensor(name, shape, dt))

    def psum(name, shape, dt=F32):
        return ctx.enter_context(nc.psum_tensor(name, shape, dt))

    def clear():
        nc.clear_and_free_semaphores(ctx.semaphores)
        nc.all_engine_barrier()

    def sem(name):
        if not ctx.semaphores:
            ctx.callback(clear)
        ctx.semaphores.append(nc.alloc_semaphore(name))
        return ctx.semaphores[-1]

    return sb, psum, sem


def constants(prog, keep):
    nc, s = prog.nc, prog.s
    sb, _, sem = in_scope(nc, keep)
    prog.ident = ident = sb("ident", [P, P])
    prog.below = below = sb("below", [P, P])
    prog.below16 = below16 = sb("below16", [P, P], BF16)
    prog.ones16 = ones16 = sb("ones16", [P, P], BF16)
    prog.bins = bins = sb("bins", [P, P])
    prog.lane = lane = sb("lane", [P, 1])
    prog.node = node = sb("node", [P, s.NT])
    prog.node_i = node_i = sb("node_i", [P, s.NT], I32)
    prog.real = real = sb("real", [P, s.NT])
    with Stage() as ctx:
        _, _, sem = in_scope(nc, ctx)
        made = sem("const_made")
        block = ctx.enter_context(nc.Block())

        @block.gpsimd
        def _(pool):
            nc.gpsimd.memset(ident[:], 0.0)
            nc.gpsimd.memset(below[:], 1.0)
            nc.gpsimd.iota(bins[:], [[1, P]], base=0, channel_multiplier=0, allow_small_or_imprecise_dtypes=True)
            nc.gpsimd.iota(lane[:], [[0, 1]], base=0, channel_multiplier=1, allow_small_or_imprecise_dtypes=True)
            nc.gpsimd.iota(node[:], [[P, s.NT]], base=0, channel_multiplier=1, allow_small_or_imprecise_dtypes=True)
            nc.gpsimd.iota(node_i[:], [[P, s.NT]], base=0, channel_multiplier=1)
            nc.gpsimd.memset(ones16[:], 1.0)
            pool.drain()
            nc.gpsimd.affine_select(out=ident[:], in_=ident[:], compare_op=ALU.not_equal, fill=1.0, base=0,
                                    pattern=[[-1, P]], channel_multiplier=1)
            nc.gpsimd.affine_select(out=below[:], in_=below[:], compare_op=ALU.is_gt, fill=0.0, base=0,
                                    pattern=[[1, P]], channel_multiplier=-1)
            pool.drain()
            nc.gpsimd.tensor_copy(below16[:], below[:])
            nc.gpsimd.tensor_scalar(real[:], node[:], float(s.N), None, ALU.is_lt).then_inc(made, 1)

        @block.vector
        def _(dve):
            dve.wait_ge(made, 1)


def pad_inputs(prog):
    nc, s, ins = prog.nc, prog.s, prog.ins
    prog.xp = xp = prog.dram("x_padded", [s.NP, s.D])
    prog.edges = edges = {k: prog.dram(f"{k}_padded", [s.EP], I32) for k in ("src", "dst", "edge_type_64")}
    fill = {"src": 0, "dst": s.NP + P * 8, "edge_type_64": 0}
    cut = 50
    extra = s.EP - s.E
    with Stage() as ctx:
        sb, _, sem = in_scope(nc, ctx)
        zeros = sb("pad_zeros", [P, s.D])
        pads = sb("pad_edges", [1, 3, extra], I32)
        made, copied = sem("pad_made"), sem("pad_copied")
        block = ctx.enter_context(nc.Block())

        @block.vector
        def _(dve):
            nc.vector.memset(zeros[:], 0.0)
            for j, k in enumerate(edges):
                nc.vector.memset(pads[:, j, :], fill[k])
            dve.drain()
            nc.vector.memset(zeros[0:1, 0:1], 0.0).then_inc(made, 1)

        @block.sync
        def _(sp):
            sp.dma_start(xp[0:s.N, :], ins["x"][:, :]).then_inc(copied, 16)
            for k in edges:
                sp.dma_start(edges[k][0:s.E].rearrange("(a b) -> a b", a=cut),
                             ins[k].rearrange("(a b) -> a b", a=cut)).then_inc(copied, 16)
            sp.wait_ge(made, 1)
            sp.dma_start(xp[s.N:s.NP, :], zeros[0:s.NP - s.N, :]).then_inc(copied, 16)
            for j, k in enumerate(edges):
                sp.dma_start(edges[k][s.E:s.EP].rearrange("(a b) -> a b", a=1), pads[:, j, :]).then_inc(copied, 16)
            sp.wait_ge(copied, 16 * 8)


def project(prog, ctx, tag, tiles, tiles_ready, w, width, used):
    nc, s = prog.nc, prog.s
    sb, psum, sem = in_scope(nc, ctx)
    halves = -(-width // 512)
    turned = psum(f"{tag}_turned", [P, 2, 512])
    out = psum(f"{tag}_out", [P, 2, halves * 512])
    cols = sb(f"{tag}_cols", [P, 2, s.DK * P])
    turned_done, cols_ready, done = sem(f"{tag}_turned_done"), sem(f"{tag}_cols_ready"), sem(f"{tag}_done")

    def before(k):
        return 1 if k == 0 else 2

    def turn(pe, i, k):
        n = i * s.U + k
        pe.wait_ge(tiles_ready, n + 1)
        if not (isinstance(i, int) and n < 2):
            pe.wait_ge(cols_ready, n - before(k) + 1)
        for c in range(s.DK):
            m = nc.tensor.transpose(turned[:, k % 2, c * P:(c + 1) * P], tiles[:, k, c * P:(c + 1) * P], prog.ident[:])
        m.then_inc(turned_done, 1)

    def multiply(pe, i, k):
        n = i * s.U + k
        pe.wait_ge(cols_ready, n + 1)
        if not (isinstance(i, int) and n < 2):
            used(pe, n - before(k) + 1)
        for h in range(halves):
            a, b = h * 512, min(width, h * 512 + 512)
            for c in range(s.DK):
                m = nc.tensor.matmul(out[:, k % 2, a:b], cols[:, k % 2, c * P:(c + 1) * P], w[:, c, a:b],
                                     start=c == 0, stop=c == s.DK - 1)
        m.then_inc(done, 1)

    def copy_cols(act, i, k):
        n = i * s.U + k
        act.wait_ge(turned_done, n + 1)
        if not (isinstance(i, int) and n < 2):
            act.wait_ge(done, n - before(k) + 1)
        nc.scalar.activation(cols[:, k % 2, :], turned[:, k % 2, 0:s.DK * P], ACT.Copy).then_inc(cols_ready, 1)

    def run_pe(pe, i):
        for k in range(s.U):
            turn(pe, i, k)
            if k:
                multiply(pe, i, k - 1)
        multiply(pe, i, s.U - 1)

    return out, done, turned_done, run_pe, copy_cols


def rounds(eng, s, body):
    body(0)
    with eng.Fori(1, s.IT) as i:
        body(i)


class LayerNorm:

    def __init__(self, prog, ctx, tag):
        sb, _, sem = in_scope(prog.nc, ctx)
        self.nc, self.s = prog.nc, prog.s
        self.stats, self.agg = sb(f"{tag}_stats", [P, self.s.U, 6]), sb(f"{tag}_agg", [P, self.s.U, 2])
        self.inverse, self.rstd = sb(f"{tag}_inverse", [P, self.s.U]), sb(f"{tag}_rstd", [P, self.s.U])
        self.var_ready, self.rstd_ready = sem(f"{tag}_var_ready"), sem(f"{tag}_rstd_ready")

    def vector(self, dve, i, src, dst, ready, free=None):
        nc, s = self.nc, self.s
        for k in range(s.U):
            nc.vector.bn_stats(self.stats[:, k, :], src(k))
        dve.drain()
        for k in range(s.U):
            nc.vector.bn_aggr(self.agg[:, k, :], self.stats[:, k, :])
        dve.drain()
        nc.vector.tensor_scalar(self.inverse[:], self.agg[:, :, 1], 1e-5, None, ALU.add)
        dve.drain()
        nc.vector.reciprocal(self.inverse[:], self.inverse[:]).then_inc(self.var_ready, 1)
        dve.wait_ge(self.rstd_ready, i + 1)
        for k in range(s.U):
            if free is not None and not isinstance(i, int):
                dve.wait_ge(free, (i - 1) * s.U + k + 1)
            nc.vector.tensor_scalar(dst(k), src(k), self.agg[:, k, 0:1], self.rstd[:, k:k + 1],
                                    ALU.subtract, ALU.mult).then_inc(ready, 1)

    def vector_end(self, dve):
        dve.drain()
        self.nc.vector.memset(self.inverse[:], 1.0).then_inc(self.var_ready, 1)

    def root(self, act, i):
        act.wait_ge(self.var_ready, i + 1)
        self.nc.scalar.activation(self.rstd[:], self.inverse[:], ACT.Sqrt).then_inc(self.rstd_ready, 1)


def tile_of(buf, n):
    return buf[:, n, :] if isinstance(n, int) else buf[:, bass.ds(n, 1), :].rearrange("p a f -> p (a f)")


def row(ap):
    return ap.rearrange("(a b) -> a b", a=1)


def tile_rows(table, i, s):
    return table.rearrange("(t p) f -> p t f", p=P)[:, bass.ds(i * s.U, s.U), :]


def turn_lists(prog, keep, tag, lists, dt=U32):
    nc = prog.nc
    sbk, _, _ = in_scope(nc, keep)
    m = len(lists)
    cols = sbk(f"{tag}_cols", [P, m, P], dt)
    with Stage() as ctx:
        sb, psum, sem = in_scope(nc, ctx)
        rows = sb(f"{tag}_rows", [P, m, P], I32)
        rows_f = sb(f"{tag}_rows_f", [P, m, P])
        turned = psum(f"{tag}_turned", [P, m, P])
        rows_in, cast, turn_done, ready = sem(f"{tag}_in"), sem(f"{tag}_cast"), sem(f"{tag}_turn"), sem(f"{tag}_ready")
        block = ctx.enter_context(nc.Block())

        @block.sync
        def _(sp):
            for j, l in enumerate(lists):
                sp.dma_start(rows[0:l.shape[0], j, :], l).then_inc(rows_in, 16)

        @block.vector
        def _(dve):
            nc.vector.memset(rows_f[:], 0.0)
            dve.drain()
            dve.wait_ge(rows_in, 16 * m)
            for j, l in enumerate(lists):
                nc.vector.tensor_copy(rows_f[0:l.shape[0], j, :], rows[0:l.shape[0], j, :])
            dve.drain()
            nc.vector.memset(rows[0:1, 0, 0:1], 0).then_inc(cast, 1)
            dve.wait_ge(turn_done, 1)
            nc.vector.tensor_copy(cols[:], turned[:]).then_inc(ready, 1)
            dve.wait_ge(ready, 1)

        @block.tensor
        def _(pe):
            pe.wait_ge(cast, 1)
            for j in range(m):
                t = nc.tensor.transpose(turned[:, j, :], rows_f[:, j, :], prog.ident[:])
            t.then_inc(turn_done, 1)
    return cols


def l0_tables(prog):
    nc, s, ins = prog.nc, prog.s, prog.ins
    H, HD, D = s.H, s.HD, s.D
    W1 = D + 2 * H
    prog.xt_table = xt_table = prog.dram("xt_table", [s.NP, D + H])
    prog.al_table = al_table = prog.dram("al_table", [s.NP, H])
    with Stage() as ctx:
        sb, psum, sem = in_scope(nc, ctx)
        xs = sb("a_x", [P, s.NT, D])
        xn = sb("a_xn", [P, s.U, D])
        w = sb("a_w", [P, s.DK, W1])
        attn = sb("a_attn", [P, 2, D])
        prod = sb("a_prod", [P, 2, s.DK, D])
        rows = sb("a_rows", [P, s.U, W1])
        norm = LayerNorm(prog, ctx, "a")
        x_in, w_in, w_ready, xn_ready, rows_ready, stored = (
            sem("a_x_in"), sem("a_w_in"), sem("a_w_ready"), sem("a_xn_ready"), sem("a_rows_ready"), sem("a_stored"))
        out, done, turned, run_pe, copy_cols = project(prog, ctx, "a", xn, xn_ready, w, W1,
                                                       lambda pe, m: pe.wait_ge(rows_ready, m))
        block = ctx.enter_context(nc.Block())

        @block.sync
        def _(sp):
            sp.dma_start(w[:, :, 0:D], ins["L0_gnn_weight"].rearrange("(c p) f -> p c f", p=P)).then_inc(w_in, 16)
            for j, k in enumerate(("L0_gnn_attn_r", "L0_gnn_attn_l")):
                sp.dma_start(attn[:, j, :], row(ins[k].rearrange("h d -> (h d)")).to_broadcast([P, D])).then_inc(w_in, 16)
            def load(i):
                if not isinstance(i, int):
                    sp.wait_ge(x_in, i * 16)
                sp.dma_start(xs[:, bass.ds(i * s.U, s.U), :], tile_rows(prog.xp, i, s)).then_inc(x_in, 16)

            rounds(sp, s, load)

            def store(i):
                sp.wait_ge(rows_ready, (i + 1) * s.U)
                sp.dma_start(tile_rows(xt_table, i, s), rows[:, :, 0:D + H]).then_inc(stored, 16)
                sp.dma_start(tile_rows(al_table, i, s), rows[:, :, D + H:W1]).then_inc(stored, 16)

            with sp.Fori(0, s.IT) as i:
                store(i)
            sp.wait_ge(stored, 32 * s.IT)

        @block.vector
        def _(dve):
            dve.wait_ge(w_in, 48)
            for j in range(2):
                for c in range(s.DK):
                    nc.vector.tensor_tensor(prod[:, j, c, :], w[:, c, 0:D], attn[:, j, :], ALU.mult)
            dve.drain()
            for j in range(2):
                for c in range(s.DK):
                    nc.vector.tensor_reduce(w[:, c, D + j * H:D + j * H + H],
                                            prod[:, j, c, :].rearrange("p (h d) -> p h d", h=H), AX.X, ALU.add)
            dve.drain()
            nc.vector.tensor_copy(attn[0:1, 0, 0:1], w[0:1, 0, 0:1]).then_inc(w_ready, 1)

            def body(i):
                if not isinstance(i, int):
                    dve.drain()
                dve.wait_ge(x_in, (i + 1) * 16)
                norm.vector(dve, i, lambda k: tile_of(xs, i * s.U + k), lambda k: xn[:, k, :], xn_ready, turned)

            rounds(dve, s, body)
            norm.vector_end(dve)

        @block.tensor
        def _(pe):
            pe.wait_ge(w_ready, 1)
            rounds(pe, s, lambda i: run_pe(pe, i))

        @block.scalar
        def _(act):
            def keep(i, k):
                n = i * s.U + k
                act.wait_ge(done, n + 1)
                if k == 0 and not isinstance(i, int):
                    act.wait_ge(stored, i * 32)
                nc.scalar.activation(rows[:, k, :], out[:, k % 2, 0:W1], ACT.Copy).then_inc(rows_ready, 1)

            def body(i):
                for k in range(s.U):
                    copy_cols(act, i, k)
                    if k:
                        keep(i, k - 1)
                    if k == s.U // 2:
                        norm.root(act, i + 1)
                keep(i, s.U - 1)

            norm.root(act, 0)
            rounds(act, s, body)


def cols_of(buf, i, s):
    return buf[:, bass.ds(i * s.U, s.U)]


def gather(nc, out, table, index, rows):
    return nc.gpsimd.indirect_dma_start(out=out, out_offset=None, in_=table,
                                        in_offset=bass.IndirectOffsetOnAxis(ap=index, axis=0),
                                        bounds_check=rows - 1, oob_is_err=False)


def scatter(nc, table, index, data, rows):
    return nc.gpsimd.indirect_dma_start(out=table, out_offset=bass.IndirectOffsetOnAxis(ap=index, axis=0),
                                        in_=data, in_offset=None, bounds_check=rows - 1, oob_is_err=False)


def l0_attend(prog, keep):
    nc, s, ins = prog.nc, prog.s, prog.ins
    H, HD, D, U = s.H, s.HD, s.D, s.U
    sbk, _, _ = in_scope(nc, keep)
    prog.x = xs = sbk("x_now", [P, s.NT, D])
    prog.logits = logits = sbk("logits", [P, s.NT, s.X])
    prog.xn_table = xn_table = prog.dram("xn_table", [s.NP, D])
    with Stage() as ctx:
        sb, psum, sem = in_scope(nc, ctx)
        ends = turn_lists(prog, ctx, "ends", [prog.edges[k][0:s.NP].rearrange("(t p) -> t p", p=P)
                                              for k in ("dst", "src")])
        ends_now = sb("b_ends_now", [P, 2, U], U32)
        xt = sb("b_xt", [P, U, D + H])
        al = sb("b_al", [P, U, H])
        z = sb("b_z", [P, U, H])
        zs = sb("b_zs", [P, U, H])
        top = sb("b_top", [P, U])
        ez = sb("b_ez", [P, U, H])
        total = sb("b_total", [P, U])
        prod = sb("b_prod", [P, U, D])
        tmp = sb("b_tmp", [P, U, HD])
        xn = sb("b_xn", [P, U, D])
        w = sb("b_w", [P, s.DK, s.X])
        bias = sb("b_bias", [P, 2, s.X])
        norm = LayerNorm(prog, ctx, "b")
        x_in, w_in = sem("b_x_in"), sem("b_w_in")
        rows_in = [sem(f"b_rows_in{k}") for k in range(U)]
        shifted, exp_done, rows_used = sem("b_shifted"), sem("b_exp_done"), sem("b_rows_used")
        xn_ready, kept, stored, ended = sem("b_xn_ready"), sem("b_kept"), sem("b_stored"), sem("b_ended")
        out, done, turned, run_pe, copy_cols = project(prog, ctx, "b", xn, xn_ready, w, s.X,
                                                       lambda pe, m: pe.wait_ge(kept, m))
        block = ctx.enter_context(nc.Block())

        @block.sync
        def _(sp):
            sp.dma_start(w[:], ins["L0_ffn_Wg"].rearrange("(c p) f -> p c f", p=P)).then_inc(w_in, 16)
            for j, k in enumerate(("L0_ffn_bg", "L0_ffn_bias")):
                sp.dma_start(bias[:, j, :], row(ins[k]).to_broadcast([P, s.X])).then_inc(w_in, 16)

            def body(i):
                if not isinstance(i, int):
                    sp.wait_ge(x_in, i * 16)
                sp.dma_start(xs[:, bass.ds(i * U, U), :], tile_rows(prog.xp, i, s)).then_inc(x_in, 16)
                sp.wait_ge(xn_ready, (i + 1) * U)
                sp.dma_start(tile_rows(xn_table, i, s), xn[:]).then_inc(stored, 16)

            rounds(sp, s, body)
            sp.wait_ge(stored, 16 * s.IT)

        @block.gpsimd
        def _(pool):
            def body(i):
                if not isinstance(i, int):
                    pool.wait_ge(rows_used, i)
                for j in range(2):
                    nc.gpsimd.tensor_copy(ends_now[:, j, :], ends[:, j, bass.ds(i * U, U)])
                pool.drain()
                for k in range(U):
                    gather(nc, xt[:, k, :], prog.xt_table, ends_now[:, 0, k:k + 1], s.NP).then_inc(rows_in[k], 16)
                    gather(nc, al[:, k, :], prog.al_table, ends_now[:, 1, k:k + 1], s.NP).then_inc(rows_in[k], 16)

            rounds(pool, s, body)

        @block.vector
        def _(dve):
            def body(i):
                if not isinstance(i, int):
                    dve.drain()
                for k in range(U):
                    dve.wait_ge(rows_in[k], (i + 1) * 32)
                nc.vector.tensor_tensor(z[:], xt[:, :, D:D + H], al[:], ALU.add)
                dve.drain()
                nc.vector.scalar_tensor_tensor(out=zs[:], in0=z[:], scalar=0.01, in1=z[:], op0=ALU.mult, op1=ALU.max)
                dve.drain()
                nc.vector.tensor_reduce(top[:], zs[:], AX.X, ALU.max)
                dve.drain()
                nc.vector.tensor_tensor(zs[:], zs[:], columns(top, [P, U, H]), ALU.subtract).then_inc(shifted, 1)
                dve.wait_ge(exp_done, i + 1)
                nc.vector.tensor_reduce(total[:], ez[:], AX.X, ALU.add)
                dve.drain()
                nc.vector.reciprocal(total[:], total[:])
                dve.drain()
                nc.vector.tensor_tensor(ez[:], ez[:], columns(total, [P, U, H]), ALU.mult)
                dve.drain()
                nc.vector.tensor_tensor(prod[:].rearrange("p u (h d) -> p u h d", h=H),
                                        xt[:, :, 0:D].rearrange("p u (h d) -> p u h d", h=H),
                                        ez[:].unsqueeze(3).to_broadcast([P, U, H, HD]), ALU.mult).then_inc(rows_used, 1)
                dve.drain()
                nc.vector.tensor_reduce(tmp[:], prod[:].rearrange("p u (h d) -> p u d h", h=H), AX.X, ALU.add)
                dve.drain()
                if not isinstance(i, int):
                    dve.wait_ge(stored, i * 16)
                dve.wait_ge(x_in, (i + 1) * 16)
                now = xs[:, bass.ds(i * U, U), :].rearrange("p u (h d) -> p u h d", h=H)
                nc.vector.tensor_tensor(now, now, tmp[:].unsqueeze(2).to_broadcast([P, U, H, HD]), ALU.add)
                dve.drain()
                norm.vector(dve, i, lambda k: tile_of(xs, i * U + k), lambda k: xn[:, k, :], xn_ready, turned)

            rounds(dve, s, body)
            norm.vector_end(dve)
            dve.wait_ge(w_in, 48)
            dve.wait_ge(kept, s.NT)
            for j in range(2):
                nc.vector.tensor_tensor(logits[:], logits[:], bias[:, j, :].unsqueeze(1).to_broadcast([P, s.NT, s.X]), ALU.add)
                dve.drain()
            nc.vector.memset(top[:], 0.0).then_inc(ended, 1)

        @block.tensor
        def _(pe):
            pe.wait_ge(w_in, 48)
            rounds(pe, s, lambda i: run_pe(pe, i))

        @block.scalar
        def _(act):
            def expo(i):
                act.wait_ge(shifted, i + 1)
                nc.scalar.activation(ez[:], zs[:], ACT.Exp).then_inc(exp_done, 1)

            def keep_logits(i, k):
                n = i * U + k
                act.wait_ge(done, n + 1)
                nc.scalar.activation(tile_of(logits, n), out[:, k % 2, 0:s.X], ACT.Copy).then_inc(kept, 1)

            def body(i):
                expo(i)
                norm.root(act, i)
                for k in range(U):
                    copy_cols(act, i, k)
                    if k:
                        keep_logits(i, k - 1)
                keep_logits(i, U - 1)

            rounds(act, s, body)


def route(prog, keep, tag, experts, groups):
    nc, s = prog.nc, prog.s
    X, NT, U, GT = s.X, s.NT, s.U, s.GT
    sbk, _, _ = in_scope(nc, keep)
    weight = [sbk(f"{tag}_weight{j}", [P, NT]) for j in range(experts)]
    slot = [sbk(f"{tag}_slot{j}", [P, NT], I32) for j in range(experts)]
    of_group = sbk(f"{tag}_of_group", [1, P], I32)
    slots = groups * GT
    halves = groups * GT // P
    slot_node = prog.dram(f"{tag}_slot_node", [slots, 1], I32)
    with Stage() as ctx:
        sb, psum, sem = in_scope(nc, ctx)
        L = sb(f"{tag}_L", [P, NT, X])
        eq = sb(f"{tag}_eq", [P, NT, X])
        hot = [sb(f"{tag}_hot{j}", [P, X, NT]) for j in range(experts)]
        hot16 = sb(f"{tag}_hot16", [P, X, NT], BF16)
        best = [sb(f"{tag}_best{j}", [P, NT]) for j in range(2)]
        which = sb(f"{tag}_which", [P, NT])
        ex = sb(f"{tag}_ex", [P, NT])
        edge = sb(f"{tag}_edge", [P, X, NT])
        upto = sb(f"{tag}_upto", [P, X, NT])
        place = sb(f"{tag}_place", [P, X, NT])
        tot_i = sb(f"{tag}_tot_i", [P, X], I32)
        ng = sb(f"{tag}_ng", [P, X])
        endg = sb(f"{tag}_endg", [P, X])
        base = sb(f"{tag}_base", [P, X])
        pos = sb(f"{tag}_pos", [P, NT])
        keepm = sb(f"{tag}_keepm", [P, NT])
        scat = [sb(f"{tag}_scat{j}", [P, NT], U32) for j in range(experts)]
        now = sb(f"{tag}_now", [P, experts, U], U32)
        now_node = sb(f"{tag}_now_node", [P, U], I32)
        zeros = sb(f"{tag}_zeros", [P, slots // P], I32)
        gcmp = sb(f"{tag}_gcmp", [1, P, X])
        gex = sb(f"{tag}_gex", [1, P])
        tiles_ps = psum(f"{tag}_tiles_ps", [P, 512])
        below_ps = psum(f"{tag}_below_ps", [P, 512])
        hot_ready, counted, exp_in, exp_done = (sem(f"{tag}_hot_ready"), sem(f"{tag}_counted"), sem(f"{tag}_exp_in"),
                                                sem(f"{tag}_exp_done"))
        placed, zeroed, zero_ready, scattered = (sem(f"{tag}_placed"), sem(f"{tag}_zeroed"), sem(f"{tag}_zero_ready"),
                                                 sem(f"{tag}_scattered"))
        block = ctx.enter_context(nc.Block())
        bins8 = prog.bins[:, 0:X].unsqueeze(1).to_broadcast([P, NT, X])

        @block.sync
        def _(sp):
            sp.wait_ge(zero_ready, 1)
            sp.dma_start(slot_node.rearrange("(p c) a -> p (c a)", p=P), zeros[:]).then_inc(zeroed, 16)

        @block.tensor
        def _(pe):
            pe.wait_ge(hot_ready, 1)
            flat = hot16[:].rearrange("p e t -> p (e t)")
            nc.tensor.matmul(tiles_ps[:, 0:X * NT], prog.ones16[:], flat, start=True, stop=True)
            nc.tensor.matmul(below_ps[:, 0:X * NT], prog.below16[:], flat, start=True, stop=True).then_inc(counted, 1)

        @block.scalar
        def _(act):
            act.wait_ge(exp_in, 1)
            if experts == 2:
                nc.scalar.activation(pos[:], best[1][:], ACT.Exp).then_inc(exp_done, 1)
            else:
                nc.scalar.activation(eq[:], L[:], ACT.Exp).then_inc(exp_done, 1)

        @block.vector
        def _(dve):
            v = nc.vector

            def step(ins):
                dve.drain()
                return ins

            def by_tile(t):
                return t[:].rearrange("p e t -> p t e")

            def per_expert(t):
                return t[:, :].unsqueeze(2).to_broadcast([P, X, NT])

            v.memset(zeros[:], 0).then_inc(zero_ready, 1)
            v.memset(edge[:], 1.0)
            v.tensor_copy(L[:], prog.logits[:])
            step(None)
            v.memset(edge[:, :, 0:1], 0.0)
            for j in range(experts):
                step(v.tensor_reduce(best[j][:], L[:], AX.X, ALU.max))
                step(v.tensor_tensor(eq[:], L[:], columns(best[j], [P, NT, X]), ALU.not_equal))
                step(v.scalar_tensor_tensor(out=eq[:], in0=eq[:], scalar=float(X), in1=bins8, op0=ALU.mult, op1=ALU.add))
                step(v.tensor_reduce(which[:], eq[:], AX.X, ALU.min))
                step(v.tensor_tensor(eq[:], bins8, columns(which, [P, NT, X]), ALU.is_equal))
                step(v.tensor_tensor(by_tile(hot[j]), eq[:], columns(prog.real, [P, NT, X]), ALU.mult))
                if experts == 2 and j == 0:
                    step(v.scalar_tensor_tensor(out=L[:], in0=eq[:], scalar=-3e38, in1=L[:], op0=ALU.mult, op1=ALU.add))
            if experts == 2:
                step(v.tensor_tensor(hot16[:], hot[0][:], hot[1][:], ALU.add))
            else:
                step(v.tensor_copy(hot16[:], hot[0][:]))
            v.memset(now_node[:], 0).then_inc(hot_ready, 1)
            if experts == 2:
                v.tensor_tensor(best[1][:], best[1][:], best[0][:], ALU.subtract).then_inc(exp_in, 1)
                dve.wait_ge(exp_done, 1)
                step(v.tensor_scalar(ex[:], pos[:], 1.0, None, ALU.add))
                step(v.reciprocal(weight[0][:], ex[:]))
                step(v.tensor_tensor(weight[1][:], pos[:], weight[0][:], ALU.mult))
            else:
                v.tensor_tensor(L[:], L[:], columns(best[0], [P, NT, X]), ALU.subtract).then_inc(exp_in, 1)
                dve.wait_ge(exp_done, 1)
                step(v.tensor_reduce(ex[:], eq[:], AX.X, ALU.add))
                step(v.reciprocal(weight[0][:], ex[:]))
            dve.wait_ge(counted, 1)
            flat = lambda t: t[:].rearrange("p e t -> p (e t)")
            step(v.tensor_tensor_scan(flat(upto), flat(edge), tiles_ps[:, 0:X * NT], 0.0, ALU.mult, ALU.add))
            step(v.tensor_tensor(flat(place), flat(upto), tiles_ps[:, 0:X * NT], ALU.subtract))
            step(v.tensor_tensor(flat(place), flat(place), below_ps[:, 0:X * NT], ALU.add))
            if experts == 2:
                step(v.tensor_scalar(tot_i[:], upto[:, :, NT - 1], float(GT - 1), None, ALU.add))
                step(v.tensor_scalar(tot_i[:], tot_i[:], GT.bit_length() - 1, None, ALU.arith_shift_right))
                step(v.tensor_copy(ng[:], tot_i[:]))
                step(v.tensor_tensor_scan(endg[:], ng[:], ng[:], 0.0, ALU.add, ALU.bypass))
            else:
                step(v.memset(ng[:], float(s.GPE)))
                step(v.tensor_tensor_scan(endg[:], ng[:], ng[:], 0.0, ALU.add, ALU.bypass))
            step(v.tensor_tensor(base[:], endg[:], ng[:], ALU.subtract))
            step(v.tensor_scalar(base[:], base[:], float(GT), None, ALU.mult))
            if experts == 2:
                step(v.tensor_tensor(place[:], place[:], per_expert(base), ALU.add))
            for j in range(experts):
                step(v.tensor_tensor(upto[:], hot[j][:], place[:], ALU.mult))
                step(v.tensor_reduce(pos[:], by_tile(upto), AX.X, ALU.add))
                if experts == 2:
                    step(v.tensor_copy(slot[j][:], pos[:]))
                    step(v.tensor_scalar(ex[:], prog.real[:], -float(SKIP), float(SKIP), ALU.mult, ALU.add))
                    step(v.tensor_tensor(scat[j][:], ex[:], pos[:], ALU.add))
                else:
                    step(v.tensor_scalar(keepm[:], pos[:], float(s.CAP), None, ALU.is_lt))
                    step(v.tensor_tensor(weight[0][:], weight[0][:], keepm[:], ALU.mult))
                    step(v.tensor_tensor(keepm[:], keepm[:], prog.real[:], ALU.mult))
                    step(v.tensor_scalar(pos[:], pos[:], float(s.CAP - 1), None, ALU.min))
                    step(v.tensor_tensor(upto[:], hot[j][:], per_expert(base), ALU.mult))
                    step(v.tensor_reduce(ex[:], by_tile(upto), AX.X, ALU.add))
                    step(v.tensor_tensor(pos[:], pos[:], ex[:], ALU.add))
                    step(v.tensor_copy(slot[j][:], pos[:]))
                    step(v.tensor_scalar(ex[:], keepm[:], -float(SKIP), float(SKIP), ALU.mult, ALU.add))
                    step(v.tensor_tensor(scat[j][:], ex[:], pos[:], ALU.add))
            step(v.tensor_tensor(gcmp[:], prog.bins[0:1, :].unsqueeze(2).to_broadcast([1, P, X]),
                                 endg[0:1, :].unsqueeze(1).to_broadcast([1, P, X]), ALU.is_ge))
            step(v.tensor_reduce(gex[:], gcmp[:], AX.X, ALU.add))
            v.tensor_scalar(of_group[:], gex[:], float(X - 1), None, ALU.min).then_inc(placed, 1)

        @block.gpsimd
        def _(pool):
            pool.wait_ge(placed, 1)
            pool.wait_ge(zeroed, 16)

            def body(i):
                if not isinstance(i, int):
                    pool.wait_ge(scattered, i * 16 * U * experts)
                for j in range(experts):
                    nc.gpsimd.tensor_copy(now[:, j, :], cols_of(scat[j], i, s))
                nc.gpsimd.tensor_copy(now_node[:], cols_of(prog.node_i, i, s))
                pool.drain()
                for k in range(U):
                    for j in range(experts):
                        scatter(nc, slot_node, now[:, j, k:k + 1], now_node[:, k:k + 1], slots).then_inc(scattered, 16)

            rounds(pool, s, body)
            pool.wait_ge(scattered, 16 * U * experts * s.IT)
    return weight, slot, slot_node, of_group


def mlp(prog, tag, table, slot_node, of_group, groups, F, w1, b1, w2, b2):
    nc, s = prog.nc, prog.s
    D, DK, GT, X = s.D, s.DK, s.GT, s.X
    FC = F // P
    SUB = GT // P
    sub_all = groups * SUB
    y_table = prog.dram(f"{tag}_y", [groups * GT, D])
    with Stage() as ctx:
        sb, psum, sem = in_scope(nc, ctx)
        node_rows = sb(f"{tag}_node_rows", [P, P], I32)
        node_f = sb(f"{tag}_node_f", [P, P])
        nodes = sb(f"{tag}_nodes", [P, P], U32)
        b1_rows = sb(f"{tag}_b1_rows", [P, P])
        b1_cols = sb(f"{tag}_b1_cols", [P, P])
        nodes_now = sb(f"{tag}_nodes_now", [P, 2, SUB], U32)
        xg = sb(f"{tag}_xg", [P, 2, SUB, D])
        xT = sb(f"{tag}_xT", [P, 2, DK * GT])
        w1s = sb(f"{tag}_w1s", [P, 2, DK, F])
        w2s = sb(f"{tag}_w2s", [P, 2, FC, D])
        b2s = sb(f"{tag}_b2s", [P, 2, D])
        hT = sb(f"{tag}_hT", [P, 2, FC, GT])
        ys = sb(f"{tag}_ys", [P, 2, SUB, D])
        turned = psum(f"{tag}_turned", [P, 2, 512])
        hid = psum(f"{tag}_hid", [P, 4, 512])
        yp = psum(f"{tag}_yp", [P, 2, 512])
        lists_in, lists_f, lists_T, lists_ready = (sem(f"{tag}_lists_in"), sem(f"{tag}_lists_f"), sem(f"{tag}_lists_T"),
                                                   sem(f"{tag}_lists_ready"))
        w_in = [sem(f"{tag}_w_in{j}") for j in range(2)]
        x_in = [sem(f"{tag}_x_in{j}") for j in range(2)]
        y_out = [sem(f"{tag}_y_out{j}") for j in range(2)]
        turn_done, xT_ready, hid_done, h_ready = (sem(f"{tag}_turn_done"), sem(f"{tag}_xT_ready"), sem(f"{tag}_hid_done"),
                                                  sem(f"{tag}_h_ready"))
        y_done, y_ready, cleared = sem(f"{tag}_y_done"), sem(f"{tag}_y_ready"), sem(f"{tag}_cleared")
        block = ctx.enter_context(nc.Block())

        def pairs(eng, body):
            for j in range(2):
                body(0, j)
            with eng.Fori(1, groups // 2) as i:
                for j in range(2):
                    body(i, j)

        def later(i):
            return not isinstance(i, int)

        @block.sync
        def _(sp):
            sp.dma_start(node_rows[0:sub_all, :], slot_node.rearrange("(c p) a -> c (p a)", p=P)).then_inc(lists_in, 16)
            sp.wait_ge(cleared, 1)
            sp.dma_start(b1_rows[0:X * FC, :], b1.rearrange("e (c p) -> (e c) p", p=P)).then_inc(lists_in, 16)

            def store(i, j):
                sp.dma_start(y_table[bass.ds((i * 2 + j) * GT, GT), :].rearrange("(c p) f -> p c f", p=P),
                             ys[:, j]).then_inc(y_out[j], 16)

            def body(i, j):
                e = sp.value_load(of_group[0:1, bass.ds(i * 2 + j, 1)], min_val=0, max_val=X - 1)
                if later(i):
                    sp.wait_ge(y_ready, i * 2 + j - 1)
                    store(i - 1, j)
                sp.dma_start(w1s[:, j], w1[bass.ds(e, 1)].rearrange("a (c p) f -> p (a c) f", p=P)).then_inc(w_in[j], 16)
                sp.dma_start(w2s[:, j], w2[bass.ds(e, 1)].rearrange("a (c p) f -> p (a c) f", p=P)).then_inc(w_in[j], 16)
                sp.dma_start(b2s[:, j], b2[bass.ds(e, 1), :].to_broadcast([P, D])).then_inc(w_in[j], 16)

            pairs(sp, body)
            for j in range(2):
                sp.wait_ge(y_ready, groups - 1 + j)
                store(groups // 2 - 1, j)
            for j in range(2):
                sp.wait_ge(y_out[j], 16 * (groups // 2))

        @block.gpsimd
        def _(pool):
            pool.wait_ge(lists_ready, 1)

            def body(i, j):
                if later(i):
                    pool.wait_ge(turn_done, i * 2 + j - 1)
                nc.gpsimd.tensor_copy(nodes_now[:, j, :], nodes[:, bass.ds((i * 2 + j) * SUB, SUB)])
                pool.drain()
                for c in range(SUB):
                    gather(nc, xg[:, j, c, :], table, nodes_now[:, j, c:c + 1], s.NP).then_inc(x_in[j], 16)

            pairs(pool, body)

        @block.tensor
        def _(pe):
            pe.wait_ge(lists_f, 1)
            nc.tensor.transpose(turned[:, 0, 0:P], node_f[:], prog.ident[:])
            nc.tensor.transpose(turned[:, 1, 0:P], b1_rows[:], prog.ident[:]).then_inc(lists_T, 1)
            pe.wait_ge(lists_ready, 1)

            def turn(i, j):
                pe.wait_ge(x_in[j], (i + 1) * 16 * SUB)
                if later(i):
                    pe.wait_ge(xT_ready, i * 2 + j - 1)
                for c in range(DK):
                    for t in range(SUB):
                        m = nc.tensor.transpose(turned[:, j, c * GT + t * P:c * GT + (t + 1) * P],
                                                xg[:, j, t, c * P:(c + 1) * P], prog.ident[:])
                m.then_inc(turn_done, 1)

            def first(i, j):
                g = i * 2 + j
                pe.wait_ge(xT_ready, g + 1)
                pe.wait_ge(w_in[j], (i + 1) * 48)
                for f in range(FC):
                    if later(i) or j * FC + f >= 4:
                        pe.wait_ge(h_ready, g * FC + f - 3)
                    for c in range(DK):
                        m = nc.tensor.matmul(hid[:, f % 4, 0:GT], w1s[:, j, c, f * P:(f + 1) * P],
                                             xT[:, j, c * GT:(c + 1) * GT], start=c == 0, stop=c == DK - 1)
                    m.then_inc(hid_done, 1)

            def second(i, j):
                g = i * 2 + j
                pe.wait_ge(h_ready, (g + 1) * FC)
                for t in range(SUB):
                    if later(i) or j * SUB + t >= 2:
                        pe.wait_ge(y_ready, g)
                    for f in range(FC):
                        m = nc.tensor.matmul(yp[:, t, 0:D], hT[:, j, f, t * P:(t + 1) * P], w2s[:, j, f, :],
                                             start=f == 0, stop=f == FC - 1)
                    m.then_inc(y_done, 1)

            def body(i, j):
                turn(i, j)
                if later(i) or j:
                    second(*((i, 0) if j else (i - 1, 1)))
                first(i, j)

            pairs(pe, body)
            second(groups // 2 - 1, 1)

        @block.scalar
        def _(act):
            act.wait_ge(lists_ready, 1)

            def body(i, j):
                g = i * 2 + j
                e = act.value_load(of_group[0:1, bass.ds(g, 1)], min_val=0, max_val=X - 1)
                act.wait_ge(turn_done, g + 1)
                if later(i):
                    act.wait_ge(hid_done, (g - 1) * FC)
                nc.scalar.activation(xT[:, j, :], turned[:, j, :], ACT.Copy).then_inc(xT_ready, 1)
                if later(i):
                    act.wait_ge(y_done, (g - 1) * SUB)
                for f in range(FC):
                    act.wait_ge(hid_done, g * FC + f + 1)
                    nc.scalar.activation(hT[:, j, f, :], hid[:, f % 4, 0:GT], ACT.Relu,
                                         bias=b1_cols[:, bass.ds(e * FC + f, 1)]).then_inc(h_ready, 1)

            pairs(act, body)

        @block.vector
        def _(dve):
            nc.vector.memset(node_f[:], 0.0)
            nc.vector.memset(b1_rows[:], 0.0).then_inc(cleared, 1)
            dve.drain()
            dve.wait_ge(lists_in, 32)
            nc.vector.tensor_copy(node_f[0:sub_all, :], node_rows[0:sub_all, :]).then_inc(lists_f, 1)
            dve.wait_ge(lists_T, 1)
            nc.vector.tensor_copy(nodes[:], turned[:, 0, 0:P])
            nc.vector.tensor_copy(b1_cols[:], turned[:, 1, 0:P])
            dve.drain()
            nc.vector.memset(node_f[:], 0.0).then_inc(lists_ready, 1)

            def body(i, j):
                g = i * 2 + j
                dve.wait_ge(w_in[j], (i + 1) * 48)
                if later(i):
                    dve.wait_ge(y_out[j], i * 16)
                for t in range(SUB):
                    dve.wait_ge(y_done, g * SUB + t + 1)
                    m = nc.vector.tensor_tensor(ys[:, j, t, :], yp[:, t, 0:D], b2s[:, j, :], ALU.add)
                m.then_inc(y_ready, 1)

            pairs(dve, body)
    return y_table


def l1_tables(prog, weight, slot, y_table):
    nc, s, ins = prog.nc, prog.s, prog.ins
    H, HD, D, U = s.H, s.HD, s.D, s.U
    HV = HD + 1
    KV = D + H * HV
    xs = prog.x
    prog.q_table = q_table = prog.dram("q_table", [s.NP, D])
    prog.kv_table = kv_table = prog.dram("kv_table", [s.NP, KV])
    prog.nx_table = nx_table = prog.dram("nx_table", [s.NP, 2 * D])
    scale = HD ** -0.5
    with Stage() as ctx:
        sb, psum, sem = in_scope(nc, ctx)
        slot_now = sb("d_slot_now", [P, 2, U], U32)
        y = sb("d_y", [P, 2, U, D])
        xn = sb("d_xn", [P, U, D])
        enh = sb("d_enh", [P, U, D])
        w = sb("d_w", [P, s.DK, 3 * D])
        bias = sb("d_bias", [P, 3 * D])
        query = sb("d_query", [P, D])
        rows = sb("d_rows", [P, U, D + KV])
        norm = LayerNorm(prog, ctx, "d")
        y_in = [sem(f"d_y_in{k}") for k in range(U)]
        w_in, w_ready, summed = sem("d_w_in"), sem("d_w_ready"), sem("d_summed")
        xn_ready, enh_ready, rows_ready, stored = sem("d_xn_ready"), sem("d_enh_ready"), sem("d_rows_ready"), sem("d_stored")
        out, done, turned, run_pe, copy_cols = project(prog, ctx, "d", enh, enh_ready, w, 3 * D,
                                                       lambda pe, m: pe.wait_ge(rows_ready, m))
        block = ctx.enter_context(nc.Block())

        @block.sync
        def _(sp):
            for j, k in enumerate(("q", "k", "v")):
                sp.dma_start(w[:, :, j * D:(j + 1) * D], ins[f"L1_gnn_W{k}"].rearrange("(c p) f -> p c f", p=P)).then_inc(w_in, 16)
                sp.dma_start(bias[:, j * D:(j + 1) * D], row(ins[f"L1_gnn_b{k}"]).to_broadcast([P, D])).then_inc(w_in, 16)
            sp.dma_start(query[:], row(ins["L1_gnn_query_emb"]).to_broadcast([P, D])).then_inc(w_in, 16)

            def body(i):
                sp.wait_ge(xn_ready, (i + 1) * U)
                nx = tile_rows(nx_table, i, s)
                sp.dma_start(nx[:, :, 0:D], xn[:]).then_inc(stored, 16)
                sp.dma_start(nx[:, :, D:2 * D], xs[:, bass.ds(i * U, U), :]).then_inc(stored, 16)
                sp.wait_ge(rows_ready, (i + 1) * U)
                sp.dma_start(tile_rows(q_table, i, s), rows[:, :, 0:D]).then_inc(stored, 16)
                sp.dma_start(tile_rows(kv_table, i, s), rows[:, :, D:D + KV]).then_inc(stored, 16)

            rounds(sp, s, body)
            sp.wait_ge(stored, 64 * s.IT)

        @block.gpsimd
        def _(pool):
            def body(i):
                if not isinstance(i, int):
                    pool.wait_ge(summed, i)
                for j in range(2):
                    nc.gpsimd.tensor_copy(slot_now[:, j, :], cols_of(slot[j], i, s).bitcast(U32))
                pool.drain()
                for k in range(U):
                    for j in range(2):
                        gather(nc, y[:, j, k, :], y_table, slot_now[:, j, k:k + 1], s.GA * s.GT).then_inc(y_in[k], 16)

            rounds(pool, s, body)

        @block.vector
        def _(dve):
            nc.vector.memset(rows[:], 1.0)
            dve.drain()
            dve.wait_ge(w_in, 16 * 7)
            nc.vector.tensor_scalar(w[:, :, 0:D], w[:, :, 0:D], scale, None, ALU.mult)
            nc.vector.tensor_scalar(bias[:, 0:D], bias[:, 0:D], scale, None, ALU.mult)
            nc.vector.tensor_scalar(query[:], query[:], 0.1, None, ALU.mult)
            dve.drain()
            nc.vector.memset(enh[:], 0.0).then_inc(w_ready, 1)
            dve.wait_ge(w_ready, 1)

            def gathered(i):
                for k in range(U):
                    dve.wait_ge(y_in[k], (i + 1) * 32)
                for k in range(U):
                    n = i * U + k
                    x = tile_of(xs, n)
                    wt = [weight[j][:, n:n + 1] if isinstance(n, int) else weight[j][:, bass.ds(n, 1)] for j in range(2)]
                    nc.vector.scalar_tensor_tensor(out=x, in0=y[:, 0, k, :], scalar=wt[0], in1=x, op0=ALU.mult, op1=ALU.add)
                dve.drain()
                for k in range(U):
                    n = i * U + k
                    x = tile_of(xs, n)
                    wt = [weight[j][:, n:n + 1] if isinstance(n, int) else weight[j][:, bass.ds(n, 1)] for j in range(2)]
                    m = nc.vector.scalar_tensor_tensor(out=x, in0=y[:, 1, k, :], scalar=wt[1], in1=x, op0=ALU.mult, op1=ALU.add)
                m.then_inc(summed, 1)

            def keep_rows(i):
                for k in range(U):
                    n = i * U + k
                    dve.wait_ge(done, n + 1)
                    nc.vector.tensor_tensor(rows[:, k, 0:2 * D], out[:, k % 2, 0:2 * D], bias[:, 0:2 * D], ALU.add)
                    nc.vector.tensor_tensor(rows[:, k, 2 * D:D + KV].rearrange("p (h d) -> p h d", h=H)[:, :, 0:HD],
                                            out[:, k % 2, 2 * D:3 * D].rearrange("p (h d) -> p h d", h=H),
                                            bias[:, 2 * D:3 * D].rearrange("p (h d) -> p h d", h=H), ALU.add).then_inc(rows_ready, 1)

            def body(i):
                if not isinstance(i, int):
                    dve.drain()
                    dve.wait_ge(stored, i * 64)
                gathered(i)
                dve.drain()
                norm.vector(dve, i, lambda k: tile_of(xs, i * U + k), lambda k: xn[:, k, :], xn_ready)
                dve.drain()
                for k in range(U):
                    if not isinstance(i, int):
                        dve.wait_ge(turned, (i - 1) * U + k + 1)
                    nc.vector.tensor_tensor(enh[:, k, :], xn[:, k, :], query[:], ALU.add).then_inc(enh_ready, 1)
                keep_rows(i)

            rounds(dve, s, body)
            norm.vector_end(dve)

        @block.tensor
        def _(pe):
            pe.wait_ge(w_ready, 1)
            rounds(pe, s, lambda i: run_pe(pe, i))

        @block.scalar
        def _(act):
            def body(i):
                norm.root(act, i)
                for k in range(U):
                    copy_cols(act, i, k)

            rounds(act, s, body)


def edge_records(prog):
    nc, s, ins = prog.nc, prog.s, prog.ins
    B, GR, HD, R = s.B, s.GR, s.HD, s.RELS
    RW = B * HD + 2 * B
    NG = s.EC // B
    steps = NG // GR
    prog.records = records = prog.dram("edge_records", [s.NB, RW])
    prog.RW = RW
    types_T = prog.dram("types_turned", [s.EC, P])
    chunks = [(c, min(P, s.EC - c)) for c in range(0, s.EC, P)]
    with Stage() as ctx:
        sb, psum, sem = in_scope(nc, ctx)
        lists = sb("e_lists", [P, 3, s.EC], I32)
        types_f = sb("e_types_f", [P, s.EC])
        types_t = sb("e_types_t", [P, len(chunks), P])
        rel = sb("e_rel", [R, HD])
        wide = sb("e_wide", [R, 2, GR, B * P])
        hot = sb("e_hot", [R, 2, GR, B * P])
        rec = sb("e_rec", [P, 2, GR, RW])
        turned = psum("e_turned", [P, 2, 512])
        made = psum("e_made", [P, 4, 512])
        lists_in, cast, turn_done, turn_copied, stored_T = (sem("e_lists_in"), sem("e_cast"), sem("e_turn_done"),
                                                            sem("e_turn_copied"), sem("e_stored_T"))
        rel_ready = sem("e_rel_ready")
        wide_in = [sem(f"e_wide_in{j}") for j in range(2)]
        rec_out = [sem(f"e_rec_out{j}") for j in range(2)]
        hot_ready, made_done, rec_ready, ends_ready = sem("e_hot_ready"), sem("e_made_done"), sem("e_rec_ready"), sem("e_ends_ready")
        block = ctx.enter_context(nc.Block())

        def pairs(eng, body):
            for j in range(2):
                body(0, j)
            with eng.Fori(1, steps // 2) as i:
                for j in range(2):
                    body(i, j)

        @block.sync
        def _(sp):
            for j, k in enumerate(("edge_type_64", "src", "dst")):
                sp.dma_start(lists[:, j, :], prog.edges[k].rearrange("(p c) -> p c", p=P)).then_inc(lists_in, 16)
            sp.dma_start(rel[:], ins["L1_gnn_rel_w"][:, :]).then_inc(lists_in, 16)
            sp.wait_ge(turn_copied, len(chunks))
            for c, (a, n) in enumerate(chunks):
                sp.dma_start(types_T[a:a + n, :], types_t[0:n, c, :]).then_inc(stored_T, 16)
            sp.wait_ge(stored_T, 16 * len(chunks))

            def store(i, j):
                sp.wait_ge(rec_ready, (i * 2 + j + 1) * GR)
                sp.wait_ge(ends_ready, i * 2 + j + 1)
                sp.dma_start(records.rearrange("(p b) f -> p b f", p=P)[:, bass.ds((i * 2 + j) * GR, GR), :],
                             rec[:, j]).then_inc(rec_out[j], 16)

            def body(i, j):
                g = i * 2 + j
                if not isinstance(i, int):
                    sp.wait_ge(hot_ready, g - 1)
                sp.dma_start(wide[:, j], types_T.rearrange("(a c) p -> a (c p)", c=B * GR)[bass.ds(g, 1), :]
                             .to_broadcast([R, GR * B * P]).rearrange("r (g x) -> r g x", g=GR)).then_inc(wide_in[j], 16)
                if not isinstance(i, int):
                    store(*((i, 0) if j else (i - 1, 1)))
                elif j:
                    store(0, 0)

            pairs(sp, body)
            store(steps // 2 - 1, 1)
            for j in range(2):
                sp.wait_ge(rec_out[j], 16 * (steps // 2))

        @block.vector
        def _(dve):
            dve.wait_ge(lists_in, 64)
            nc.vector.tensor_copy(types_f[:], lists[:, 0, :]).then_inc(cast, 1)
            nc.vector.tensor_scalar(rel[:], rel[:], 0.2, None, ALU.mult).then_inc(rel_ready, 1)

            def body(i, j):
                g = i * 2 + j
                dve.wait_ge(wide_in[j], (i + 1) * 16)
                if not isinstance(i, int):
                    dve.wait_ge(made_done, (g - 1) * GR)
                nc.vector.tensor_scalar(hot[:, j], wide[:, j], prog.lane[0:R, :], None, ALU.is_equal).then_inc(hot_ready, 1)

            pairs(dve, body)

        @block.gpsimd
        def _(pool):
            pool.wait_ge(lists_in, 64)

            def body(i, j):
                g = i * 2 + j
                if not isinstance(i, int):
                    pool.wait_ge(rec_out[j], i * 16)
                for m in range(2):
                    c = nc.gpsimd.tensor_copy(rec[:, j, :, B * HD + m * B:B * HD + (m + 1) * B],
                                              lists[:, 1 + m, bass.ds(g * GR * B, GR * B)].rearrange("p (g b) -> p g b", b=B))
                c.then_inc(ends_ready, 1)

            pairs(pool, body)

        @block.tensor
        def _(pe):
            pe.wait_ge(cast, 1)
            for c, (a, n) in enumerate(chunks):
                if c >= 2:
                    pe.wait_ge(turn_copied, c - 1)
                nc.tensor.transpose(turned[0:n, c % 2, 0:P], types_f[:, a:a + n], prog.ident[:]).then_inc(turn_done, 1)
            pe.wait_ge(rel_ready, 1)

            def body(i, j):
                g = i * 2 + j
                pe.wait_ge(hot_ready, g + 1)
                for b in range(GR):
                    if not isinstance(i, int):
                        pe.wait_ge(rec_ready, g * GR + b - 3)
                    elif j * GR + b >= 4:
                        pe.wait_ge(rec_ready, j * GR + b - 3)
                    for e in range(B):
                        m = nc.tensor.matmul(made[:, b % 4, e * HD:(e + 1) * HD], hot[:, j, b, e * P:(e + 1) * P], rel[:],
                                             start=True, stop=True)
                    m.then_inc(made_done, 1)

            pairs(pe, body)

        @block.scalar
        def _(act):
            for c, (a, n) in enumerate(chunks):
                act.wait_ge(turn_done, c + 1)
                nc.scalar.activation(types_t[0:n, c, :], turned[0:n, c % 2, 0:P], ACT.Copy).then_inc(turn_copied, 1)

            def body(i, j):
                g = i * 2 + j
                if not isinstance(i, int):
                    act.wait_ge(rec_out[j], i * 16)
                for b in range(GR):
                    act.wait_ge(made_done, g * GR + b + 1)
                    nc.scalar.activation(rec[:, j, b, 0:B * HD], made[:, b % 4, 0:B * HD], ACT.Copy).then_inc(rec_ready, 1)

            pairs(act, body)


def node_order(prog, keep):
    nc, s = prog.nc, prog.s
    NT, EC, U, B = s.NT, s.EC, s.U, s.B
    CB = 13
    steps = EC // CB
    assert EC % CB == 0 and steps % 2 == 0
    sbk, _, _ = in_scope(nc, keep)
    prog.sorted_node = sbk("sorted_node", [P, NT + 1], U32)
    prog.sorted_node_f = sbk("sorted_node_f", [P, NT + 1])
    prog.sorted_block = sbk("sorted_block", [P, NT + 1], U32)
    prog.sorted_deg = sbk("sorted_deg", [P, NT])
    prog.trips = trips = sbk("trips", [1, 2, P], I32)
    table = prog.dram("sorted_table", [s.NP, 4])
    with Stage() as ctx:
        sb, psum, sem = in_scope(nc, ctx)
        stay = ctx.enter_context(Stage())
        count = sb("n_count", [P, P])
        col = sb("n_col", [P, 3, P])
        with Stage() as inner:
            sb1, psum1, sem1 = in_scope(nc, inner)
            dst = sb1("n_dst", [P, EC], I32)
            part = sb1("n_part", [P, EC], I32)
            hi = sb1("n_hi", [P, EC])
            lo = sb1("n_lo", [P, EC])
            hot_hi = sb1("n_hot_hi", [P, 2, CB, P], BF16)
            hot_lo = sb1("n_hot_lo", [P, 2, CB, P], BF16)
            hist = psum1("n_hist", [P, P])
            dst_in, hot_ready, used, zero = sem1("n_dst_in"), sem1("n_hot_ready"), sem1("n_used"), sem1("n_zero")
            counted = sem1("n_counted")
            block = inner.enter_context(nc.Block())

            def pairs(eng, body):
                for j in range(2):
                    body(0, j)
                with eng.Fori(1, steps // 2) as i:
                    for j in range(2):
                        body(i, j)

            @block.sync
            def _(sp):
                sp.dma_start(dst[:], prog.edges["dst"].rearrange("(p c) -> p c", p=P)).then_inc(dst_in, 16)

            @block.vector
            def _(dve):
                v = nc.vector
                v.memset(hot_hi[:], 0.0)
                dve.wait_ge(dst_in, 16)
                v.tensor_scalar(part[:], dst[:], 7, None, ALU.arith_shift_right)
                dve.drain()
                v.tensor_copy(hi[:], part[:])
                dve.drain()
                v.tensor_scalar(part[:], dst[:], P - 1, None, ALU.bitwise_and)
                dve.drain()
                v.tensor_copy(lo[:], part[:])
                dve.drain()

                def body(i, j):
                    g = i * 2 + j
                    if not isinstance(i, int):
                        dve.wait_ge(used, g - 1)
                    for hot, src, n in ((hot_hi, hi, NT), (hot_lo, lo, P)):
                        m = v.tensor_tensor(hot[:, j, :, 0:n], prog.bins[:, 0:n].unsqueeze(1).to_broadcast([P, CB, n]),
                                            src[:, bass.ds(g * CB, CB)].unsqueeze(2).to_broadcast([P, CB, n]), ALU.is_equal)
                    m.then_inc(hot_ready, 1)

                pairs(dve, body)
                dve.wait_ge(used, steps)
                v.tensor_copy(count[:], hist[:]).then_inc(counted, 1)

            @block.tensor
            def _(pe):
                def body(i, j):
                    g = i * 2 + j
                    pe.wait_ge(hot_ready, g + 1)
                    for c in range(CB):
                        first = isinstance(i, int) and j == 0 and c == 0
                        m = nc.tensor.matmul(hist[:], hot_hi[:, j, c, :], hot_lo[:, j, c, :], start=first, stop=True,
                                             skip_group_check=True)
                    m.then_inc(used, 1)

                pairs(pe, body)

        with Stage() as inner:
            sb1, psum1, sem1 = in_scope(nc, inner)
            upto = sb1("n_upto", [P, P])
            first = sb1("n_first", [P, P])
            work_i = sb1("n_work_i", [P, 2, P], I32)
            blk = sb1("n_blk", [P, 3, P])
            ps_base = psum1("n_ps_base", [P, 512])
            ps_turn = psum1("n_ps_turn", [P, 3, P])
            scanned, based, ready, turn_done, done = (sem1("n_scanned"), sem1("n_based"), sem1("n_ready"),
                                                      sem1("n_turn_done"), sem1("n_end"))
            block = inner.enter_context(nc.Block())

            @block.vector
            def _(dve):
                v = nc.vector

                def step(ins):
                    dve.drain()

                step(v.tensor_tensor_scan(upto[:], count[:], count[:], 0.0, ALU.add, ALU.bypass))
                step(v.tensor_tensor(first[:], upto[:], count[:], ALU.subtract))
                v.memset(work_i[:], 0).then_inc(scanned, 1)
                dve.wait_ge(based, 1)
                step(v.tensor_scalar(first[:], first[:], ps_base[:, 0:1], None, ALU.add))
                v.tensor_copy(work_i[:, 0, :], first[:])
                step(v.tensor_tensor(upto[:], first[:], count[:], ALU.add))
                step(v.tensor_scalar(upto[:], upto[:], float(B - 1), None, ALU.add))
                step(v.tensor_copy(work_i[:, 1, :], upto[:]))
                step(v.tensor_scalar(work_i[:], work_i[:], B.bit_length() - 1, None, ALU.arith_shift_right))
                step(v.tensor_copy(blk[:, 0:2, :], work_i[:]))
                step(v.tensor_tensor(blk[:, 1, :], blk[:, 1, :], blk[:, 0, :], ALU.subtract))
                v.tensor_copy(blk[:, 2, :], count[:]).then_inc(ready, 1)
                dve.wait_ge(turn_done, 1)
                v.tensor_copy(col[:], ps_turn[:]).then_inc(done, 1)

            @block.tensor
            def _(pe):
                pe.wait_ge(scanned, 1)
                nc.tensor.matmul(ps_base[:, 0:1], prog.below[:], upto[:, P - 1:P], start=True, stop=True).then_inc(based, 1)
                pe.wait_ge(ready, 1)
                for j in range(3):
                    m = nc.tensor.transpose(ps_turn[:, j, :], blk[:, j, :], prog.ident[:])
                m.then_inc(turn_done, 1)

        with Stage() as inner:
            sb1, psum1, sem1 = in_scope(nc, inner)
            key = sb1("n_key", [P, NT])
            hot = sb1("n_hot", [P, P, NT], BF16)
            tiles = sb1("n_tiles", [P, P, NT])
            place = sb1("n_place", [P, P, NT])
            pos = sb1("n_pos", [P, NT])
            pos_u = sb1("n_pos_u", [P, NT], U32)
            data = sb1("n_data", [P, NT, 4])
            now = sb1("n_now", [P, U], U32)
            now_data = sb1("n_now_data", [P, U, 4])
            got = sb1("n_got", [P, NT, 4])
            square = sb1("n_square", [P, P])
            most = sb1("n_most", [P, P])
            trip_f = sb1("n_trip_f", [1, 3, P])
            ps = psum1("n_ps", [P, 2, 2, 512])
            ps_sq = psum1("n_ps_sq", [P, 2, P])
            hot_ready, counted, taken, ready, scattered, got_in = (sem1("n_hot_r"), sem1("n_cnt"), sem1("n_taken"),
                                                                   sem1("n_ready2"), sem1("n_scattered"), sem1("n_got_in"))
            sq_ready, sq_done, trips_ready = sem1("n_sq_ready"), sem1("n_sq_done"), sem1("n_trips_ready")
            W = P * NT
            cuts = [(a, min(512, W - a)) for a in range(0, W, 512)]
            block = inner.enter_context(nc.Block())

            def flat(t):
                return t[:].rearrange("p b t -> p (b t)")

            @block.vector
            def _(dve):
                v = nc.vector

                def step(ins):
                    dve.drain()

                step(v.tensor_scalar(key[:], col[:, 1, 0:NT], float(P - 1), -1.0, ALU.min, ALU.mult))
                step(v.tensor_scalar(key[:], key[:], float(P - 1), None, ALU.add))
                v.tensor_tensor(hot[:], prog.bins[:].unsqueeze(2).to_broadcast([P, P, NT]),
                                key[:].unsqueeze(1).to_broadcast([P, P, NT]), ALU.is_equal).then_inc(hot_ready, 1)
                for n, (a, w) in enumerate(cuts):
                    dve.wait_ge(counted, n + 1)
                    v.tensor_copy(flat(tiles)[:, a:a + w], ps[:, n % 2, 0, 0:w])
                    v.tensor_copy(flat(place)[:, a:a + w], ps[:, n % 2, 1, 0:w]).then_inc(taken, 1)
                dve.drain()
                step(v.tensor_tensor(flat(place), flat(place), flat(tiles), ALU.subtract))
                step(v.tensor_tensor_scan(flat(tiles), flat(tiles), flat(tiles), 0.0, ALU.add, ALU.bypass))
                step(v.tensor_tensor(flat(place), flat(place), flat(tiles), ALU.add))
                step(v.tensor_tensor(flat(place), flat(place), flat(hot), ALU.mult))
                step(v.tensor_reduce(pos[:], place[:].rearrange("p b t -> p t b"), AX.X, ALU.add))
                step(v.tensor_copy(pos_u[:], pos[:]))
                v.tensor_copy(data[:, :, 0], prog.node[:])
                v.tensor_copy(data[:, :, 1], col[:, 0, 0:NT])
                v.tensor_copy(data[:, :, 2], col[:, 1, 0:NT])
                step(v.tensor_copy(data[:, :, 3], col[:, 2, 0:NT]))
                v.memset(square[:], 0.0).then_inc(ready, 1)
                dve.wait_ge(got_in, 16)
                dve.drain()
                v.memset(prog.sorted_node[:, NT:NT + 1], 0)
                v.tensor_copy(prog.sorted_node[:, 0:NT], got[:, :, 0])
                v.memset(prog.sorted_node_f[:, NT:NT + 1], 0.0)
                v.tensor_copy(prog.sorted_node_f[:, 0:NT], got[:, :, 0])
                v.memset(prog.sorted_block[:, NT:NT + 1], 0)
                v.tensor_copy(prog.sorted_block[:, 0:NT], got[:, :, 1])
                v.tensor_copy(prog.sorted_deg[:], got[:, :, 3])
                v.tensor_copy(square[:, 0:NT], got[:, :, 2])
                v.memset(most[:], 0.0).then_inc(sq_ready, 1)
                dve.wait_ge(sq_done, 1)
                dve.drain()
                v.tensor_reduce(most[:, 0:1], ps_sq[:, 0, :], AX.X, ALU.max).then_inc(sq_ready, 1)
                dve.wait_ge(sq_done, 2)
                step(v.tensor_scalar(trip_f[:, 0, :], ps_sq[0:1, 1, :], 2.0, None, ALU.max))
                step(v.tensor_tensor_scan(trip_f[:, 1, :], trip_f[:, 0, :], trip_f[:, 0, :], 0.0, ALU.add, ALU.bypass))
                step(v.tensor_tensor(trip_f[:, 2, :], trip_f[:, 1, :], trip_f[:, 0, :], ALU.subtract))
                v.tensor_copy(trips[:, 0, :], trip_f[:, 0, :])
                v.tensor_copy(trips[:, 1, :], trip_f[:, 2, :]).then_inc(trips_ready, 1)

            @block.tensor
            def _(pe):
                pe.wait_ge(hot_ready, 1)
                for n, (a, w) in enumerate(cuts):
                    if n >= 2:
                        pe.wait_ge(taken, n - 1)
                    nc.tensor.matmul(ps[:, n % 2, 0, 0:w], prog.ones16[:], flat(hot)[:, a:a + w], start=True, stop=True)
                    nc.tensor.matmul(ps[:, n % 2, 1, 0:w], prog.below16[:], flat(hot)[:, a:a + w],
                                     start=True, stop=True).then_inc(counted, 1)
                pe.wait_ge(sq_ready, 1)
                nc.tensor.transpose(ps_sq[:, 0, :], square[:], prog.ident[:]).then_inc(sq_done, 1)
                pe.wait_ge(sq_ready, 2)
                nc.tensor.transpose(ps_sq[:, 1, :], most[:], prog.ident[:]).then_inc(sq_done, 1)

            @block.gpsimd
            def _(pool):
                pool.wait_ge(ready, 1)

                def body(i):
                    if not isinstance(i, int):
                        pool.wait_ge(scattered, i * 16 * U)
                    nc.gpsimd.tensor_copy(now[:], cols_of(pos_u, i, s))
                    nc.gpsimd.tensor_copy(now_data[:], data[:, bass.ds(i * U, U), :])
                    pool.drain()
                    for k in range(U):
                        scatter(nc, table, now[:, k:k + 1], now_data[:, k, :], s.NP).then_inc(scattered, 16)

                rounds(pool, s, body)
                pool.wait_ge(scattered, 16 * s.NT)
                pool.dma_start(got[:], table.rearrange("(t p) f -> p t f", p=P)).then_inc(got_in, 16)


def l1_attend(prog, keep):
    nc, s = prog.nc, prog.s
    H, HD, D, B, NT = s.H, s.HD, s.D, s.B, s.NT
    HV = HD + 1
    KV = D + H * HV
    RW = prog.RW
    trips = prog.trips
    sbk, _, _ = in_scope(nc, keep)
    prog.attended = attended = sbk("attended", [P, NT, H * HV])
    with Stage() as ctx:
        sb, psum, sem = in_scope(nc, ctx)
        rec_at = sb("g_rec_at", [P, 1], U32)
        node_at = sb("g_node_at", [P, 1], U32)
        one = sb("g_one", [P, 1], U32)
        rec = sb("g_rec", [P, RW])
        rel = sb("g_rel", [P, 2, B, HD])
        away = sb("g_away", [P, 2, B])
        kv_at = sb("g_kv_at", [P, 2, B], U32)
        kv = sb("g_kv", [P, 2, B, KV])
        q_in = sb("g_q_in", [P, D])
        q = sb("g_q", [P, D])
        kr = sb("g_kr", [P, B, D])
        prod = sb("g_prod", [P, B, D])
        sc = sb("g_sc", [P, B + 1, H])
        top = sb("g_top", [P, H])
        dif = sb("g_dif", [P, B + 1, H])
        pr = sb("g_pr", [P, B + 1, H])
        pv = sb("g_pv", [P, B + 1, H * HV])
        acc = psum("g_acc", [P, 512])
        kv_in = [sem(f"g_kv_in{j}") for j in range(2)]
        rec_in, node_in, cleared = sem("g_rec_in"), sem("g_node_in"), sem("g_cleared")
        kv_at_ready, rel_ready, q_ready = sem("g_kv_at_ready"), sem("g_rel_ready"), sem("g_q_ready")
        kr_done = sem("g_kr_done")
        prod_done = sem("g_prod_done")
        rows_used = sem("g_rows_used")
        summed = sem("g_summed")
        kept = sem("g_kept")
        dif_ready, exp_done, pv_ready = sem("g_dif_ready"), sem("g_exp_done"), sem("g_pv_ready")
        block = ctx.enter_context(nc.Block())

        def steps_of(eng, t):
            return [eng.value_load(trips[0:1, r, bass.ds(t, 1)], min_val=lo, max_val=s.NB) for r, lo in ((0, 2), (1, 0))]

        def by_parity(eng, g, body):
            with eng.If(g % 2 == 0):
                body(0)
            with eng.Else():
                body(1)

        def tiles(eng, begin, step, end):
            with eng.Fori(0, NT) as t:
                n, before = steps_of(eng, t)
                begin(t, before)
                with eng.Fori(0, n - 1) as i:
                    step(before + i, t, False)
                step(before + n - 1, t, True)
                end(t, before + n)

        @block.gpsimd
        def _(pool):
            def load_node(t):
                nc.gpsimd.tensor_copy(node_at[:], prog.sorted_node[:, bass.ds(t, 1)])
                pool.drain()
                gather(nc, q_in[:], prog.q_table, node_at[:], s.NP).then_inc(node_in, 16)

            def get_record():
                gather(nc, rec[:], prog.records, rec_at[:], s.NB).then_inc(rec_in, 16)

            nc.gpsimd.memset(one[:], 1)
            pool.wait_ge(cleared, 1)
            nc.gpsimd.tensor_copy(rec_at[:], prog.sorted_block[:, 0:1])
            load_node(0)
            get_record()

            def step(g, t, last):
                pool.wait_ge(kv_at_ready, g + 1)
                pool.wait_ge(rel_ready, g + 1)
                if last:
                    nc.gpsimd.tensor_copy(rec_at[:], prog.sorted_block[:, bass.ds(t + 1, 1)])
                else:
                    nc.gpsimd.tensor_tensor(rec_at[:], rec_at[:], one[:], ALU.add)
                pool.drain()
                get_record()
                pool.wait_ge(rows_used, g + 1)

                def rows(j):
                    for b in range(B):
                        gather(nc, kv[:, j, b, :], prog.kv_table, kv_at[:, j, b:b + 1], s.NP).then_inc(kv_in[j], 16)

                by_parity(pool, g, rows)

            def end(t, g):
                pool.wait_ge(q_ready, t + 1)
                load_node(t + 1)

            tiles(pool, lambda t, g: None, step, end)
            pool.wait_ge(node_in, (NT + 1) * 16)

        @block.vector
        def _(dve):
            v = nc.vector
            v.memset(kv[:], 0.0)
            v.memset(top[:], 0.0).then_inc(rows_used, 2)
            v.memset(q[:], 0.0).then_inc(kr_done, 1)
            dve.drain()
            v.memset(prod[:], 0.0).then_inc(prod_done, 1)
            dve.drain()
            v.memset(pv[:], 0.0).then_inc(cleared, 1)

            def sources(g, j, node):
                dve.wait_ge(rec_in, (g + 1) * 16)
                v.tensor_scalar(away[:, j, :], rec[:, B * HD + B:RW], node, 2.0 * s.NP, ALU.not_equal, ALU.mult)
                dve.drain()
                v.tensor_tensor(kv_at[:, j, :], away[:, j, :], rec[:, B * HD:B * HD + B], ALU.add).then_inc(kv_at_ready, 1)

            sources(0, 0, prog.sorted_node_f[:, 0:1])

            def begin(t, g):
                dve.drain()
                v.memset(top[:], -1e30)
                dve.wait_ge(q_ready, t + 1)
                dve.wait_ge(kept, t + 1)
                v.memset(dif[:], 0.0)

            def step(g, t, last):
                node = prog.sorted_node_f[:, bass.ds(t + 1 if last else t, 1)]

                def work(j):
                    sources(g + 1, 1 - j, node)
                    dve.drain()
                    v.tensor_copy(sc[:, B, :], top[:])
                    dve.wait_ge(rel_ready, g + 1)
                    dve.wait_ge(kv_in[j], (g + 2) // 2 * (16 * B))
                    k4 = kv[:, j, :, 0:D].rearrange("p b (h d) -> p b h d", h=H)
                    v.tensor_tensor(kr[:].rearrange("p b (h d) -> p b h d", h=H), k4,
                                    rel[:, j].unsqueeze(2).to_broadcast([P, B, H, HD]), ALU.add).then_inc(kr_done, 1)
                    dve.drain()
                    v.tensor_tensor(prod[:], kr[:], q[:].unsqueeze(1).to_broadcast([P, B, D]), ALU.mult).then_inc(prod_done, 1)
                    dve.drain()
                    v.tensor_reduce(sc[:, 0:B, :], prod[:].rearrange("p b (h d) -> p b h d", h=H), AX.X, ALU.add)
                    dve.drain()
                    v.scalar_tensor_tensor(out=sc[:, 0:B, :], in0=away[:, j, :].unsqueeze(2).to_broadcast([P, B, H]),
                                           scalar=-1e26, in1=sc[:, 0:B, :], op0=ALU.mult, op1=ALU.add)
                    dve.drain()
                    v.tensor_reduce(top[:], sc[:].rearrange("p b h -> p h b"), AX.X, ALU.max)
                    dve.drain()
                    v.tensor_tensor(dif[:], sc[:], top[:].unsqueeze(1).to_broadcast([P, B + 1, H]),
                                    ALU.subtract).then_inc(dif_ready, 1)
                    dve.wait_ge(summed, g + 1)
                    dve.wait_ge(exp_done, g + 1)
                    v.tensor_tensor(pv[:, B, :].rearrange("p (h d) -> p h d", h=H),
                                    acc[:, 0:H * HV].rearrange("p (h d) -> p h d", h=H),
                                    pr[:, B, :].unsqueeze(2).to_broadcast([P, H, HV]), ALU.mult)
                    v.tensor_tensor(pv[:, 0:B, :].rearrange("p b (h d) -> p b h d", h=H),
                                    kv[:, j, :, D:KV].rearrange("p b (h d) -> p b h d", h=H),
                                    pr[:, 0:B, :].unsqueeze(3).to_broadcast([P, B, H, HV]), ALU.mult).then_inc(rows_used, 1)
                    dve.drain()
                    v.memset(sc[0:1, 0:1, 0:1], 0.0).then_inc(pv_ready, 1)

                by_parity(dve, g, work)

            tiles(dve, begin, step, lambda t, g: None)

        @block.tensor
        def _(pe):
            def add_up(first=False):
                for b in range(B + 1):
                    m = nc.tensor.matmul(acc[:, 0:H * HV], prog.ident[:], pv[:, b, :], start=b == 0, stop=b == B)
                m.then_inc(summed, 1)

            pe.wait_ge(cleared, 1)
            add_up()

            def step(g, t, last):
                pe.wait_ge(pv_ready, g + 1)
                add_up()

            tiles(pe, lambda t, g: None, step, lambda t, g: None)

        @block.scalar
        def _(act):
            def copy_rel(g, j):
                act.wait_ge(rec_in, (g + 1) * 16)
                nc.scalar.activation(rel[:, j].rearrange("p b d -> p (b d)"), rec[:, 0:B * HD], ACT.Copy).then_inc(rel_ready, 1)

            act.wait_ge(cleared, 1)
            nc.scalar.activation(pr[:], prog.bins[:, 0:(B + 1) * H].rearrange("p (b h) -> p b h", b=B + 1), ACT.Copy).then_inc(kept, 1)
            copy_rel(0, 0)

            def begin(t, g):
                act.wait_ge(node_in, (t + 1) * 16)
                act.wait_ge(prod_done, g + 1)
                nc.scalar.activation(q[:], q_in[:], ACT.Copy).then_inc(q_ready, 1)

            def step(g, t, last):
                def work(j):
                    act.wait_ge(kr_done, g + 1)
                    copy_rel(g + 1, 1 - j)
                    act.wait_ge(dif_ready, g + 1)
                    nc.scalar.activation(pr[:], dif[:], ACT.Exp).then_inc(exp_done, 1)

                by_parity(act, g, work)

            def end(t, g):
                act.wait_ge(summed, g + 1)
                nc.scalar.activation(tile_of(attended, t), acc[:, 0:H * HV], ACT.Copy).then_inc(kept, 1)

            tiles(act, begin, step, end)


def l1_out(prog):
    nc, s, ins = prog.nc, prog.s, prog.ins
    H, HD, D, U = s.H, s.HD, s.D, s.U
    HV = HD + 1
    KV = D + H * HV
    prog.x3_table = x3_table = prog.dram("x3_table", [s.NP, D])
    with Stage() as ctx:
        sb, psum, sem = in_scope(nc, ctx)
        at = sb("f_at", [P, U], U32)
        put_at = sb("f_put_at", [P, U], U32)
        none = sb("f_none", [P, U], U32)
        nx = sb("f_nx", [P, U, 2 * D])
        kv = sb("f_kv", [P, U, KV])
        has = sb("f_has", [P, s.NT])
        hasnt = sb("f_hasnt", [P, s.NT])
        inv = sb("f_inv", [P, U, H])
        msg = sb("f_msg", [P, U, D])
        own = sb("f_own", [P, U, D])
        y = sb("f_y", [P, U, D])
        yn = sb("f_yn", [P, U, D])
        x3 = sb("f_x3", [P, U, D])
        w = sb("f_w", [P, s.DK, D])
        par = sb("f_par", [P, 3, D])
        norm = LayerNorm(prog, ctx, "f")
        rows_in = [sem(f"f_rows_in{k}") for k in range(U)]
        w_in, msg_ready, y_ready, yn_ready = sem("f_w_in"), sem("f_msg_ready"), sem("f_y_ready"), sem("f_yn_ready")
        x3_ready, stored = sem("f_x3_ready"), sem("f_stored")
        out, done, turned, run_pe, copy_cols = project(prog, ctx, "f", msg, msg_ready, w, D,
                                                       lambda pe, m: pe.wait_ge(y_ready, m))
        block = ctx.enter_context(nc.Block())

        @block.sync
        def _(sp):
            sp.dma_start(w[:], ins["L1_gnn_Wo"].rearrange("(c p) f -> p c f", p=P)).then_inc(w_in, 16)
            for j, k in enumerate(("bo", "gamma", "beta")):
                sp.dma_start(par[:, j, :], row(ins[f"L1_gnn_{k}"]).to_broadcast([P, D])).then_inc(w_in, 16)

        @block.gpsimd
        def _(pool):
            nc.gpsimd.memset(none[:], 0)

            def put(i):
                pool.wait_ge(x3_ready, i + 1)
                nc.gpsimd.tensor_tensor(put_at[:], at[:], none[:], ALU.add)
                pool.drain()
                for k in range(U):
                    scatter(nc, x3_table, put_at[:, k:k + 1], x3[:, k, :], s.NP).then_inc(stored, 16)

            def body(i):
                if not isinstance(i, int):
                    pool.wait_ge(stored, i * 16 * U)
                nc.gpsimd.tensor_copy(at[:], cols_of(prog.sorted_node, i, s))
                pool.drain()
                for k in range(U):
                    gather(nc, nx[:, k, :], prog.nx_table, at[:, k:k + 1], s.NP).then_inc(rows_in[k], 16)
                    gather(nc, kv[:, k, :], prog.kv_table, at[:, k:k + 1], s.NP).then_inc(rows_in[k], 16)
                put(i)

            rounds(pool, s, body)
            pool.wait_ge(stored, 16 * s.NT)

        @block.vector
        def _(dve):
            v = nc.vector
            v.tensor_scalar(has[:], prog.sorted_deg[:], 0.0, None, ALU.is_gt)
            v.tensor_scalar(hasnt[:], prog.sorted_deg[:], 0.0, None, ALU.is_equal)
            dve.drain()
            dve.wait_ge(w_in, 64)

            def heads(t):
                return t.rearrange("p (h d) -> p h d", h=H)

            def body(i):
                if not isinstance(i, int):
                    dve.drain()
                now = prog.attended[:, bass.ds(i * U, U), :].rearrange("p u (h d) -> p u h d", h=H)
                for k in range(U):
                    dve.wait_ge(rows_in[k], (i + 1) * 32)
                v.tensor_scalar(inv[:], now[:, :, :, HD], 1e-30, None, ALU.max)
                dve.drain()
                v.reciprocal(inv[:], inv[:])
                dve.drain()
                v.tensor_tensor(own[:].rearrange("p u (h d) -> p u h d", h=H), now[:, :, :, 0:HD],
                                inv[:].unsqueeze(3).to_broadcast([P, U, H, HD]), ALU.mult)
                dve.drain()
                one = [t[:, bass.ds(i * U, U)].unsqueeze(2).to_broadcast([P, U, D]) for t in (has, hasnt)]
                v.tensor_tensor(own[:], own[:], one[0], ALU.mult)
                v.tensor_tensor(y[:].rearrange("p u (h d) -> p u h d", h=H),
                                kv[:, :, D:KV].rearrange("p u (h d) -> p u h d", h=H)[:, :, :, 0:HD],
                                one[1].rearrange("p u (h d) -> p u h d", h=H), ALU.mult)
                dve.drain()
                for k in range(U):
                    if not isinstance(i, int):
                        dve.wait_ge(turned, (i - 1) * U + k + 1)
                    v.tensor_tensor(msg[:, k, :], own[:, k, :], y[:, k, :], ALU.add).then_inc(msg_ready, 1)
                dve.drain()
                v.tensor_tensor(own[:], nx[:, :, 0:D], par[:, 0, :].unsqueeze(1).to_broadcast([P, U, D]), ALU.add)
                dve.drain()
                for k in range(U):
                    dve.wait_ge(done, i * U + k + 1)
                    v.tensor_tensor(y[:, k, :], out[:, k % 2, 0:D], own[:, k, :], ALU.add).then_inc(y_ready, 1)
                dve.drain()
                norm.vector(dve, i, lambda k: y[:, k, :], lambda k: yn[:, k, :], yn_ready)
                dve.drain()
                v.tensor_tensor(yn[:], yn[:], par[:, 1, :].unsqueeze(1).to_broadcast([P, U, D]), ALU.mult)
                v.tensor_tensor(own[:], nx[:, :, D:2 * D], par[:, 2, :].unsqueeze(1).to_broadcast([P, U, D]), ALU.add)
                dve.drain()
                v.tensor_tensor(x3[:], yn[:], own[:], ALU.add).then_inc(x3_ready, 1)

            rounds(dve, s, body)

        @block.tensor
        def _(pe):
            pe.wait_ge(w_in, 64)
            rounds(pe, s, lambda i: run_pe(pe, i))

        @block.scalar
        def _(act):
            def body(i):
                for k in range(U):
                    copy_cols(act, i, k)
                norm.root(act, i)

            rounds(act, s, body)


def l1_gate(prog):
    nc, s, ins = prog.nc, prog.s, prog.ins
    D, U = s.D, s.U
    xs, logits = prog.x, prog.logits
    with Stage() as ctx:
        sb, psum, sem = in_scope(nc, ctx)
        xn = sb("h_xn", [P, U, D])
        w = sb("h_w", [P, s.DK, s.X])
        bias = sb("h_bias", [P, s.X])
        norm = LayerNorm(prog, ctx, "h")
        x_in, w_in, xn_ready, kept, stored = sem("h_x_in"), sem("h_w_in"), sem("h_xn_ready"), sem("h_kept"), sem("h_stored")
        out, done, turned, run_pe, copy_cols = project(prog, ctx, "h", xn, xn_ready, w, s.X,
                                                       lambda pe, m: pe.wait_ge(kept, m))
        block = ctx.enter_context(nc.Block())

        @block.sync
        def _(sp):
            sp.dma_start(w[:], ins["L1_ffn_gate_w"].rearrange("(c p) f -> p c f", p=P)).then_inc(w_in, 16)
            sp.dma_start(bias[:], row(ins["L1_ffn_gate_b"]).to_broadcast([P, s.X])).then_inc(w_in, 16)

            def body(i):
                if not isinstance(i, int):
                    sp.wait_ge(x_in, i * 16)
                sp.dma_start(xs[:, bass.ds(i * U, U), :], tile_rows(prog.x3_table, i, s)).then_inc(x_in, 16)
                sp.wait_ge(xn_ready, (i + 1) * U)
                sp.dma_start(tile_rows(prog.xn_table, i, s), xn[:]).then_inc(stored, 16)

            rounds(sp, s, body)
            sp.wait_ge(stored, 16 * s.IT)

        @block.vector
        def _(dve):
            def body(i):
                if not isinstance(i, int):
                    dve.drain()
                    dve.wait_ge(stored, i * 16)
                dve.wait_ge(x_in, (i + 1) * 16)
                norm.vector(dve, i, lambda k: tile_of(xs, i * U + k), lambda k: xn[:, k, :], xn_ready, turned)

            rounds(dve, s, body)
            norm.vector_end(dve)
            dve.wait_ge(w_in, 32)
            dve.wait_ge(kept, s.NT)
            nc.vector.tensor_tensor(logits[:], logits[:], bias[:].unsqueeze(1).to_broadcast([P, s.NT, s.X]), ALU.add)

        @block.tensor
        def _(pe):
            pe.wait_ge(w_in, 32)
            rounds(pe, s, lambda i: run_pe(pe, i))

        @block.scalar
        def _(act):
            def keep_logits(i, k):
                n = i * U + k
                act.wait_ge(done, n + 1)
                nc.scalar.activation(tile_of(logits, n), out[:, k % 2, 0:s.X], ACT.Copy).then_inc(kept, 1)

            def body(i):
                norm.root(act, i)
                for k in range(U):
                    copy_cols(act, i, k)
                    if k:
                        keep_logits(i, k - 1)
                keep_logits(i, U - 1)

            rounds(act, s, body)


def l1_combine(prog, weight, slot, y_table):
    nc, s = prog.nc, prog.s
    D, U = s.D, s.U
    xs = prog.x
    BIG = 3.4028235e38
    with Stage() as ctx:
        sb, psum, sem = in_scope(nc, ctx)
        at = sb("o_at", [P, U], U32)
        y = sb("o_y", [P, U, D])
        z = sb("o_z", [P, U, D])
        mask = sb("o_mask", [P, 3, U, D], mybir.dt.uint8)
        const = sb("o_const", [P, 3, D])
        y_in = [sem(f"o_y_in{k}") for k in range(U)]
        used, ready, stored = sem("o_used"), sem("o_ready"), sem("o_stored")
        block = ctx.enter_context(nc.Block())

        @block.gpsimd
        def _(pool):
            def body(i):
                if not isinstance(i, int):
                    pool.wait_ge(used, i)
                nc.gpsimd.tensor_copy(at[:], cols_of(slot[0], i, s).bitcast(U32))
                pool.drain()
                for k in range(U):
                    gather(nc, y[:, k, :], y_table, at[:, k:k + 1], s.GB * s.GT).then_inc(y_in[k], 16)

            rounds(pool, s, body)

        @block.vector
        def _(dve):
            v = nc.vector
            for j, c in enumerate((0.0, 1e4, -1e4)):
                v.memset(const[:, j, :], c)
            dve.drain()

            def body(i):
                if not isinstance(i, int):
                    dve.drain()
                now = xs[:, bass.ds(i * U, U), :]
                for k in range(U):
                    dve.wait_ge(y_in[k], (i + 1) * 16)
                v.tensor_tensor(z[:], y[:], weight[0][:, bass.ds(i * U, U)].unsqueeze(2).to_broadcast([P, U, D]),
                                ALU.mult).then_inc(used, 1)
                dve.drain()
                v.tensor_tensor(mask[:, 0], z[:], z[:], ALU.not_equal)
                v.tensor_scalar(mask[:, 1], z[:], BIG, None, ALU.is_gt)
                v.tensor_scalar(mask[:, 2], z[:], -BIG, None, ALU.is_lt)
                dve.drain()
                for j in range(3):
                    v.copy_predicated(z[:], mask[:, j], const[:, j, :].unsqueeze(1).to_broadcast([P, U, D]))
                    dve.drain()
                v.tensor_tensor(now, now, z[:], ALU.add).then_inc(ready, 1)

            rounds(dve, s, body)

        @block.sync
        def _(sp):
            full = s.IT - 1
            with sp.Fori(0, full) as i:
                sp.wait_ge(ready, i + 1)
                sp.dma_start(prog.out[0:full * U * P, :].rearrange("(t p) f -> p t f", p=P)[:, bass.ds(i * U, U), :],
                             xs[:, bass.ds(i * U, U), :]).then_inc(stored, 16)
            sp.wait_ge(ready, s.IT)
            rest = prog.out[full * U * P:s.N, :]
            whole = (U - 1) * P
            sp.dma_start(rest[0:whole, :].rearrange("(t p) f -> p t f", p=P), xs[:, full * U:s.NT - 1, :]).then_inc(stored, 16)
            sp.dma_start(rest[whole:whole + s.LAST, :], xs[0:s.LAST, s.NT - 1, :]).then_inc(stored, 16)
            sp.wait_ge(stored, 16 * (full + 2))


_OUT = (6250, 256)


def build(nc, ins, out, stop=None):
    prog = Program(nc, ins, out, stop)
    with Stage() as keep:
        constants(prog, keep)
        pad_inputs(prog)
        l0_tables(prog)
        if stop == "a":
            return dump(prog, prog.xt_table[0:prog.s.N, 0:prog.s.D])
        l0_attend(prog, keep)
        if stop == "b":
            return dump_x(prog)
        with Stage() as layer:
            weight, slot, slot_node, of_group = route(prog, layer, "r0", 2, prog.s.GA)
            y = mlp(prog, "m0", prog.xn_table, slot_node, of_group, prog.s.GA, prog.s.FA,
                    ins["L0_ffn_W1"], ins["L0_ffn_b1"], ins["L0_ffn_W2"], ins["L0_ffn_b2"])
            l1_tables(prog, weight, slot, y)
        if stop == "d":
            return dump_x(prog)
        if stop == "q":
            return dump(prog, prog.kv_table[0:prog.s.N, 0:prog.s.D])
        with Stage() as layer:
            edge_records(prog)
            node_order(prog, layer)
            l1_attend(prog, layer)
            l1_out(prog)
        l1_gate(prog)
        if stop == "f":
            return dump_x(prog)
        weight, slot, slot_node, of_group = route(prog, keep, "r1", 1, prog.s.GB)
        y = mlp(prog, "m1", prog.xn_table, slot_node, of_group, prog.s.GB, prog.s.FB,
                ins["L1_ffn_w1"], ins["L1_ffn_b1"], ins["L1_ffn_w2"], ins["L1_ffn_b2"])
        l1_combine(prog, weight, slot, y)


def dump(prog, src):
    nc = prog.nc
    with Stage() as ctx:
        t = in_scope(nc, ctx)[2]("dumped")
        block = ctx.enter_context(nc.Block())

        @block.sync
        def _(sp):
            sp.dma_start(prog.out, src).then_inc(t, 16)
            sp.wait_ge(t, 16)


def dump_x(prog):
    nc, s = prog.nc, prog.s
    with Stage() as ctx:
        t = in_scope(nc, ctx)[2]("dumped")
        block = ctx.enter_context(nc.Block())

        @block.sync
        def _(sp):
            full = (s.NT - 1) * P
            sp.dma_start(prog.out[0:full, :].rearrange("(t p) f -> p t f", p=P), prog.x[:, 0:s.NT - 1, :]).then_inc(t, 16)
            sp.dma_start(prog.out[full:s.N, :], prog.x[0:s.LAST, s.NT - 1, :]).then_inc(t, 16)
            sp.wait_ge(t, 32)


def kernel(**inputs):
    import numpy as np
    import concourse.bacc as bacc
    from concourse import mybir as mb
    from concourse.bass_utils import run_bass_kernel_spmd as run

    nc = bacc.Bacc("TRN2", target_bir_lowering=False, num_devices=1)
    arrays, ins = {}, {}
    for name, a in inputs.items():
        a = np.ascontiguousarray(a)
        arrays[f"in_{name}"] = a
        ins[name] = nc.dram_tensor(f"in_{name}", a.shape, mb.dt.from_np(a.dtype), kind="ExternalInput").ap()
    out = nc.dram_tensor("out_0", _OUT, mb.dt.float32, kind="ExternalOutput").ap()
    build(nc, ins, out, STOP)
    return run(nc, [arrays], core_ids=[0]).results[0]["out_0"]


STOP = None
```

```python
from contextlib import ExitStack

import concourse.bass as bass
from concourse import mybir

ALU = mybir.AluOpType
ACT = mybir.ActivationFunctionType
AX = mybir.AxisListType
F32 = mybir.dt.float32
BF16 = mybir.dt.bfloat16
I32 = mybir.dt.int32
U32 = mybir.dt.uint32
U16 = mybir.dt.uint16

P = 128
SKIP = 1 << 20


class Shapes:

    def __init__(self, x, dst, rel_w, attn, W1a, W1b):
        self.N, self.D = x.shape
        self.E = dst.shape[0]
        self.RELS, self.HD = rel_w.shape
        self.H = attn.shape[0]
        self.NT = -(-self.N // P)
        self.NP = self.NT * P
        self.U = 7
        self.IT = self.NT // self.U
        self.LAST = self.N - (self.NT - 1) * P
        self.B = 4
        self.CH = 8
        self.WIN = self.B * self.CH
        self.EC = -(-self.E // (16 * P)) * 16
        self.EP = self.EC * P
        self.NB = self.EP // self.B
        self.DK = self.D // P
        self.X = W1a.shape[0]
        self.GT = 256
        self.FA = W1a.shape[2]
        self.FB = W1b.shape[2]
        most = (2 * self.N + self.X * (self.GT - 1)) // self.GT
        self.GA = most + most % 2
        self.CAP = -(-5 * self.N // (4 * self.X))
        self.GPE = -(-self.CAP // self.GT)
        self.GB = self.X * self.GPE
        assert self.NT == self.U * self.IT and self.D == self.H * self.HD


def columns(col, n):
    return col[:, :].unsqueeze(2).to_broadcast(n)


class Program:
    def __init__(self, nc, ins, out, stop=None):
        self.nc, self.ins, self.out, self.stop = nc, ins, out, stop
        self.s = Shapes(ins["x"], ins["dst"], ins["L1_gnn_rel_w"], ins["L0_gnn_attn_l"], ins["L0_ffn_W1"], ins["L1_ffn_w1"])
        self.n_sem = 0

    def dram(self, name, shape, dt=F32):
        return self.nc.dram_tensor(name, shape, dt, kind="Internal").ap()


class Stage(ExitStack):

    def __init__(self):
        super().__init__()
        self.semaphores = []


def in_scope(nc, ctx):
    def sb(name, shape, dt=F32):
        return ctx.enter_context(nc.sbuf_tensor(name, shape, dt))

    def psum(name, shape, dt=F32):
        return ctx.enter_context(nc.psum_tensor(name, shape, dt))

    def clear():
        nc.clear_and_free_semaphores(ctx.semaphores)
        nc.all_engine_barrier()

    def sem(name):
        if not ctx.semaphores:
            ctx.callback(clear)
        ctx.semaphores.append(nc.alloc_semaphore(name))
        return ctx.semaphores[-1]

    return sb, psum, sem


def constants(prog, keep):
    nc, s = prog.nc, prog.s
    sb, _, sem = in_scope(nc, keep)
    prog.ident = ident = sb("ident", [P, P])
    prog.below = below = sb("below", [P, P])
    prog.below16 = below16 = sb("below16", [P, P], BF16)
    prog.ones16 = ones16 = sb("ones16", [P, P], BF16)
    prog.bins = bins = sb("bins", [P, P])
    prog.lane = lane = sb("lane", [P, 1])
    prog.node = node = sb("node", [P, s.NT])
    prog.node_i = node_i = sb("node_i", [P, s.NT], I32)
    prog.real = real = sb("real", [P, s.NT])
    with Stage() as ctx:
        _, _, sem = in_scope(nc, ctx)
        made = sem("const_made")
        block = ctx.enter_context(nc.Block())

        @block.gpsimd
        def _(pool):
            nc.gpsimd.memset(ident[:], 0.0)
            nc.gpsimd.memset(below[:], 1.0)
            nc.gpsimd.iota(bins[:], [[1, P]], base=0, channel_multiplier=0, allow_small_or_imprecise_dtypes=True)
            nc.gpsimd.iota(lane[:], [[0, 1]], base=0, channel_multiplier=1, allow_small_or_imprecise_dtypes=True)
            nc.gpsimd.iota(node[:], [[P, s.NT]], base=0, channel_multiplier=1, allow_small_or_imprecise_dtypes=True)
            nc.gpsimd.iota(node_i[:], [[P, s.NT]], base=0, channel_multiplier=1)
            nc.gpsimd.memset(ones16[:], 1.0)
            pool.drain()
            nc.gpsimd.affine_select(out=ident[:], in_=ident[:], compare_op=ALU.not_equal, fill=1.0, base=0,
                                    pattern=[[-1, P]], channel_multiplier=1)
            nc.gpsimd.affine_select(out=below[:], in_=below[:], compare_op=ALU.is_gt, fill=0.0, base=0,
                                    pattern=[[1, P]], channel_multiplier=-1)
            pool.drain()
            nc.gpsimd.tensor_copy(below16[:], below[:])
            nc.gpsimd.tensor_scalar(real[:], node[:], float(s.N), None, ALU.is_lt).then_inc(made, 1)

        @block.vector
        def _(dve):
            dve.wait_ge(made, 1)


def pad_inputs(prog):
    nc, s, ins = prog.nc, prog.s, prog.ins
    prog.xp = xp = prog.dram("x_padded", [s.NP, s.D])
    prog.edges = edges = {k: prog.dram(f"{k}_padded", [s.EP], I32) for k in ("src", "dst", "edge_type_64")}
    fill = {"src": 0, "dst": s.NP + P * 8, "edge_type_64": 0}
    cut = 50
    extra = s.EP - s.E
    with Stage() as ctx:
        sb, _, sem = in_scope(nc, ctx)
        zeros = sb("pad_zeros", [P, s.D])
        pads = sb("pad_edges", [1, 3, extra], I32)
        made, copied = sem("pad_made"), sem("pad_copied")
        block = ctx.enter_context(nc.Block())

        @block.vector
        def _(dve):
            nc.vector.memset(zeros[:], 0.0)
            for j, k in enumerate(edges):
                nc.vector.memset(pads[:, j, :], fill[k])
            dve.drain()
            nc.vector.memset(zeros[0:1, 0:1], 0.0).then_inc(made, 1)

        @block.sync
        def _(sp):
            sp.dma_start(xp[0:s.N, :], ins["x"][:, :]).then_inc(copied, 16)
            for k in edges:
                sp.dma_start(edges[k][0:s.E].rearrange("(a b) -> a b", a=cut),
                             ins[k].rearrange("(a b) -> a b", a=cut)).then_inc(copied, 16)
            sp.wait_ge(made, 1)
            sp.dma_start(xp[s.N:s.NP, :], zeros[0:s.NP - s.N, :]).then_inc(copied, 16)
            for j, k in enumerate(edges):
                sp.dma_start(edges[k][s.E:s.EP].rearrange("(a b) -> a b", a=1), pads[:, j, :]).then_inc(copied, 16)
            sp.wait_ge(copied, 16 * 8)


def project(prog, ctx, tag, tiles, tiles_ready, w, width, used):
    nc, s = prog.nc, prog.s
    sb, psum, sem = in_scope(nc, ctx)
    halves = -(-width // 512)
    turned = psum(f"{tag}_turned", [P, 2, 512])
    out = psum(f"{tag}_out", [P, 2, halves * 512])
    cols = sb(f"{tag}_cols", [P, 2, s.DK * P])
    turned_done, cols_ready, done = sem(f"{tag}_turned_done"), sem(f"{tag}_cols_ready"), sem(f"{tag}_done")

    def before(k):
        return 1 if k == 0 else 2

    def turn(pe, i, k):
        n = i * s.U + k
        pe.wait_ge(tiles_ready, n + 1)
        if not (isinstance(i, int) and n < 2):
            pe.wait_ge(cols_ready, n - before(k) + 1)
        for c in range(s.DK):
            m = nc.tensor.transpose(turned[:, k % 2, c * P:(c + 1) * P], tiles[:, k, c * P:(c + 1) * P], prog.ident[:])
        m.then_inc(turned_done, 1)

    def multiply(pe, i, k):
        n = i * s.U + k
        pe.wait_ge(cols_ready, n + 1)
        if not (isinstance(i, int) and n < 2):
            used(pe, n - before(k) + 1)
        for h in range(halves):
            a, b = h * 512, min(width, h * 512 + 512)
            for c in range(s.DK):
                m = nc.tensor.matmul(out[:, k % 2, a:b], cols[:, k % 2, c * P:(c + 1) * P], w[:, c, a:b],
                                     start=c == 0, stop=c == s.DK - 1)
        m.then_inc(done, 1)

    def copy_cols(act, i, k):
        n = i * s.U + k
        act.wait_ge(turned_done, n + 1)
        if not (isinstance(i, int) and n < 2):
            act.wait_ge(done, n - before(k) + 1)
        nc.scalar.activation(cols[:, k % 2, :], turned[:, k % 2, 0:s.DK * P], ACT.Copy).then_inc(cols_ready, 1)

    def run_pe(pe, i):
        for k in range(s.U):
            turn(pe, i, k)
            if k:
                multiply(pe, i, k - 1)
        multiply(pe, i, s.U - 1)

    return out, done, turned_done, run_pe, copy_cols


def rounds(eng, s, body):
    body(0)
    with eng.Fori(1, s.IT) as i:
        body(i)


class LayerNorm:

    def __init__(self, prog, ctx, tag):
        sb, _, sem = in_scope(prog.nc, ctx)
        self.nc, self.s = prog.nc, prog.s
        self.stats, self.agg = sb(f"{tag}_stats", [P, self.s.U, 6]), sb(f"{tag}_agg", [P, self.s.U, 2])
        self.inverse, self.rstd = sb(f"{tag}_inverse", [P, self.s.U]), sb(f"{tag}_rstd", [P, self.s.U])
        self.var_ready, self.rstd_ready = sem(f"{tag}_var_ready"), sem(f"{tag}_rstd_ready")

    def vector(self, dve, i, src, dst, ready, free=None):
        nc, s = self.nc, self.s
        for k in range(s.U):
            nc.vector.bn_stats(self.stats[:, k, :], src(k))
        dve.drain()
        for k in range(s.U):
            nc.vector.bn_aggr(self.agg[:, k, :], self.stats[:, k, :])
        dve.drain()
        nc.vector.tensor_scalar(self.inverse[:], self.agg[:, :, 1], 1e-5, None, ALU.add)
        dve.drain()
        nc.vector.reciprocal(self.inverse[:], self.inverse[:]).then_inc(self.var_ready, 1)
        dve.wait_ge(self.rstd_ready, i + 1)
        for k in range(s.U):
            if free is not None and not isinstance(i, int):
                dve.wait_ge(free, (i - 1) * s.U + k + 1)
            nc.vector.tensor_scalar(dst(k), src(k), self.agg[:, k, 0:1], self.rstd[:, k:k + 1],
                                    ALU.subtract, ALU.mult).then_inc(ready, 1)

    def vector_end(self, dve):
        dve.drain()
        self.nc.vector.memset(self.inverse[:], 1.0).then_inc(self.var_ready, 1)

    def root(self, act, i):
        act.wait_ge(self.var_ready, i + 1)
        self.nc.scalar.activation(self.rstd[:], self.inverse[:], ACT.Sqrt).then_inc(self.rstd_ready, 1)


def tile_of(buf, n):
    return buf[:, n, :] if isinstance(n, int) else buf[:, bass.ds(n, 1), :].rearrange("p a f -> p (a f)")


def row(ap):
    return ap.rearrange("(a b) -> a b", a=1)


def tile_rows(table, i, s):
    return table.rearrange("(t p) f -> p t f", p=P)[:, bass.ds(i * s.U, s.U), :]


def turn_lists(prog, keep, tag, lists, dt=U32):
    nc = prog.nc
    sbk, _, _ = in_scope(nc, keep)
    m = len(lists)
    cols = sbk(f"{tag}_cols", [P, m, P], dt)
    with Stage() as ctx:
        sb, psum, sem = in_scope(nc, ctx)
        rows = sb(f"{tag}_rows", [P, m, P], I32)
        rows_f = sb(f"{tag}_rows_f", [P, m, P])
        turned = psum(f"{tag}_turned", [P, m, P])
        rows_in, cast, turn_done, ready = sem(f"{tag}_in"), sem(f"{tag}_cast"), sem(f"{tag}_turn"), sem(f"{tag}_ready")
        block = ctx.enter_context(nc.Block())

        @block.sync
        def _(sp):
            for j, l in enumerate(lists):
                sp.dma_start(rows[0:l.shape[0], j, :], l).then_inc(rows_in, 16)

        @block.vector
        def _(dve):
            nc.vector.memset(rows_f[:], 0.0)
            dve.drain()
            dve.wait_ge(rows_in, 16 * m)
            for j, l in enumerate(lists):
                nc.vector.tensor_copy(rows_f[0:l.shape[0], j, :], rows[0:l.shape[0], j, :])
            dve.drain()
            nc.vector.memset(rows[0:1, 0, 0:1], 0).then_inc(cast, 1)
            dve.wait_ge(turn_done, 1)
            nc.vector.tensor_copy(cols[:], turned[:]).then_inc(ready, 1)
            dve.wait_ge(ready, 1)

        @block.tensor
        def _(pe):
            pe.wait_ge(cast, 1)
            for j in range(m):
                t = nc.tensor.transpose(turned[:, j, :], rows_f[:, j, :], prog.ident[:])
            t.then_inc(turn_done, 1)
    return cols


def l0_tables(prog):
    nc, s, ins = prog.nc, prog.s, prog.ins
    H, HD, D = s.H, s.HD, s.D
    W1 = D + 2 * H
    prog.xt_table = xt_table = prog.dram("xt_table", [s.NP, D + H])
    prog.al_table = al_table = prog.dram("al_table", [s.NP, H])
    with Stage() as ctx:
        sb, psum, sem = in_scope(nc, ctx)
        xs = sb("a_x", [P, s.NT, D])
        xn = sb("a_xn", [P, s.U, D])
        w = sb("a_w", [P, s.DK, W1])
        attn = sb("a_attn", [P, 2, D])
        prod = sb("a_prod", [P, 2, s.DK, D])
        rows = sb("a_rows", [P, s.U, W1])
        norm = LayerNorm(prog, ctx, "a")
        x_in, w_in, w_ready, xn_ready, rows_ready, stored = (
            sem("a_x_in"), sem("a_w_in"), sem("a_w_ready"), sem("a_xn_ready"), sem("a_rows_ready"), sem("a_stored"))
        out, done, turned, run_pe, copy_cols = project(prog, ctx, "a", xn, xn_ready, w, W1,
                                                       lambda pe, m: pe.wait_ge(rows_ready, m))
        block = ctx.enter_context(nc.Block())

        @block.sync
        def _(sp):
            sp.dma_start(w[:, :, 0:D], ins["L0_gnn_weight"].rearrange("(c p) f -> p c f", p=P)).then_inc(w_in, 16)
            for j, k in enumerate(("L0_gnn_attn_r", "L0_gnn_attn_l")):
                sp.dma_start(attn[:, j, :], row(ins[k].rearrange("h d -> (h d)")).to_broadcast([P, D])).then_inc(w_in, 16)
            def load(i):
                if not isinstance(i, int):
                    sp.wait_ge(x_in, i * 16)
                sp.dma_start(xs[:, bass.ds(i * s.U, s.U), :], tile_rows(prog.xp, i, s)).then_inc(x_in, 16)

            rounds(sp, s, load)

            def store(i):
                sp.wait_ge(rows_ready, (i + 1) * s.U)
                sp.dma_start(tile_rows(xt_table, i, s), rows[:, :, 0:D + H]).then_inc(stored, 16)
                sp.dma_start(tile_rows(al_table, i, s), rows[:, :, D + H:W1]).then_inc(stored, 16)

            with sp.Fori(0, s.IT) as i:
                store(i)
            sp.wait_ge(stored, 32 * s.IT)

        @block.vector
        def _(dve):
            dve.wait_ge(w_in, 48)
            for j in range(2):
                for c in range(s.DK):
                    nc.vector.tensor_tensor(prod[:, j, c, :], w[:, c, 0:D], attn[:, j, :], ALU.mult)
            dve.drain()
            for j in range(2):
                for c in range(s.DK):
                    nc.vector.tensor_reduce(w[:, c, D + j * H:D + j * H + H],
                                            prod[:, j, c, :].rearrange("p (h d) -> p h d", h=H), AX.X, ALU.add)
            dve.drain()
            nc.vector.tensor_copy(attn[0:1, 0, 0:1], w[0:1, 0, 0:1]).then_inc(w_ready, 1)

            def body(i):
                if not isinstance(i, int):
                    dve.drain()
                dve.wait_ge(x_in, (i + 1) * 16)
                norm.vector(dve, i, lambda k: tile_of(xs, i * s.U + k), lambda k: xn[:, k, :], xn_ready, turned)

            rounds(dve, s, body)
            norm.vector_end(dve)

        @block.tensor
        def _(pe):
            pe.wait_ge(w_ready, 1)
            rounds(pe, s, lambda i: run_pe(pe, i))

        @block.scalar
        def _(act):
            def keep(i, k):
                n = i * s.U + k
                act.wait_ge(done, n + 1)
                if k == 0 and not isinstance(i, int):
                    act.wait_ge(stored, i * 32)
                nc.scalar.activation(rows[:, k, :], out[:, k % 2, 0:W1], ACT.Copy).then_inc(rows_ready, 1)

            def body(i):
                for k in range(s.U):
                    copy_cols(act, i, k)
                    if k:
                        keep(i, k - 1)
                    if k == s.U // 2:
                        norm.root(act, i + 1)
                keep(i, s.U - 1)

            norm.root(act, 0)
            rounds(act, s, body)


def cols_of(buf, i, s):
    return buf[:, bass.ds(i * s.U, s.U)]


def gather(nc, out, table, index, rows):
    return nc.gpsimd.indirect_dma_start(out=out, out_offset=None, in_=table,
                                        in_offset=bass.IndirectOffsetOnAxis(ap=index, axis=0),
                                        bounds_check=rows - 1, oob_is_err=False)


def scatter(nc, table, index, data, rows):
    return nc.gpsimd.indirect_dma_start(out=table, out_offset=bass.IndirectOffsetOnAxis(ap=index, axis=0),
                                        in_=data, in_offset=None, bounds_check=rows - 1, oob_is_err=False)


def l0_attend(prog, keep):
    nc, s, ins = prog.nc, prog.s, prog.ins
    H, HD, D, U = s.H, s.HD, s.D, s.U
    sbk, _, _ = in_scope(nc, keep)
    prog.x = xs = sbk("x_now", [P, s.NT, D])
    prog.logits = logits = sbk("logits", [P, s.NT, s.X])
    prog.xn_table = xn_table = prog.dram("xn_table", [s.NP, D])
    with Stage() as ctx:
        sb, psum, sem = in_scope(nc, ctx)
        ends = turn_lists(prog, ctx, "ends", [prog.edges[k][0:s.NP].rearrange("(t p) -> t p", p=P)
                                              for k in ("dst", "src")])
        ends_now = sb("b_ends_now", [P, 2, U], U32)
        xt = sb("b_xt", [P, U, D + H])
        al = sb("b_al", [P, U, H])
        z = sb("b_z", [P, U, H])
        zs = sb("b_zs", [P, U, H])
        top = sb("b_top", [P, U])
        ez = sb("b_ez", [P, U, H])
        total = sb("b_total", [P, U])
        prod = sb("b_prod", [P, U, D])
        tmp = sb("b_tmp", [P, U, HD])
        xn = sb("b_xn", [P, U, D])
        w = sb("b_w", [P, s.DK, s.X])
        bias = sb("b_bias", [P, 2, s.X])
        norm = LayerNorm(prog, ctx, "b")
        x_in, w_in = sem("b_x_in"), sem("b_w_in")
        rows_in = [sem(f"b_rows_in{k}") for k in range(U)]
        shifted, exp_done, rows_used = sem("b_shifted"), sem("b_exp_done"), sem("b_rows_used")
        xn_ready, kept, stored, ended = sem("b_xn_ready"), sem("b_kept"), sem("b_stored"), sem("b_ended")
        out, done, turned, run_pe, copy_cols = project(prog, ctx, "b", xn, xn_ready, w, s.X,
                                                       lambda pe, m: pe.wait_ge(kept, m))
        block = ctx.enter_context(nc.Block())

        @block.sync
        def _(sp):
            sp.dma_start(w[:], ins["L0_ffn_Wg"].rearrange("(c p) f -> p c f", p=P)).then_inc(w_in, 16)
            for j, k in enumerate(("L0_ffn_bg", "L0_ffn_bias")):
                sp.dma_start(bias[:, j, :], row(ins[k]).to_broadcast([P, s.X])).then_inc(w_in, 16)

            def body(i):
                if not isinstance(i, int):
                    sp.wait_ge(x_in, i * 16)
                sp.dma_start(xs[:, bass.ds(i * U, U), :], tile_rows(prog.xp, i, s)).then_inc(x_in, 16)
                sp.wait_ge(xn_ready, (i + 1) * U)
                sp.dma_start(tile_rows(xn_table, i, s), xn[:]).then_inc(stored, 16)

            rounds(sp, s, body)
            sp.wait_ge(stored, 16 * s.IT)

        @block.gpsimd
        def _(pool):
            def body(i):
                if not isinstance(i, int):
                    pool.wait_ge(rows_used, i)
                for j in range(2):
                    nc.gpsimd.tensor_copy(ends_now[:, j, :], ends[:, j, bass.ds(i * U, U)])
                pool.drain()
                for k in range(U):
                    gather(nc, xt[:, k, :], prog.xt_table, ends_now[:, 0, k:k + 1], s.NP).then_inc(rows_in[k], 16)
                    gather(nc, al[:, k, :], prog.al_table, ends_now[:, 1, k:k + 1], s.NP).then_inc(rows_in[k], 16)

            rounds(pool, s, body)

        @block.vector
        def _(dve):
            def body(i):
                if not isinstance(i, int):
                    dve.drain()
                for k in range(U):
                    dve.wait_ge(rows_in[k], (i + 1) * 32)
                nc.vector.tensor_tensor(z[:], xt[:, :, D:D + H], al[:], ALU.add)
                dve.drain()
                nc.vector.scalar_tensor_tensor(out=zs[:], in0=z[:], scalar=0.01, in1=z[:], op0=ALU.mult, op1=ALU.max)
                dve.drain()
                nc.vector.tensor_reduce(top[:], zs[:], AX.X, ALU.max)
                dve.drain()
                nc.vector.tensor_tensor(zs[:], zs[:], columns(top, [P, U, H]), ALU.subtract).then_inc(shifted, 1)
                dve.wait_ge(exp_done, i + 1)
                nc.vector.tensor_reduce(total[:], ez[:], AX.X, ALU.add)
                dve.drain()
                nc.vector.reciprocal(total[:], total[:])
                dve.drain()
                nc.vector.tensor_tensor(ez[:], ez[:], columns(total, [P, U, H]), ALU.mult)
                dve.drain()
                nc.vector.tensor_tensor(prod[:].rearrange("p u (h d) -> p u h d", h=H),
                                        xt[:, :, 0:D].rearrange("p u (h d) -> p u h d", h=H),
                                        ez[:].unsqueeze(3).to_broadcast([P, U, H, HD]), ALU.mult).then_inc(rows_used, 1)
                dve.drain()
                nc.vector.tensor_reduce(tmp[:], prod[:].rearrange("p u (h d) -> p u d h", h=H), AX.X, ALU.add)
                dve.drain()
                if not isinstance(i, int):
                    dve.wait_ge(stored, i * 16)
                dve.wait_ge(x_in, (i + 1) * 16)
                now = xs[:, bass.ds(i * U, U), :].rearrange("p u (h d) -> p u h d", h=H)
                nc.vector.tensor_tensor(now, now, tmp[:].unsqueeze(2).to_broadcast([P, U, H, HD]), ALU.add)
                dve.drain()
                norm.vector(dve, i, lambda k: tile_of(xs, i * U + k), lambda k: xn[:, k, :], xn_ready, turned)

            rounds(dve, s, body)
            norm.vector_end(dve)
            dve.wait_ge(w_in, 48)
            dve.wait_ge(kept, s.NT)
            for j in range(2):
                nc.vector.tensor_tensor(logits[:], logits[:], bias[:, j, :].unsqueeze(1).to_broadcast([P, s.NT, s.X]), ALU.add)
                dve.drain()
            nc.vector.memset(top[:], 0.0).then_inc(ended, 1)

        @block.tensor
        def _(pe):
            pe.wait_ge(w_in, 48)
            rounds(pe, s, lambda i: run_pe(pe, i))

        @block.scalar
        def _(act):
            def expo(i):
                act.wait_ge(shifted, i + 1)
                nc.scalar.activation(ez[:], zs[:], ACT.Exp).then_inc(exp_done, 1)

            def keep_logits(i, k):
                n = i * U + k
                act.wait_ge(done, n + 1)
                nc.scalar.activation(tile_of(logits, n), out[:, k % 2, 0:s.X], ACT.Copy).then_inc(kept, 1)

            def body(i):
                expo(i)
                norm.root(act, i)
                for k in range(U):
                    copy_cols(act, i, k)
                    if k:
                        keep_logits(i, k - 1)
                keep_logits(i, U - 1)

            rounds(act, s, body)


def route(prog, keep, tag, experts, groups):
    nc, s = prog.nc, prog.s
    X, NT, U, GT = s.X, s.NT, s.U, s.GT
    sbk, _, _ = in_scope(nc, keep)
    weight = [sbk(f"{tag}_weight{j}", [P, NT]) for j in range(experts)]
    slot = [sbk(f"{tag}_slot{j}", [P, NT], I32) for j in range(experts)]
    of_group = sbk(f"{tag}_of_group", [1, P], I32)
    slots = groups * GT
    halves = groups * GT // P
    slot_node = prog.dram(f"{tag}_slot_node", [slots, 1], I32)
    with Stage() as ctx:
        sb, psum, sem = in_scope(nc, ctx)
        L = sb(f"{tag}_L", [P, NT, X])
        eq = sb(f"{tag}_eq", [P, NT, X])
        hot = [sb(f"{tag}_hot{j}", [P, X, NT]) for j in range(experts)]
        hot16 = sb(f"{tag}_hot16", [P, X, NT], BF16)
        best = [sb(f"{tag}_best{j}", [P, NT]) for j in range(2)]
        which = sb(f"{tag}_which", [P, NT])
        ex = sb(f"{tag}_ex", [P, NT])
        edge = sb(f"{tag}_edge", [P, X, NT])
        upto = sb(f"{tag}_upto", [P, X, NT])
        place = sb(f"{tag}_place", [P, X, NT])
        tot_i = sb(f"{tag}_tot_i", [P, X], I32)
        ng = sb(f"{tag}_ng", [P, X])
        endg = sb(f"{tag}_endg", [P, X])
        base = sb(f"{tag}_base", [P, X])
        pos = sb(f"{tag}_pos", [P, NT])
        keepm = sb(f"{tag}_keepm", [P, NT])
        scat = [sb(f"{tag}_scat{j}", [P, NT], U32) for j in range(experts)]
        now = sb(f"{tag}_now", [P, experts, U], U32)
        now_node = sb(f"{tag}_now_node", [P, U], I32)
        zeros = sb(f"{tag}_zeros", [P, slots // P], I32)
        gcmp = sb(f"{tag}_gcmp", [1, P, X])
        gex = sb(f"{tag}_gex", [1, P])
        tiles_ps = psum(f"{tag}_tiles_ps", [P, 512])
        below_ps = psum(f"{tag}_below_ps", [P, 512])
        hot_ready, counted, exp_in, exp_done = (sem(f"{tag}_hot_ready"), sem(f"{tag}_counted"), sem(f"{tag}_exp_in"),
                                                sem(f"{tag}_exp_done"))
        placed, zeroed, zero_ready, scattered = (sem(f"{tag}_placed"), sem(f"{tag}_zeroed"), sem(f"{tag}_zero_ready"),
                                                 sem(f"{tag}_scattered"))
        block = ctx.enter_context(nc.Block())
        bins8 = prog.bins[:, 0:X].unsqueeze(1).to_broadcast([P, NT, X])

        @block.sync
        def _(sp):
            sp.wait_ge(zero_ready, 1)
            sp.dma_start(slot_node.rearrange("(p c) a -> p (c a)", p=P), zeros[:]).then_inc(zeroed, 16)

        @block.tensor
        def _(pe):
            pe.wait_ge(hot_ready, 1)
            flat = hot16[:].rearrange("p e t -> p (e t)")
            nc.tensor.matmul(tiles_ps[:, 0:X * NT], prog.ones16[:], flat, start=True, stop=True)
            nc.tensor.matmul(below_ps[:, 0:X * NT], prog.below16[:], flat, start=True, stop=True).then_inc(counted, 1)

        @block.scalar
        def _(act):
            act.wait_ge(exp_in, 1)
            if experts == 2:
                nc.scalar.activation(pos[:], best[1][:], ACT.Exp).then_inc(exp_done, 1)
            else:
                nc.scalar.activation(eq[:], L[:], ACT.Exp).then_inc(exp_done, 1)

        @block.vector
        def _(dve):
            v = nc.vector

            def step(ins):
                dve.drain()
                return ins

            def by_tile(t):
                return t[:].rearrange("p e t -> p t e")

            def per_expert(t):
                return t[:, :].unsqueeze(2).to_broadcast([P, X, NT])

            v.memset(zeros[:], 0).then_inc(zero_ready, 1)
            v.memset(edge[:], 1.0)
            v.tensor_copy(L[:], prog.logits[:])
            step(None)
            v.memset(edge[:, :, 0:1], 0.0)
            for j in range(experts):
                step(v.tensor_reduce(best[j][:], L[:], AX.X, ALU.max))
                step(v.tensor_tensor(eq[:], L[:], columns(best[j], [P, NT, X]), ALU.not_equal))
                step(v.scalar_tensor_tensor(out=eq[:], in0=eq[:], scalar=float(X), in1=bins8, op0=ALU.mult, op1=ALU.add))
                step(v.tensor_reduce(which[:], eq[:], AX.X, ALU.min))
                step(v.tensor_tensor(eq[:], bins8, columns(which, [P, NT, X]), ALU.is_equal))
                step(v.tensor_tensor(by_tile(hot[j]), eq[:], columns(prog.real, [P, NT, X]), ALU.mult))
                if experts == 2 and j == 0:
                    step(v.scalar_tensor_tensor(out=L[:], in0=eq[:], scalar=-3e38, in1=L[:], op0=ALU.mult, op1=ALU.add))
            if experts == 2:
                step(v.tensor_tensor(hot16[:], hot[0][:], hot[1][:], ALU.add))
            else:
                step(v.tensor_copy(hot16[:], hot[0][:]))
            v.memset(now_node[:], 0).then_inc(hot_ready, 1)
            if experts == 2:
                v.tensor_tensor(best[1][:], best[1][:], best[0][:], ALU.subtract).then_inc(exp_in, 1)
                dve.wait_ge(exp_done, 1)
                step(v.tensor_scalar(ex[:], pos[:], 1.0, None, ALU.add))
                step(v.reciprocal(weight[0][:], ex[:]))
                step(v.tensor_tensor(weight[1][:], pos[:], weight[0][:], ALU.mult))
            else:
                v.tensor_tensor(L[:], L[:], columns(best[0], [P, NT, X]), ALU.subtract).then_inc(exp_in, 1)
                dve.wait_ge(exp_done, 1)
                step(v.tensor_reduce(ex[:], eq[:], AX.X, ALU.add))
                step(v.reciprocal(weight[0][:], ex[:]))
            dve.wait_ge(counted, 1)
            flat = lambda t: t[:].rearrange("p e t -> p (e t)")
            step(v.tensor_tensor_scan(flat(upto), flat(edge), tiles_ps[:, 0:X * NT], 0.0, ALU.mult, ALU.add))
            step(v.tensor_tensor(flat(place), flat(upto), tiles_ps[:, 0:X * NT], ALU.subtract))
            step(v.tensor_tensor(flat(place), flat(place), below_ps[:, 0:X * NT], ALU.add))
            if experts == 2:
                step(v.tensor_scalar(tot_i[:], upto[:, :, NT - 1], float(GT - 1), None, ALU.add))
                step(v.tensor_scalar(tot_i[:], tot_i[:], GT.bit_length() - 1, None, ALU.arith_shift_right))
                step(v.tensor_copy(ng[:], tot_i[:]))
                step(v.tensor_tensor_scan(endg[:], ng[:], ng[:], 0.0, ALU.add, ALU.bypass))
            else:
                step(v.memset(ng[:], float(s.GPE)))
                step(v.tensor_tensor_scan(endg[:], ng[:], ng[:], 0.0, ALU.add, ALU.bypass))
            step(v.tensor_tensor(base[:], endg[:], ng[:], ALU.subtract))
            step(v.tensor_scalar(base[:], base[:], float(GT), None, ALU.mult))
            if experts == 2:
                step(v.tensor_tensor(place[:], place[:], per_expert(base), ALU.add))
            for j in range(experts):
                step(v.tensor_tensor(upto[:], hot[j][:], place[:], ALU.mult))
                step(v.tensor_reduce(pos[:], by_tile(upto), AX.X, ALU.add))
                if experts == 2:
                    step(v.tensor_copy(slot[j][:], pos[:]))
                    step(v.tensor_scalar(ex[:], prog.real[:], -float(SKIP), float(SKIP), ALU.mult, ALU.add))
                    step(v.tensor_tensor(scat[j][:], ex[:], pos[:], ALU.add))
                else:
                    step(v.tensor_scalar(keepm[:], pos[:], float(s.CAP), None, ALU.is_lt))
                    step(v.tensor_tensor(weight[0][:], weight[0][:], keepm[:], ALU.mult))
                    step(v.tensor_tensor(keepm[:], keepm[:], prog.real[:], ALU.mult))
                    step(v.tensor_scalar(pos[:], pos[:], float(s.CAP - 1), None, ALU.min))
                    step(v.tensor_tensor(upto[:], hot[j][:], per_expert(base), ALU.mult))
                    step(v.tensor_reduce(ex[:], by_tile(upto), AX.X, ALU.add))
                    step(v.tensor_tensor(pos[:], pos[:], ex[:], ALU.add))
                    step(v.tensor_copy(slot[j][:], pos[:]))
                    step(v.tensor_scalar(ex[:], keepm[:], -float(SKIP), float(SKIP), ALU.mult, ALU.add))
                    step(v.tensor_tensor(scat[j][:], ex[:], pos[:], ALU.add))
            step(v.tensor_tensor(gcmp[:], prog.bins[0:1, :].unsqueeze(2).to_broadcast([1, P, X]),
                                 endg[0:1, :].unsqueeze(1).to_broadcast([1, P, X]), ALU.is_ge))
            step(v.tensor_reduce(gex[:], gcmp[:], AX.X, ALU.add))
            v.tensor_scalar(of_group[:], gex[:], float(X - 1), None, ALU.min).then_inc(placed, 1)

        @block.gpsimd
        def _(pool):
            pool.wait_ge(placed, 1)
            pool.wait_ge(zeroed, 16)

            def body(i):
                if not isinstance(i, int):
                    pool.wait_ge(scattered, i * 16 * U * experts)
                for j in range(experts):
                    nc.gpsimd.tensor_copy(now[:, j, :], cols_of(scat[j], i, s))
                nc.gpsimd.tensor_copy(now_node[:], cols_of(prog.node_i, i, s))
                pool.drain()
                for k in range(U):
                    for j in range(experts):
                        scatter(nc, slot_node, now[:, j, k:k + 1], now_node[:, k:k + 1], slots).then_inc(scattered, 16)

            rounds(pool, s, body)
            pool.wait_ge(scattered, 16 * U * experts * s.IT)
    return weight, slot, slot_node, of_group


def mlp(prog, tag, table, slot_node, of_group, groups, F, w1, b1, w2, b2):
    nc, s = prog.nc, prog.s
    D, DK, GT, X = s.D, s.DK, s.GT, s.X
    FC = F // P
    SUB = GT // P
    sub_all = groups * SUB
    y_table = prog.dram(f"{tag}_y", [groups * GT, D])
    with Stage() as ctx:
        sb, psum, sem = in_scope(nc, ctx)
        node_rows = sb(f"{tag}_node_rows", [P, P], I32)
        node_f = sb(f"{tag}_node_f", [P, P])
        nodes = sb(f"{tag}_nodes", [P, P], U32)
        b1_rows = sb(f"{tag}_b1_rows", [P, P])
        b1_cols = sb(f"{tag}_b1_cols", [P, P])
        nodes_now = sb(f"{tag}_nodes_now", [P, 2, SUB], U32)
        xg = sb(f"{tag}_xg", [P, 2, SUB, D])
        xT = sb(f"{tag}_xT", [P, 2, DK * GT])
        w1s = sb(f"{tag}_w1s", [P, 2, DK, F])
        w2s = sb(f"{tag}_w2s", [P, 2, FC, D])
        b2s = sb(f"{tag}_b2s", [P, 2, D])
        hT = sb(f"{tag}_hT", [P, 2, FC, GT])
        ys = sb(f"{tag}_ys", [P, 2, SUB, D])
        turned = psum(f"{tag}_turned", [P, 2, 512])
        hid = psum(f"{tag}_hid", [P, 4, 512])
        yp = psum(f"{tag}_yp", [P, 2, 512])
        lists_in, lists_f, lists_T, lists_ready = (sem(f"{tag}_lists_in"), sem(f"{tag}_lists_f"), sem(f"{tag}_lists_T"),
                                                   sem(f"{tag}_lists_ready"))
        w_in = [sem(f"{tag}_w_in{j}") for j in range(2)]
        x_in = [sem(f"{tag}_x_in{j}") for j in range(2)]
        y_out = [sem(f"{tag}_y_out{j}") for j in range(2)]
        turn_done, xT_ready, hid_done, h_ready = (sem(f"{tag}_turn_done"), sem(f"{tag}_xT_ready"), sem(f"{tag}_hid_done"),
                                                  sem(f"{tag}_h_ready"))
        y_done, y_ready, cleared = sem(f"{tag}_y_done"), sem(f"{tag}_y_ready"), sem(f"{tag}_cleared")
        block = ctx.enter_context(nc.Block())

        def pairs(eng, body):
            for j in range(2):
                body(0, j)
            with eng.Fori(1, groups // 2) as i:
                for j in range(2):
                    body(i, j)

        def later(i):
            return not isinstance(i, int)

        @block.sync
        def _(sp):
            sp.dma_start(node_rows[0:sub_all, :], slot_node.rearrange("(c p) a -> c (p a)", p=P)).then_inc(lists_in, 16)
            sp.wait_ge(cleared, 1)
            sp.dma_start(b1_rows[0:X * FC, :], b1.rearrange("e (c p) -> (e c) p", p=P)).then_inc(lists_in, 16)

            def store(i, j):
                sp.dma_start(y_table[bass.ds((i * 2 + j) * GT, GT), :].rearrange("(c p) f -> p c f", p=P),
                             ys[:, j]).then_inc(y_out[j], 16)

            def body(i, j):
                e = sp.value_load(of_group[0:1, bass.ds(i * 2 + j, 1)], min_val=0, max_val=X - 1)
                if later(i):
                    sp.wait_ge(y_ready, i * 2 + j - 1)
                    store(i - 1, j)
                sp.dma_start(w1s[:, j], w1[bass.ds(e, 1)].rearrange("a (c p) f -> p (a c) f", p=P)).then_inc(w_in[j], 16)
                sp.dma_start(w2s[:, j], w2[bass.ds(e, 1)].rearrange("a (c p) f -> p (a c) f", p=P)).then_inc(w_in[j], 16)
                sp.dma_start(b2s[:, j], b2[bass.ds(e, 1), :].to_broadcast([P, D])).then_inc(w_in[j], 16)

            pairs(sp, body)
            for j in range(2):
                sp.wait_ge(y_ready, groups - 1 + j)
                store(groups // 2 - 1, j)
            for j in range(2):
                sp.wait_ge(y_out[j], 16 * (groups // 2))

        @block.gpsimd
        def _(pool):
            pool.wait_ge(lists_ready, 1)

            def body(i, j):
                if later(i):
                    pool.wait_ge(turn_done, i * 2 + j - 1)
                nc.gpsimd.tensor_copy(nodes_now[:, j, :], nodes[:, bass.ds((i * 2 + j) * SUB, SUB)])
                pool.drain()
                for c in range(SUB):
                    gather(nc, xg[:, j, c, :], table, nodes_now[:, j, c:c + 1], s.NP).then_inc(x_in[j], 16)

            pairs(pool, body)

        @block.tensor
        def _(pe):
            pe.wait_ge(lists_f, 1)
            nc.tensor.transpose(turned[:, 0, 0:P], node_f[:], prog.ident[:])
            nc.tensor.transpose(turned[:, 1, 0:P], b1_rows[:], prog.ident[:]).then_inc(lists_T, 1)
            pe.wait_ge(lists_ready, 1)

            def turn(i, j):
                pe.wait_ge(x_in[j], (i + 1) * 16 * SUB)
                if later(i):
                    pe.wait_ge(xT_ready, i * 2 + j - 1)
                for c in range(DK):
                    for t in range(SUB):
                        m = nc.tensor.transpose(turned[:, j, c * GT + t * P:c * GT + (t + 1) * P],
                                                xg[:, j, t, c * P:(c + 1) * P], prog.ident[:])
                m.then_inc(turn_done, 1)

            def first(i, j):
                g = i * 2 + j
                pe.wait_ge(xT_ready, g + 1)
                pe.wait_ge(w_in[j], (i + 1) * 48)
                for f in range(FC):
                    if later(i) or j * FC + f >= 4:
                        pe.wait_ge(h_ready, g * FC + f - 3)
                    for c in range(DK):
                        m = nc.tensor.matmul(hid[:, f % 4, 0:GT], w1s[:, j, c, f * P:(f + 1) * P],
                                             xT[:, j, c * GT:(c + 1) * GT], start=c == 0, stop=c == DK - 1)
                    m.then_inc(hid_done, 1)

            def second(i, j):
                g = i * 2 + j
                pe.wait_ge(h_ready, (g + 1) * FC)
                for t in range(SUB):
                    if later(i) or j * SUB + t >= 2:
                        pe.wait_ge(y_ready, g)
                    for f in range(FC):
                        m = nc.tensor.matmul(yp[:, t, 0:D], hT[:, j, f, t * P:(t + 1) * P], w2s[:, j, f, :],
                                             start=f == 0, stop=f == FC - 1)
                    m.then_inc(y_done, 1)

            def body(i, j):
                turn(i, j)
                if later(i) or j:
                    second(*((i, 0) if j else (i - 1, 1)))
                first(i, j)

            pairs(pe, body)
            second(groups // 2 - 1, 1)

        @block.scalar
        def _(act):
            act.wait_ge(lists_ready, 1)

            def body(i, j):
                g = i * 2 + j
                e = act.value_load(of_group[0:1, bass.ds(g, 1)], min_val=0, max_val=X - 1)
                act.wait_ge(turn_done, g + 1)
                if later(i):
                    act.wait_ge(hid_done, (g - 1) * FC)
                nc.scalar.activation(xT[:, j, :], turned[:, j, :], ACT.Copy).then_inc(xT_ready, 1)
                if later(i):
                    act.wait_ge(y_done, (g - 1) * SUB)
                for f in range(FC):
                    act.wait_ge(hid_done, g * FC + f + 1)
                    nc.scalar.activation(hT[:, j, f, :], hid[:, f % 4, 0:GT], ACT.Relu,
                                         bias=b1_cols[:, bass.ds(e * FC + f, 1)]).then_inc(h_ready, 1)

            pairs(act, body)

        @block.vector
        def _(dve):
            nc.vector.memset(node_f[:], 0.0)
            nc.vector.memset(b1_rows[:], 0.0).then_inc(cleared, 1)
            dve.drain()
            dve.wait_ge(lists_in, 32)
            nc.vector.tensor_copy(node_f[0:sub_all, :], node_rows[0:sub_all, :]).then_inc(lists_f, 1)
            dve.wait_ge(lists_T, 1)
            nc.vector.tensor_copy(nodes[:], turned[:, 0, 0:P])
            nc.vector.tensor_copy(b1_cols[:], turned[:, 1, 0:P])
            dve.drain()
            nc.vector.memset(node_f[:], 0.0).then_inc(lists_ready, 1)

            def body(i, j):
                g = i * 2 + j
                dve.wait_ge(w_in[j], (i + 1) * 48)
                if later(i):
                    dve.wait_ge(y_out[j], i * 16)
                for t in range(SUB):
                    dve.wait_ge(y_done, g * SUB + t + 1)
                    m = nc.vector.tensor_tensor(ys[:, j, t, :], yp[:, t, 0:D], b2s[:, j, :], ALU.add)
                m.then_inc(y_ready, 1)

            pairs(dve, body)
    return y_table


def l1_tables(prog, weight, slot, y_table):
    nc, s, ins = prog.nc, prog.s, prog.ins
    H, HD, D, U = s.H, s.HD, s.D, s.U
    HV = HD + 1
    KV = D + H * HV
    xs = prog.x
    prog.q_table = q_table = prog.dram("q_table", [s.NP, D])
    prog.kv_table = kv_table = prog.dram("kv_table", [s.NP, KV])
    prog.nx_table = nx_table = prog.dram("nx_table", [s.NP, 2 * D])
    scale = HD ** -0.5
    with Stage() as ctx:
        sb, psum, sem = in_scope(nc, ctx)
        slot_now = sb("d_slot_now", [P, 2, U], U32)
        y = sb("d_y", [P, 2, U, D])
        xn = sb("d_xn", [P, U, D])
        enh = sb("d_enh", [P, U, D])
        w = sb("d_w", [P, s.DK, 3 * D])
        bias = sb("d_bias", [P, 3 * D])
        query = sb("d_query", [P, D])
        rows = sb("d_rows", [P, U, D + KV])
        norm = LayerNorm(prog, ctx, "d")
        y_in = [sem(f"d_y_in{k}") for k in range(U)]
        w_in, w_ready, summed = sem("d_w_in"), sem("d_w_ready"), sem("d_summed")
        xn_ready, enh_ready, rows_ready, stored = sem("d_xn_ready"), sem("d_enh_ready"), sem("d_rows_ready"), sem("d_stored")
        out, done, turned, run_pe, copy_cols = project(prog, ctx, "d", enh, enh_ready, w, 3 * D,
                                                       lambda pe, m: pe.wait_ge(rows_ready, m))
        block = ctx.enter_context(nc.Block())

        @block.sync
        def _(sp):
            for j, k in enumerate(("q", "k", "v")):
                sp.dma_start(w[:, :, j * D:(j + 1) * D], ins[f"L1_gnn_W{k}"].rearrange("(c p) f -> p c f", p=P)).then_inc(w_in, 16)
                sp.dma_start(bias[:, j * D:(j + 1) * D], row(ins[f"L1_gnn_b{k}"]).to_broadcast([P, D])).then_inc(w_in, 16)
            sp.dma_start(query[:], row(ins["L1_gnn_query_emb"]).to_broadcast([P, D])).then_inc(w_in, 16)

            def body(i):
                sp.wait_ge(xn_ready, (i + 1) * U)
                nx = tile_rows(nx_table, i, s)
                sp.dma_start(nx[:, :, 0:D], xn[:]).then_inc(stored, 16)
                sp.dma_start(nx[:, :, D:2 * D], xs[:, bass.ds(i * U, U), :]).then_inc(stored, 16)
                sp.wait_ge(rows_ready, (i + 1) * U)
                sp.dma_start(tile_rows(q_table, i, s), rows[:, :, 0:D]).then_inc(stored, 16)
                sp.dma_start(tile_rows(kv_table, i, s), rows[:, :, D:D + KV]).then_inc(stored, 16)

            rounds(sp, s, body)
            sp.wait_ge(stored, 64 * s.IT)

        @block.gpsimd
        def _(pool):
            def body(i):
                if not isinstance(i, int):
                    pool.wait_ge(summed, i)
                for j in range(2):
                    nc.gpsimd.tensor_copy(slot_now[:, j, :], cols_of(slot[j], i, s).bitcast(U32))
                pool.drain()
                for k in range(U):
                    for j in range(2):
                        gather(nc, y[:, j, k, :], y_table, slot_now[:, j, k:k + 1], s.GA * s.GT).then_inc(y_in[k], 16)

            rounds(pool, s, body)

        @block.vector
        def _(dve):
            nc.vector.memset(rows[:], 1.0)
            dve.drain()
            dve.wait_ge(w_in, 16 * 7)
            nc.vector.tensor_scalar(w[:, :, 0:D], w[:, :, 0:D], scale, None, ALU.mult)
            nc.vector.tensor_scalar(bias[:, 0:D], bias[:, 0:D], scale, None, ALU.mult)
            nc.vector.tensor_scalar(query[:], query[:], 0.1, None, ALU.mult)
            dve.drain()
            nc.vector.memset(enh[:], 0.0).then_inc(w_ready, 1)
            dve.wait_ge(w_ready, 1)

            def gathered(i):
                for k in range(U):
                    dve.wait_ge(y_in[k], (i + 1) * 32)
                for k in range(U):
                    n = i * U + k
                    x = tile_of(xs, n)
                    wt = [weight[j][:, n:n + 1] if isinstance(n, int) else weight[j][:, bass.ds(n, 1)] for j in range(2)]
                    nc.vector.scalar_tensor_tensor(out=x, in0=y[:, 0, k, :], scalar=wt[0], in1=x, op0=ALU.mult, op1=ALU.add)
                dve.drain()
                for k in range(U):
                    n = i * U + k
                    x = tile_of(xs, n)
                    wt = [weight[j][:, n:n + 1] if isinstance(n, int) else weight[j][:, bass.ds(n, 1)] for j in range(2)]
                    m = nc.vector.scalar_tensor_tensor(out=x, in0=y[:, 1, k, :], scalar=wt[1], in1=x, op0=ALU.mult, op1=ALU.add)
                m.then_inc(summed, 1)

            def keep_rows(i):
                for k in range(U):
                    n = i * U + k
                    dve.wait_ge(done, n + 1)
                    nc.vector.tensor_tensor(rows[:, k, 0:2 * D], out[:, k % 2, 0:2 * D], bias[:, 0:2 * D], ALU.add)
                    nc.vector.tensor_tensor(rows[:, k, 2 * D:D + KV].rearrange("p (h d) -> p h d", h=H)[:, :, 0:HD],
                                            out[:, k % 2, 2 * D:3 * D].rearrange("p (h d) -> p h d", h=H),
                                            bias[:, 2 * D:3 * D].rearrange("p (h d) -> p h d", h=H), ALU.add).then_inc(rows_ready, 1)

            def body(i):
                if not isinstance(i, int):
                    dve.drain()
                    dve.wait_ge(stored, i * 64)
                gathered(i)
                dve.drain()
                norm.vector(dve, i, lambda k: tile_of(xs, i * U + k), lambda k: xn[:, k, :], xn_ready)
                dve.drain()
                for k in range(U):
                    if not isinstance(i, int):
                        dve.wait_ge(turned, (i - 1) * U + k + 1)
                    nc.vector.tensor_tensor(enh[:, k, :], xn[:, k, :], query[:], ALU.add).then_inc(enh_ready, 1)
                keep_rows(i)

            rounds(dve, s, body)
            norm.vector_end(dve)

        @block.tensor
        def _(pe):
            pe.wait_ge(w_ready, 1)
            rounds(pe, s, lambda i: run_pe(pe, i))

        @block.scalar
        def _(act):
            def body(i):
                norm.root(act, i)
                for k in range(U):
                    copy_cols(act, i, k)

            rounds(act, s, body)


def edge_windows(prog):
    nc, s = prog.nc, prog.s
    B, EC = s.B, s.EC
    WW = s.WIN + B
    rows = EC // B
    assert s.NP < 1 << 16 and s.RELS < 1 << 16
    prog.windows = windows = prog.dram("edge_windows", [s.NB, 2 * WW], U16)
    with Stage() as ctx:
        sb, _, sem = in_scope(nc, ctx)
        lists = sb("e_lists", [P, 2, EC + WW], I32)
        wide = sb("e_wide", [P, rows, 2, WW], U16)
        cleared, lists_in, ready, stored = sem("e_cleared"), sem("e_lists_in"), sem("e_ready"), sem("e_stored")
        block = ctx.enter_context(nc.Block())

        @block.sync
        def _(sp):
            sp.wait_ge(cleared, 1)
            for j, k in enumerate(("src", "edge_type_64")):
                sp.dma_start(lists[:, j, 0:EC], prog.edges[k].rearrange("(p c) -> p c", p=P)).then_inc(lists_in, 16)
                sp.dma_start(lists[0:P - 1, j, EC:EC + WW],
                             prog.edges[k][EC:s.EP].rearrange("(p c) -> p c", c=EC)[:, 0:WW]).then_inc(lists_in, 16)
            sp.wait_ge(ready, 2 * WW // B)
            sp.dma_start(windows.rearrange("(p r) f -> p (r f)", p=P), wide[:].rearrange("p r k w -> p (r k w)")).then_inc(stored, 16)
            sp.wait_ge(stored, 16)

        @block.vector
        def _(dve):
            nc.vector.memset(lists[:], 0).then_inc(cleared, 1)
            dve.wait_ge(lists_in, 64)
            for k in range(2):
                for j in range(0, WW, B):
                    nc.vector.tensor_copy(wide[:, :, k, j:j + B],
                                          lists[:, k, j:j + EC].rearrange("p (r b) -> p r b", b=B)).then_inc(ready, 1)


def node_order(prog, keep):
    nc, s = prog.nc, prog.s
    NT, EC, U, B = s.NT, s.EC, s.U, s.B
    CB = 13
    steps = EC // CB
    assert EC % CB == 0 and steps % 2 == 0
    sbk, _, _ = in_scope(nc, keep)
    prog.sorted_node = sbk("sorted_node", [P, NT + 1], U32)
    prog.sorted_node_f = sbk("sorted_node_f", [P, NT + 1])
    prog.sorted_row = sbk("sorted_row", [P, NT + 1], U32)
    prog.sorted_shift = sbk("sorted_shift", [P, B, NT + 1])
    prog.sorted_deg = sbk("sorted_deg", [P, NT + 1])
    prog.trips = trips = sbk("trips", [1, P], I32)
    table = prog.dram("sorted_table", [s.NP, 4])
    with Stage() as ctx:
        sb, psum, sem = in_scope(nc, ctx)
        stay = ctx.enter_context(Stage())
        count = sb("n_count", [P, P])
        col = sb("n_col", [P, 3, P])
        with Stage() as inner:
            sb1, psum1, sem1 = in_scope(nc, inner)
            dst = sb1("n_dst", [P, EC], I32)
            part = sb1("n_part", [P, EC], I32)
            hi = sb1("n_hi", [P, EC])
            lo = sb1("n_lo", [P, EC])
            hot_hi = sb1("n_hot_hi", [P, 2, CB, P], BF16)
            hot_lo = sb1("n_hot_lo", [P, 2, CB, P], BF16)
            hist = psum1("n_hist", [P, P])
            dst_in, hot_ready, used, zero = sem1("n_dst_in"), sem1("n_hot_ready"), sem1("n_used"), sem1("n_zero")
            counted = sem1("n_counted")
            block = inner.enter_context(nc.Block())

            def pairs(eng, body):
                for j in range(2):
                    body(0, j)
                with eng.Fori(1, steps // 2) as i:
                    for j in range(2):
                        body(i, j)

            @block.sync
            def _(sp):
                sp.dma_start(dst[:], prog.edges["dst"].rearrange("(p c) -> p c", p=P)).then_inc(dst_in, 16)

            @block.vector
            def _(dve):
                v = nc.vector
                v.memset(hot_hi[:], 0.0)
                dve.wait_ge(dst_in, 16)
                v.tensor_scalar(part[:], dst[:], 7, None, ALU.arith_shift_right)
                dve.drain()
                v.tensor_copy(hi[:], part[:])
                dve.drain()
                v.tensor_scalar(part[:], dst[:], P - 1, None, ALU.bitwise_and)
                dve.drain()
                v.tensor_copy(lo[:], part[:])
                dve.drain()

                def body(i, j):
                    g = i * 2 + j
                    if not isinstance(i, int):
                        dve.wait_ge(used, g - 1)
                    for hot, src, n in ((hot_hi, hi, NT), (hot_lo, lo, P)):
                        m = v.tensor_tensor(hot[:, j, :, 0:n], prog.bins[:, 0:n].unsqueeze(1).to_broadcast([P, CB, n]),
                                            src[:, bass.ds(g * CB, CB)].unsqueeze(2).to_broadcast([P, CB, n]), ALU.is_equal)
                    m.then_inc(hot_ready, 1)

                pairs(dve, body)
                dve.wait_ge(used, steps)
                v.tensor_copy(count[:], hist[:]).then_inc(counted, 1)

            @block.tensor
            def _(pe):
                def body(i, j):
                    g = i * 2 + j
                    pe.wait_ge(hot_ready, g + 1)
                    for c in range(CB):
                        first = isinstance(i, int) and j == 0 and c == 0
                        m = nc.tensor.matmul(hist[:], hot_hi[:, j, c, :], hot_lo[:, j, c, :], start=first, stop=True,
                                             skip_group_check=True)
                    m.then_inc(used, 1)

                pairs(pe, body)

        with Stage() as inner:
            sb1, psum1, sem1 = in_scope(nc, inner)
            upto = sb1("n_upto", [P, P])
            first = sb1("n_first", [P, P])
            work_i = sb1("n_work_i", [P, 2, P], I32)
            blk = sb1("n_blk", [P, 3, P])
            ps_base = psum1("n_ps_base", [P, 512])
            ps_turn = psum1("n_ps_turn", [P, 3, P])
            scanned, based, ready, turn_done, done = (sem1("n_scanned"), sem1("n_based"), sem1("n_ready"),
                                                      sem1("n_turn_done"), sem1("n_end"))
            block = inner.enter_context(nc.Block())

            @block.vector
            def _(dve):
                v = nc.vector

                def step(ins):
                    dve.drain()

                step(v.tensor_tensor_scan(upto[:], count[:], count[:], 0.0, ALU.add, ALU.bypass))
                step(v.tensor_tensor(first[:], upto[:], count[:], ALU.subtract))
                v.memset(work_i[:], 0).then_inc(scanned, 1)
                dve.wait_ge(based, 1)
                step(v.tensor_scalar(first[:], first[:], ps_base[:, 0:1], None, ALU.add))
                v.tensor_copy(work_i[:, 0, :], first[:])
                step(v.tensor_copy(work_i[:, 1, :], first[:]))
                v.tensor_scalar(work_i[:, 0, :], work_i[:, 0, :], B.bit_length() - 1, None, ALU.arith_shift_right)
                step(v.tensor_scalar(work_i[:, 1, :], work_i[:, 1, :], B - 1, None, ALU.bitwise_and))
                step(v.tensor_copy(blk[:, 0:2, :], work_i[:]))
                v.tensor_copy(blk[:, 2, :], count[:]).then_inc(ready, 1)
                dve.wait_ge(turn_done, 1)
                v.tensor_copy(col[:], ps_turn[:]).then_inc(done, 1)

            @block.tensor
            def _(pe):
                pe.wait_ge(scanned, 1)
                nc.tensor.matmul(ps_base[:, 0:1], prog.below[:], upto[:, P - 1:P], start=True, stop=True).then_inc(based, 1)
                pe.wait_ge(ready, 1)
                for j in range(3):
                    m = nc.tensor.transpose(ps_turn[:, j, :], blk[:, j, :], prog.ident[:])
                m.then_inc(turn_done, 1)

        with Stage() as inner:
            sb1, psum1, sem1 = in_scope(nc, inner)
            key = sb1("n_key", [P, NT])
            blocks_i = sb1("n_blocks_i", [P, NT], I32)
            hot = sb1("n_hot", [P, P, NT], BF16)
            tiles = sb1("n_tiles", [P, P, NT])
            place = sb1("n_place", [P, P, NT])
            pos = sb1("n_pos", [P, NT])
            pos_u = sb1("n_pos_u", [P, NT], U32)
            data = sb1("n_data", [P, NT, 4])
            now = sb1("n_now", [P, U], U32)
            now_data = sb1("n_now_data", [P, U, 4])
            got = sb1("n_got", [P, NT, 4])
            square = sb1("n_square", [P, P])
            most = sb1("n_most", [P, P])
            trip_f = sb1("n_trip_f", [1, 3, P])
            trip_i = sb1("n_trip_i", [1, 2, P], I32)
            ps = psum1("n_ps", [P, 2, 2, 512])
            ps_sq = psum1("n_ps_sq", [P, 2, P])
            hot_ready, counted, taken, ready, scattered, got_in = (sem1("n_hot_r"), sem1("n_cnt"), sem1("n_taken"),
                                                                   sem1("n_ready2"), sem1("n_scattered"), sem1("n_got_in"))
            sq_ready, sq_done, trips_ready = sem1("n_sq_ready"), sem1("n_sq_done"), sem1("n_trips_ready")
            W = P * NT
            cuts = [(a, min(512, W - a)) for a in range(0, W, 512)]
            block = inner.enter_context(nc.Block())

            def flat(t):
                return t[:].rearrange("p b t -> p (b t)")

            @block.vector
            def _(dve):
                v = nc.vector

                def step(ins):
                    dve.drain()

                step(v.tensor_scalar(blocks_i[:], col[:, 2, 0:NT], float(B - 1), None, ALU.add))
                step(v.tensor_scalar(blocks_i[:], blocks_i[:], B.bit_length() - 1, None, ALU.arith_shift_right))
                step(v.tensor_scalar(key[:], blocks_i[:], float(P - 1), -1.0, ALU.min, ALU.mult))
                step(v.tensor_scalar(key[:], key[:], float(P - 1), None, ALU.add))
                v.tensor_tensor(hot[:], prog.bins[:].unsqueeze(2).to_broadcast([P, P, NT]),
                                key[:].unsqueeze(1).to_broadcast([P, P, NT]), ALU.is_equal).then_inc(hot_ready, 1)
                for n, (a, w) in enumerate(cuts):
                    dve.wait_ge(counted, n + 1)
                    v.tensor_copy(flat(tiles)[:, a:a + w], ps[:, n % 2, 0, 0:w])
                    v.tensor_copy(flat(place)[:, a:a + w], ps[:, n % 2, 1, 0:w]).then_inc(taken, 1)
                dve.drain()
                step(v.tensor_tensor(flat(place), flat(place), flat(tiles), ALU.subtract))
                step(v.tensor_tensor_scan(flat(tiles), flat(tiles), flat(tiles), 0.0, ALU.add, ALU.bypass))
                step(v.tensor_tensor(flat(place), flat(place), flat(tiles), ALU.add))
                step(v.tensor_tensor(flat(place), flat(place), flat(hot), ALU.mult))
                step(v.tensor_reduce(pos[:], place[:].rearrange("p b t -> p t b"), AX.X, ALU.add))
                step(v.tensor_copy(pos_u[:], pos[:]))
                v.tensor_copy(data[:, :, 0], prog.node[:])
                v.tensor_copy(data[:, :, 1], col[:, 0, 0:NT])
                v.tensor_copy(data[:, :, 2], col[:, 1, 0:NT])
                step(v.tensor_copy(data[:, :, 3], col[:, 2, 0:NT]))
                v.memset(square[:], 0.0).then_inc(ready, 1)
                dve.wait_ge(got_in, 16)
                dve.drain()
                v.memset(prog.sorted_node[:, NT:NT + 1], 0)
                v.tensor_copy(prog.sorted_node[:, 0:NT], got[:, :, 0])
                v.memset(prog.sorted_node_f[:, NT:NT + 1], 0.0)
                v.tensor_copy(prog.sorted_node_f[:, 0:NT], got[:, :, 0])
                v.memset(prog.sorted_row[:, NT:NT + 1], 0)
                v.tensor_copy(prog.sorted_row[:, 0:NT], got[:, :, 1])
                v.memset(prog.sorted_deg[:, NT:NT + 1], 0.0)
                v.tensor_copy(prog.sorted_deg[:, 0:NT], got[:, :, 3])
                v.memset(prog.sorted_shift[:, :, NT:NT + 1], 0.0)
                for j in range(B):
                    v.tensor_scalar(prog.sorted_shift[:, j, 0:NT], got[:, :, 2], float(j), None, ALU.is_equal)
                v.tensor_copy(square[:, 0:NT], got[:, :, 3])
                v.memset(most[:], 0.0).then_inc(sq_ready, 1)
                dve.wait_ge(sq_done, 1)
                dve.drain()
                v.tensor_reduce(most[:, 0:1], ps_sq[:, 0, :], AX.X, ALU.max).then_inc(sq_ready, 1)
                dve.wait_ge(sq_done, 2)
                shift = B.bit_length() - 1
                step(v.tensor_scalar(trip_i[:, 0, :], ps_sq[0:1, 1, :], float(B - 1), None, ALU.add))
                step(v.tensor_scalar(trip_i[:, 0, :], trip_i[:, 0, :], shift, None, ALU.arith_shift_right))
                step(v.tensor_scalar(trip_i[:, 0, :], trip_i[:, 0, :], 2, None, ALU.max))
                step(v.tensor_scalar(trip_i[:, 1, :], trip_i[:, 0, :], s.CH - 1, None, ALU.bitwise_and))
                step(v.tensor_scalar(trip_f[:, 1, :], trip_i[:, 1, :], 1.0, None, ALU.is_equal))
                step(v.tensor_tensor(trip_f[:, 0, :], trip_f[:, 1, :], trip_i[:, 0, :], ALU.add))
                step(v.tensor_scalar(trips[:], trip_f[:, 0, :], -1.0, None, ALU.add))
                v.memset(square[:], 0.0).then_inc(trips_ready, 1)

            @block.tensor
            def _(pe):
                pe.wait_ge(hot_ready, 1)
                for n, (a, w) in enumerate(cuts):
                    if n >= 2:
                        pe.wait_ge(taken, n - 1)
                    nc.tensor.matmul(ps[:, n % 2, 0, 0:w], prog.ones16[:], flat(hot)[:, a:a + w], start=True, stop=True)
                    nc.tensor.matmul(ps[:, n % 2, 1, 0:w], prog.below16[:], flat(hot)[:, a:a + w],
                                     start=True, stop=True).then_inc(counted, 1)
                pe.wait_ge(sq_ready, 1)
                nc.tensor.transpose(ps_sq[:, 0, :], square[:], prog.ident[:]).then_inc(sq_done, 1)
                pe.wait_ge(sq_ready, 2)
                nc.tensor.transpose(ps_sq[:, 1, :], most[:], prog.ident[:]).then_inc(sq_done, 1)

            @block.gpsimd
            def _(pool):
                pool.wait_ge(ready, 1)

                def body(i):
                    if not isinstance(i, int):
                        pool.wait_ge(scattered, i * 16 * U)
                    nc.gpsimd.tensor_copy(now[:], cols_of(pos_u, i, s))
                    nc.gpsimd.tensor_copy(now_data[:], data[:, bass.ds(i * U, U), :])
                    pool.drain()
                    for k in range(U):
                        scatter(nc, table, now[:, k:k + 1], now_data[:, k, :], s.NP).then_inc(scattered, 16)

                rounds(pool, s, body)
                pool.wait_ge(scattered, 16 * s.NT)
                pool.dma_start(got[:], table.rearrange("(t p) f -> p t f", p=P)).then_inc(got_in, 16)


def l1_attend(prog, keep):
    nc, s, ins = prog.nc, prog.s, prog.ins
    H, HD, D, B, NT, CH, WIN, R = s.H, s.HD, s.D, s.B, s.NT, s.CH, s.WIN, s.RELS
    HV = HD + 1
    KV = D + H * HV
    trips = prog.trips
    sbk, _, _ = in_scope(nc, keep)
    prog.attended = attended = sbk("attended", [P, NT, H * HV])
    with Stage() as ctx:
        sb, psum, sem = in_scope(nc, ctx)
        row_at = sb("g_row_at", [P, 1], U32)
        eight = sb("g_eight", [P, 1], U32)
        node_at = sb("g_node_at", [P, 1], U32)
        idle = sb("g_idle", [P, 1], U32)
        win = sb("g_win", [P, 2, WIN + B], U16)
        left = sb("g_left", [P, 1])
        pick = sb("g_pick", [P, B, 2, WIN])
        picked = sb("g_picked", [P, 2, WIN])
        away = sb("g_away", [P, 2, WIN])
        source = sb("g_source", [P, 2, WIN], U32)
        kind = sb("g_kind", [P, 2, WIN])
        hot = sb("g_hot", [P, B, R], BF16)
        hot_T = sb("g_hot_T", [P, B * R // P, P], BF16)
        rel_f = sb("g_rel_f", [P, 2, P])
        rel_3 = sb("g_rel_3", [P, 3, P], BF16)
        ident16 = sb("g_ident16", [P, P], BF16)
        kv_at = sb("g_kv_at", [P, 2, B], U32)
        kv = sb("g_kv", [P, 2, B, KV])
        q_in = sb("g_q_in", [P, D])
        q_row = sb("g_q", [P, D])
        kr = sb("g_kr", [P, B, D])
        prod = sb("g_prod", [P, B, H, HD + 1])
        sc = sb("g_sc", [P, B + 1, H])
        top = sb("g_top", [P, H])
        dif = sb("g_dif", [P, B + 1, H])
        pr = sb("g_pr", [P, B + 1, H])
        pv = sb("g_pv", [P, B + 1, H * HV])
        acc = psum("g_acc", [P, 512])
        rel_ps = psum("g_rel_ps", [P, 512])
        hot_ps = psum("g_hot_ps", [P, B * R // P, P], BF16)
        kv_in = [sem(f"g_kv_in{j}") for j in range(2)]
        win_in, node_in, cleared, rel_in = sem("g_win_in"), sem("g_node_in"), sem("g_cleared"), sem("g_rel_in")
        decoded, q_ready, hot_ready, turned, hot_copied = (sem("g_decoded"), sem("g_q_ready"), sem("g_hot_ready"),
                                                           sem("g_turned"), sem("g_hot_copied"))
        rel_ready, dif_ready, exp_done = sem("g_rel_ready"), sem("g_dif_ready"), sem("g_exp_done")
        kr_done = sem("g_kr_done")
        scaled, mask_ready, at_ready = sem("g_scaled"), sem("g_mask_ready"), sem("g_at_ready")
        pv_ready = sem("g_pv_ready")
        prod_done = sem("g_prod_done")
        summed = sem("g_summed")
        kept = sem("g_kept")
        block = ctx.enter_context(nc.Block())

        def by_parity(eng, g, body):
            with eng.If(g % 2 == 0):
                body(0)
            with eng.Else():
                body(1)

        def none(*_):
            pass

        def tiles(tag, eng, begin_tile=none, begin_chunk=none, step=none, end_tile=none):
            steps_done = eng.alloc_register(f"g_steps_done_{tag}")
            chunks_done = eng.alloc_register(f"g_chunks_done_{tag}")
            eng.reg_mov(steps_done, 0)
            eng.reg_mov(chunks_done, 0)
            with eng.Fori(0, NT) as t:
                g0 = eng.snap(steps_done, min_val=0, max_val=s.NB)
                q0 = eng.snap(chunks_done, min_val=0, max_val=s.NB)
                but_one = eng.value_load(trips[0:1, bass.ds(t, 1)], min_val=1, max_val=s.NB)
                full = eng.snap(but_one // CH)
                tail = eng.snap(but_one % CH)
                begin_tile(t, g0)

                def chunk(g, q, steps_but_one, last):
                    begin_chunk(q, t, last)
                    with eng.Fori(0, steps_but_one) as i:
                        step(g + i, i.with_bounds(min_val=0, max_val=CH - 2), q, False)
                    step(g + steps_but_one, steps_but_one, q, True)

                with eng.If(full > 0):
                    with eng.Fori(0, full) as c:
                        chunk(g0 + c * CH, q0 + c, CH - 1, False)
                g_last = eng.snap(g0 + full * CH)
                chunk(g_last, q0 + full, tail, True)
                end_tile(t, g_last + tail + 1)
                eng.reg_mov(steps_done, g_last + tail + 1)
                eng.reg_mov(chunks_done, q0 + full + 1)

        @block.sync
        def _(sp):
            sp.wait_ge(cleared, 1)
            for j in range(2):
                sp.dma_start(rel_f[j * R:(j + 1) * R, 0, j * HD:(j + 1) * HD], ins["L1_gnn_rel_w"][:, :]).then_inc(rel_in, 16)

        @block.gpsimd
        def _(pool):
            def load_node(t):
                nc.gpsimd.tensor_copy(node_at[:], prog.sorted_node[:, bass.ds(t, 1)])
                pool.drain()
                gather(nc, q_in[:], prog.q_table, node_at[:], s.NP).then_inc(node_in, 16)

            def get_window():
                gather(nc, win[:].rearrange("p k w -> p (k w)"), prog.windows, row_at[:], s.NB).then_inc(win_in, 16)

            nc.gpsimd.memset(eight[:], CH)
            pool.wait_ge(cleared, 1)
            nc.gpsimd.tensor_copy(row_at[:], prog.sorted_row[:, 0:1])
            load_node(0)
            get_window()

            def begin_chunk(q, t, last):
                pool.wait_ge(decoded, q + 1)
                if last:
                    nc.gpsimd.tensor_copy(row_at[:], prog.sorted_row[:, bass.ds(t + 1, 1)])
                else:
                    nc.gpsimd.tensor_tensor(row_at[:], row_at[:], eight[:], ALU.add)
                pool.drain()
                get_window()

            def step(g, i, q, last):
                def rows(j):
                    pool.wait_ge(kr_done, g + 1)
                    nc.gpsimd.tensor_copy(kv_at[:, j, :], source[:].rearrange("p a w -> p (a w)")
                                          [:, bass.ds((q % 2) * WIN + i * B, B)]).then_inc(at_ready, 1)
                    pool.wait_ge(at_ready, g + 1)
                    pool.wait_ge(pv_ready, g + 1)
                    nc.gpsimd.tensor_tensor(idle[:], eight[:], eight[:], ALU.add)
                    for b in range(B):
                        gather(nc, kv[:, j, b, :], prog.kv_table, kv_at[:, j, b:b + 1], s.NP).then_inc(kv_in[j], 16)

                by_parity(pool, g, rows)

            def end_tile(t, g):
                pool.wait_ge(q_ready, t + 1)
                load_node(t + 1)

            tiles("pool", pool, begin_chunk=begin_chunk, step=step, end_tile=end_tile)
            pool.wait_ge(node_in, (NT + 1) * 16)

        @block.vector
        def _(dve):
            v = nc.vector
            v.memset(kv[:], 0.0)
            v.memset(top[:], 0.0).then_inc(pv_ready, 2)
            v.memset(left[:], 0.0).then_inc(kr_done, 2)
            v.memset(q_row[:], 0.0)
            v.memset(rel_f[:], 0.0)
            v.memset(pv[:], 0.0).then_inc(prod_done, 1)
            v.tensor_copy(ident16[:], prog.ident[:])
            dve.drain()
            v.memset(pick[:], 0.0).then_inc(cleared, 1)
            dve.wait_ge(rel_in, 32)
            v.tensor_scalar(rel_f[:, 0, :], rel_f[:, 0, :], 0.2, None, ALU.mult)
            dve.drain()
            for j in range(3):
                v.tensor_copy(rel_3[:, j, :], rel_f[:, j % 2, :])
                dve.drain()
                v.tensor_tensor(rel_f[:, 1 - j % 2, :], rel_f[:, j % 2, :], rel_3[:, j, :], ALU.subtract)
                dve.drain()
            v.memset(top[:], 0.0).then_inc(cleared, 1)

            def decode(q, t, fresh):
                par = q % 2
                v.tensor_copy(left[:], prog.sorted_deg[:, bass.ds(t, 1)]) if fresh else \
                    v.tensor_scalar(left[:], left[:], -float(WIN), None, ALU.add)
                dve.wait_ge(win_in, (q + 1) * 16)
                for j in range(B):
                    v.tensor_scalar(pick[:, j], win[:, :, j:j + WIN], prog.sorted_shift[:, j, bass.ds(t, 1)], None, ALU.mult)
                dve.drain()
                v.tensor_scalar(away[:].rearrange("p a w -> p (a w)")[:, bass.ds(par * WIN, WIN)], prog.bins[:, 0:WIN],
                                left[:], 2.0 * s.NP, ALU.is_ge, ALU.mult)
                v.tensor_reduce(picked[:], pick[:].rearrange("p b k w -> p k w b"), AX.X, ALU.add)
                dve.drain()
                v.tensor_copy(kind[:].rearrange("p a w -> p (a w)")[:, bass.ds(par * WIN, WIN)], picked[:, 1, :])
                v.tensor_tensor(source[:].rearrange("p a w -> p (a w)")[:, bass.ds(par * WIN, WIN)], picked[:, 0, :],
                                away[:].rearrange("p a w -> p (a w)")[:, bass.ds(par * WIN, WIN)], ALU.add).then_inc(decoded, 1)
                dve.drain()

            def one_hot(i, q):
                v.tensor_tensor(hot[:], prog.bins[:, 0:R].unsqueeze(1).to_broadcast([P, B, R]),
                                kind[:].rearrange("p a w -> p (a w)")[:, bass.ds((q % 2) * WIN + i * B, B)].unsqueeze(2)
                                .to_broadcast([P, B, R]), ALU.is_equal).then_inc(hot_ready, 1)

            decode(0, 0, True)
            one_hot(0, 0)

            def begin_tile(t, g):
                dve.drain()
                v.memset(sc[:, B, :], -1e30)
                dve.wait_ge(q_ready, t + 1)
                v.memset(dif[:], 0.0)

            def begin_chunk(q, t, last):
                decode(q + 1, t + 1 if last else t, last)

            def step(g, i, q, last):
                def work(j):
                    dve.wait_ge(kv_in[j], (g + 2) // 2 * (16 * B))
                    dve.wait_ge(rel_ready, g + 1)
                    v.tensor_tensor(kr[:].rearrange("p b (h d) -> p b h d", h=H),
                                    kv[:, j, :, 0:D].rearrange("p b (h d) -> p b h d", h=H),
                                    rel_ps[:, 0:B * HD].rearrange("p (b d) -> p b d", b=B).unsqueeze(2)
                                    .to_broadcast([P, B, H, HD]), ALU.add).then_inc(kr_done, 1)
                    dve.drain()
                    v.tensor_tensor(prod[:, :, :, 0:HD], kr[:].rearrange("p b (h d) -> p b h d", h=H),
                                    q_row[:].rearrange("p (h d) -> p h d", h=H).unsqueeze(1)
                                    .to_broadcast([P, B, H, HD]), ALU.mult).then_inc(prod_done, 1)
                    dve.drain()
                    dve.wait_ge(mask_ready, g + 1)
                    v.tensor_reduce(sc[:, 0:B, :], prod[:], AX.X, ALU.add)
                    dve.drain()
                    v.tensor_reduce(top[:], sc[:].rearrange("p b h -> p h b"), AX.X, ALU.max)
                    dve.drain()
                    v.tensor_tensor(dif[:], sc[:], top[:].unsqueeze(1).to_broadcast([P, B + 1, H]),
                                    ALU.subtract).then_inc(dif_ready, 1)
                    dve.wait_ge(turned, g + 1)
                    one_hot(0 if last else i + 1, q + 1 if last else q)
                    dve.wait_ge(summed, g + 1)
                    dve.wait_ge(exp_done, g + 1)
                    v.tensor_copy(sc[:, B, :], top[:])
                    v.tensor_tensor(pv[:, B, :].rearrange("p (h d) -> p h d", h=H),
                                    acc[:, 0:H * HV].rearrange("p (h d) -> p h d", h=H),
                                    pr[:, B, :].unsqueeze(2).to_broadcast([P, H, HV]), ALU.mult).then_inc(scaled, 1)
                    v.tensor_tensor(pv[:, 0:B, :].rearrange("p b (h d) -> p b h d", h=H),
                                    kv[:, j, :, D:KV].rearrange("p b (h d) -> p b h d", h=H),
                                    pr[:, 0:B, :].unsqueeze(3).to_broadcast([P, B, H, HV]), ALU.mult).then_inc(pv_ready, 1)

                by_parity(dve, g, work)

            tiles("dve", dve, begin_tile, begin_chunk, step)

        @block.tensor
        def _(pe):
            PAIRS = B * R // P

            def turn(g):
                pe.wait_ge(hot_ready, g + 1)
                for c in range(PAIRS):
                    m = nc.tensor.transpose(hot_ps[:, c, :], hot[:].rearrange("p b r -> p (b r)")[:, c * P:(c + 1) * P],
                                            ident16[:])
                m.then_inc(turned, 1)

            def relations(g):
                pe.wait_ge(hot_copied, g + 1)
                for c in range(PAIRS):
                    for part in range(3):
                        m = nc.tensor.matmul(rel_ps[:, c * P:(c + 1) * P], hot_T[:, c, :], rel_3[:, part, :],
                                             start=part == 0, stop=part == 2)
                m.then_inc(rel_ready, 1)

            def add_up():
                for b in range(B + 1):
                    m = nc.tensor.matmul(acc[:, 0:H * HV], prog.ident[:], pv[:, b, :], start=b == 0, stop=b == B)
                m.then_inc(summed, 1)

            pe.wait_ge(cleared, 2)
            add_up()
            turn(0)
            relations(0)

            def step(g, i, q, last):
                turn(g + 1)
                pe.wait_ge(kr_done, g + 3)
                relations(g + 1)
                pe.wait_ge(scaled, g + 1)
                pe.wait_ge(pv_ready, g + 3)
                add_up()

            def begin_tile(t, g):
                pe.wait_ge(kept, t + 1)

            tiles("pe", pe, begin_tile, step=step)

        @block.scalar
        def _(act):
            def copy_hot(g):
                act.wait_ge(turned, g + 1)
                nc.scalar.activation(hot_T[:], hot_ps[:], ACT.Copy).then_inc(hot_copied, 1)

            def write_mask(i, q):
                nc.scalar.activation(prod[:, :, :, HD], away[:].rearrange("p a w -> p (a w)")
                                     [:, bass.ds((q % 2) * WIN + i * B, B)].unsqueeze(2).to_broadcast([P, B, H]),
                                     ACT.Copy, scale=-1e26).then_inc(mask_ready, 1)

            def load_q(t, g):
                act.wait_ge(node_in, (t + 1) * 16)
                act.wait_ge(prod_done, g + 1)
                nc.scalar.activation(q_row[:], q_in[:], ACT.Copy).then_inc(q_ready, 1)

            act.wait_ge(cleared, 1)
            nc.scalar.activation(pr[:], prog.bins[:, 0:(B + 1) * H].rearrange("p (b h) -> p b h", b=B + 1),
                                 ACT.Exp, scale=0.0).then_inc(kept, 1)
            act.wait_ge(decoded, 1)
            write_mask(0, 0)
            copy_hot(0)
            load_q(0, 0)

            def step(g, i, q, last):
                act.wait_ge(dif_ready, g + 1)
                nc.scalar.activation(pr[:], dif[:], ACT.Exp).then_inc(exp_done, 1)
                write_mask(0 if last else i + 1, q + 1 if last else q)
                act.wait_ge(rel_ready, g + 1)
                copy_hot(g + 1)

            def end_tile(t, g):
                load_q(t + 1, g)
                act.wait_ge(summed, g + 1)
                nc.scalar.activation(tile_of(attended, t), acc[:, 0:H * HV], ACT.Copy).then_inc(kept, 1)

            tiles("act", act, step=step, end_tile=end_tile)


def l1_out(prog):
    nc, s, ins = prog.nc, prog.s, prog.ins
    H, HD, D, U = s.H, s.HD, s.D, s.U
    HV = HD + 1
    KV = D + H * HV
    prog.x3_table = x3_table = prog.dram("x3_table", [s.NP, D])
    with Stage() as ctx:
        sb, psum, sem = in_scope(nc, ctx)
        at = sb("f_at", [P, U], U32)
        put_at = sb("f_put_at", [P, U], U32)
        none = sb("f_none", [P, U], U32)
        nx = sb("f_nx", [P, U, 2 * D])
        kv = sb("f_kv", [P, U, KV])
        has = sb("f_has", [P, s.NT])
        hasnt = sb("f_hasnt", [P, s.NT])
        inv = sb("f_inv", [P, U, H])
        msg = sb("f_msg", [P, U, D])
        own = sb("f_own", [P, U, D])
        y = sb("f_y", [P, U, D])
        yn = sb("f_yn", [P, U, D])
        x3 = sb("f_x3", [P, U, D])
        w = sb("f_w", [P, s.DK, D])
        par = sb("f_par", [P, 3, D])
        norm = LayerNorm(prog, ctx, "f")
        rows_in = [sem(f"f_rows_in{k}") for k in range(U)]
        w_in, msg_ready, y_ready, yn_ready = sem("f_w_in"), sem("f_msg_ready"), sem("f_y_ready"), sem("f_yn_ready")
        x3_ready, stored = sem("f_x3_ready"), sem("f_stored")
        out, done, turned, run_pe, copy_cols = project(prog, ctx, "f", msg, msg_ready, w, D,
                                                       lambda pe, m: pe.wait_ge(y_ready, m))
        block = ctx.enter_context(nc.Block())

        @block.sync
        def _(sp):
            sp.dma_start(w[:], ins["L1_gnn_Wo"].rearrange("(c p) f -> p c f", p=P)).then_inc(w_in, 16)
            for j, k in enumerate(("bo", "gamma", "beta")):
                sp.dma_start(par[:, j, :], row(ins[f"L1_gnn_{k}"]).to_broadcast([P, D])).then_inc(w_in, 16)

        @block.gpsimd
        def _(pool):
            nc.gpsimd.memset(none[:], 0)

            def put(i):
                pool.wait_ge(x3_ready, i + 1)
                nc.gpsimd.tensor_tensor(put_at[:], at[:], none[:], ALU.add)
                pool.drain()
                for k in range(U):
                    scatter(nc, x3_table, put_at[:, k:k + 1], x3[:, k, :], s.NP).then_inc(stored, 16)

            def body(i):
                if not isinstance(i, int):
                    pool.wait_ge(stored, i * 16 * U)
                nc.gpsimd.tensor_copy(at[:], cols_of(prog.sorted_node, i, s))
                pool.drain()
                for k in range(U):
                    gather(nc, nx[:, k, :], prog.nx_table, at[:, k:k + 1], s.NP).then_inc(rows_in[k], 16)
                    gather(nc, kv[:, k, :], prog.kv_table, at[:, k:k + 1], s.NP).then_inc(rows_in[k], 16)
                put(i)

            rounds(pool, s, body)
            pool.wait_ge(stored, 16 * s.NT)

        @block.vector
        def _(dve):
            v = nc.vector
            v.tensor_scalar(has[:], prog.sorted_deg[:, 0:s.NT], 0.0, None, ALU.is_gt)
            v.tensor_scalar(hasnt[:], prog.sorted_deg[:, 0:s.NT], 0.0, None, ALU.is_equal)
            dve.drain()
            dve.wait_ge(w_in, 64)

            def heads(t):
                return t.rearrange("p (h d) -> p h d", h=H)

            def body(i):
                if not isinstance(i, int):
                    dve.drain()
                now = prog.attended[:, bass.ds(i * U, U), :].rearrange("p u (h d) -> p u h d", h=H)
                for k in range(U):
                    dve.wait_ge(rows_in[k], (i + 1) * 32)
                v.tensor_scalar(inv[:], now[:, :, :, HD], 1e-30, None, ALU.max)
                dve.drain()
                v.reciprocal(inv[:], inv[:])
                dve.drain()
                v.tensor_tensor(own[:].rearrange("p u (h d) -> p u h d", h=H), now[:, :, :, 0:HD],
                                inv[:].unsqueeze(3).to_broadcast([P, U, H, HD]), ALU.mult)
                dve.drain()
                one = [t[:, bass.ds(i * U, U)].unsqueeze(2).to_broadcast([P, U, D]) for t in (has, hasnt)]
                v.tensor_tensor(own[:], own[:], one[0], ALU.mult)
                v.tensor_tensor(y[:].rearrange("p u (h d) -> p u h d", h=H),
                                kv[:, :, D:KV].rearrange("p u (h d) -> p u h d", h=H)[:, :, :, 0:HD],
                                one[1].rearrange("p u (h d) -> p u h d", h=H), ALU.mult)
                dve.drain()
                for k in range(U):
                    if not isinstance(i, int):
                        dve.wait_ge(turned, (i - 1) * U + k + 1)
                    v.tensor_tensor(msg[:, k, :], own[:, k, :], y[:, k, :], ALU.add).then_inc(msg_ready, 1)
                dve.drain()
                v.tensor_tensor(own[:], nx[:, :, 0:D], par[:, 0, :].unsqueeze(1).to_broadcast([P, U, D]), ALU.add)
                dve.drain()
                for k in range(U):
                    dve.wait_ge(done, i * U + k + 1)
                    v.tensor_tensor(y[:, k, :], out[:, k % 2, 0:D], own[:, k, :], ALU.add).then_inc(y_ready, 1)
                dve.drain()
                norm.vector(dve, i, lambda k: y[:, k, :], lambda k: yn[:, k, :], yn_ready)
                dve.drain()
                v.tensor_tensor(yn[:], yn[:], par[:, 1, :].unsqueeze(1).to_broadcast([P, U, D]), ALU.mult)
                v.tensor_tensor(own[:], nx[:, :, D:2 * D], par[:, 2, :].unsqueeze(1).to_broadcast([P, U, D]), ALU.add)
                dve.drain()
                v.tensor_tensor(x3[:], yn[:], own[:], ALU.add).then_inc(x3_ready, 1)

            rounds(dve, s, body)

        @block.tensor
        def _(pe):
            pe.wait_ge(w_in, 64)
            rounds(pe, s, lambda i: run_pe(pe, i))

        @block.scalar
        def _(act):
            def body(i):
                for k in range(U):
                    copy_cols(act, i, k)
                norm.root(act, i)

            rounds(act, s, body)


def l1_gate(prog):
    nc, s, ins = prog.nc, prog.s, prog.ins
    D, U = s.D, s.U
    xs, logits = prog.x, prog.logits
    with Stage() as ctx:
        sb, psum, sem = in_scope(nc, ctx)
        xn = sb("h_xn", [P, U, D])
        w = sb("h_w", [P, s.DK, s.X])
        bias = sb("h_bias", [P, s.X])
        norm = LayerNorm(prog, ctx, "h")
        x_in, w_in, xn_ready, kept, stored = sem("h_x_in"), sem("h_w_in"), sem("h_xn_ready"), sem("h_kept"), sem("h_stored")
        out, done, turned, run_pe, copy_cols = project(prog, ctx, "h", xn, xn_ready, w, s.X,
                                                       lambda pe, m: pe.wait_ge(kept, m))
        block = ctx.enter_context(nc.Block())

        @block.sync
        def _(sp):
            sp.dma_start(w[:], ins["L1_ffn_gate_w"].rearrange("(c p) f -> p c f", p=P)).then_inc(w_in, 16)
            sp.dma_start(bias[:], row(ins["L1_ffn_gate_b"]).to_broadcast([P, s.X])).then_inc(w_in, 16)

            def body(i):
                if not isinstance(i, int):
                    sp.wait_ge(x_in, i * 16)
                sp.dma_start(xs[:, bass.ds(i * U, U), :], tile_rows(prog.x3_table, i, s)).then_inc(x_in, 16)
                sp.wait_ge(xn_ready, (i + 1) * U)
                sp.dma_start(tile_rows(prog.xn_table, i, s), xn[:]).then_inc(stored, 16)

            rounds(sp, s, body)
            sp.wait_ge(stored, 16 * s.IT)

        @block.vector
        def _(dve):
            def body(i):
                if not isinstance(i, int):
                    dve.drain()
                    dve.wait_ge(stored, i * 16)
                dve.wait_ge(x_in, (i + 1) * 16)
                norm.vector(dve, i, lambda k: tile_of(xs, i * U + k), lambda k: xn[:, k, :], xn_ready, turned)

            rounds(dve, s, body)
            norm.vector_end(dve)
            dve.wait_ge(w_in, 32)
            dve.wait_ge(kept, s.NT)
            nc.vector.tensor_tensor(logits[:], logits[:], bias[:].unsqueeze(1).to_broadcast([P, s.NT, s.X]), ALU.add)

        @block.tensor
        def _(pe):
            pe.wait_ge(w_in, 32)
            rounds(pe, s, lambda i: run_pe(pe, i))

        @block.scalar
        def _(act):
            def keep_logits(i, k):
                n = i * U + k
                act.wait_ge(done, n + 1)
                nc.scalar.activation(tile_of(logits, n), out[:, k % 2, 0:s.X], ACT.Copy).then_inc(kept, 1)

            def body(i):
                norm.root(act, i)
                for k in range(U):
                    copy_cols(act, i, k)
                    if k:
                        keep_logits(i, k - 1)
                keep_logits(i, U - 1)

            rounds(act, s, body)


def l1_combine(prog, weight, slot, y_table):
    nc, s = prog.nc, prog.s
    D, U = s.D, s.U
    xs = prog.x
    BIG = 3.4028235e38
    with Stage() as ctx:
        sb, psum, sem = in_scope(nc, ctx)
        at = sb("o_at", [P, U], U32)
        y = sb("o_y", [P, U, D])
        z = sb("o_z", [P, U, D])
        mask = sb("o_mask", [P, 3, U, D], mybir.dt.uint8)
        const = sb("o_const", [P, 3, D])
        y_in = [sem(f"o_y_in{k}") for k in range(U)]
        used, ready, stored = sem("o_used"), sem("o_ready"), sem("o_stored")
        block = ctx.enter_context(nc.Block())

        @block.gpsimd
        def _(pool):
            def body(i):
                if not isinstance(i, int):
                    pool.wait_ge(used, i)
                nc.gpsimd.tensor_copy(at[:], cols_of(slot[0], i, s).bitcast(U32))
                pool.drain()
                for k in range(U):
                    gather(nc, y[:, k, :], y_table, at[:, k:k + 1], s.GB * s.GT).then_inc(y_in[k], 16)

            rounds(pool, s, body)

        @block.vector
        def _(dve):
            v = nc.vector
            for j, c in enumerate((0.0, 1e4, -1e4)):
                v.memset(const[:, j, :], c)
            dve.drain()

            def body(i):
                if not isinstance(i, int):
                    dve.drain()
                now = xs[:, bass.ds(i * U, U), :]
                for k in range(U):
                    dve.wait_ge(y_in[k], (i + 1) * 16)
                v.tensor_tensor(z[:], y[:], weight[0][:, bass.ds(i * U, U)].unsqueeze(2).to_broadcast([P, U, D]),
                                ALU.mult).then_inc(used, 1)
                dve.drain()
                v.tensor_tensor(mask[:, 0], z[:], z[:], ALU.not_equal)
                v.tensor_scalar(mask[:, 1], z[:], BIG, None, ALU.is_gt)
                v.tensor_scalar(mask[:, 2], z[:], -BIG, None, ALU.is_lt)
                dve.drain()
                for j in range(3):
                    v.copy_predicated(z[:], mask[:, j], const[:, j, :].unsqueeze(1).to_broadcast([P, U, D]))
                    dve.drain()
                v.tensor_tensor(now, now, z[:], ALU.add).then_inc(ready, 1)

            rounds(dve, s, body)

        @block.sync
        def _(sp):
            full = s.IT - 1
            with sp.Fori(0, full) as i:
                sp.wait_ge(ready, i + 1)
                sp.dma_start(prog.out[0:full * U * P, :].rearrange("(t p) f -> p t f", p=P)[:, bass.ds(i * U, U), :],
                             xs[:, bass.ds(i * U, U), :]).then_inc(stored, 16)
            sp.wait_ge(ready, s.IT)
            rest = prog.out[full * U * P:s.N, :]
            whole = (U - 1) * P
            sp.dma_start(rest[0:whole, :].rearrange("(t p) f -> p t f", p=P), xs[:, full * U:s.NT - 1, :]).then_inc(stored, 16)
            sp.dma_start(rest[whole:whole + s.LAST, :], xs[0:s.LAST, s.NT - 1, :]).then_inc(stored, 16)
            sp.wait_ge(stored, 16 * (full + 2))


_OUT = (6250, 256)


def build(nc, ins, out, stop=None):
    prog = Program(nc, ins, out, stop)
    with Stage() as keep:
        constants(prog, keep)
        pad_inputs(prog)
        l0_tables(prog)
        if stop == "a":
            return dump(prog, prog.xt_table[0:prog.s.N, 0:prog.s.D])
        l0_attend(prog, keep)
        if stop == "b":
            return dump_x(prog)
        with Stage() as layer:
            weight, slot, slot_node, of_group = route(prog, layer, "r0", 2, prog.s.GA)
            y = mlp(prog, "m0", prog.xn_table, slot_node, of_group, prog.s.GA, prog.s.FA,
                    ins["L0_ffn_W1"], ins["L0_ffn_b1"], ins["L0_ffn_W2"], ins["L0_ffn_b2"])
            l1_tables(prog, weight, slot, y)
        if stop == "d":
            return dump_x(prog)
        if stop == "q":
            return dump(prog, prog.kv_table[0:prog.s.N, 0:prog.s.D])
        with Stage() as layer:
            edge_windows(prog)
            node_order(prog, layer)
            if stop == "o":
                return dump_x(prog)
            l1_attend(prog, layer)
            if stop == "g":
                return dump_x(prog)
            l1_out(prog)
        l1_gate(prog)
        if stop == "f":
            return dump_x(prog)
        weight, slot, slot_node, of_group = route(prog, keep, "r1", 1, prog.s.GB)
        y = mlp(prog, "m1", prog.xn_table, slot_node, of_group, prog.s.GB, prog.s.FB,
                ins["L1_ffn_w1"], ins["L1_ffn_b1"], ins["L1_ffn_w2"], ins["L1_ffn_b2"])
        l1_combine(prog, weight, slot, y)


def dump(prog, src):
    nc = prog.nc
    with Stage() as ctx:
        t = in_scope(nc, ctx)[2]("dumped")
        block = ctx.enter_context(nc.Block())

        @block.sync
        def _(sp):
            sp.dma_start(prog.out, src).then_inc(t, 16)
            sp.wait_ge(t, 16)


def dump_x(prog):
    nc, s = prog.nc, prog.s
    with Stage() as ctx:
        t = in_scope(nc, ctx)[2]("dumped")
        block = ctx.enter_context(nc.Block())

        @block.sync
        def _(sp):
            full = (s.NT - 1) * P
            sp.dma_start(prog.out[0:full, :].rearrange("(t p) f -> p t f", p=P), prog.x[:, 0:s.NT - 1, :]).then_inc(t, 16)
            sp.dma_start(prog.out[full:s.N, :], prog.x[0:s.LAST, s.NT - 1, :]).then_inc(t, 16)
            sp.wait_ge(t, 32)


def kernel(**inputs):
    import numpy as np
    import concourse.bacc as bacc
    from concourse import mybir as mb
    from concourse.bass_utils import run_bass_kernel_spmd as run

    nc = bacc.Bacc("TRN2", target_bir_lowering=False, num_devices=1)
    arrays, ins = {}, {}
    for name, a in inputs.items():
        a = np.ascontiguousarray(a)
        arrays[f"in_{name}"] = a
        ins[name] = nc.dram_tensor(f"in_{name}", a.shape, mb.dt.from_np(a.dtype), kind="ExternalInput").ap()
    out = nc.dram_tensor("out_0", _OUT, mb.dt.float32, kind="ExternalOutput").ap()
    build(nc, ins, out, STOP)
    return run(nc, [arrays], core_ids=[0]).results[0]["out_0"]


STOP = None
```

```python
from contextlib import ExitStack

import concourse.bass as bass
from concourse import mybir

ALU = mybir.AluOpType
ACT = mybir.ActivationFunctionType
AX = mybir.AxisListType
F32 = mybir.dt.float32
BF16 = mybir.dt.bfloat16
I32 = mybir.dt.int32
U32 = mybir.dt.uint32
U16 = mybir.dt.uint16

P = 128
SKIP = 1 << 20


class Shapes:

    def __init__(self, x, dst, rel_w, attn, W1a, W1b):
        self.N, self.D = x.shape
        self.E = dst.shape[0]
        self.RELS, self.HD = rel_w.shape
        self.H = attn.shape[0]
        self.NT = -(-self.N // P)
        self.NP = self.NT * P
        self.U = 7
        self.IT = self.NT // self.U
        self.LAST = self.N - (self.NT - 1) * P
        self.B = 4
        self.CH = 8
        self.WIN = self.B * self.CH
        self.EC = -(-self.E // (16 * P)) * 16
        self.EP = self.EC * P
        self.NB = self.EP // self.B
        self.DK = self.D // P
        self.X = W1a.shape[0]
        self.GT = 256
        self.FA = W1a.shape[2]
        self.FB = W1b.shape[2]
        most = (2 * self.N + self.X * (self.GT - 1)) // self.GT
        self.GA = most + most % 2
        self.CAP = -(-5 * self.N // (4 * self.X))
        self.GPE = -(-self.CAP // self.GT)
        self.GB = self.X * self.GPE
        assert self.NT == self.U * self.IT and self.D == self.H * self.HD


def columns(col, n):
    return col[:, :].unsqueeze(2).to_broadcast(n)


class Program:
    def __init__(self, nc, ins, out):
        self.nc, self.ins, self.out = nc, ins, out
        self.s = Shapes(ins["x"], ins["dst"], ins["L1_gnn_rel_w"], ins["L0_gnn_attn_l"], ins["L0_ffn_W1"], ins["L1_ffn_w1"])
        self.n_sem = 0

    def dram(self, name, shape, dt=F32):
        return self.nc.dram_tensor(name, shape, dt, kind="Internal").ap()


class Stage(ExitStack):

    def __init__(self):
        super().__init__()
        self.semaphores = []


def in_scope(nc, ctx):
    def sb(name, shape, dt=F32):
        return ctx.enter_context(nc.sbuf_tensor(name, shape, dt))

    def psum(name, shape, dt=F32):
        return ctx.enter_context(nc.psum_tensor(name, shape, dt))

    def clear():
        nc.clear_and_free_semaphores(ctx.semaphores)
        nc.all_engine_barrier()

    def sem(name):
        if not ctx.semaphores:
            ctx.callback(clear)
        ctx.semaphores.append(nc.alloc_semaphore(name))
        return ctx.semaphores[-1]

    return sb, psum, sem


def constants(prog, keep):
    nc, s = prog.nc, prog.s
    sb, _, sem = in_scope(nc, keep)
    prog.ident = ident = sb("ident", [P, P])
    prog.below = below = sb("below", [P, P])
    prog.below16 = below16 = sb("below16", [P, P], BF16)
    prog.ones16 = ones16 = sb("ones16", [P, P], BF16)
    prog.bins = bins = sb("bins", [P, P])
    prog.lane = lane = sb("lane", [P, 1])
    prog.node = node = sb("node", [P, s.NT])
    prog.node_i = node_i = sb("node_i", [P, s.NT], I32)
    prog.real = real = sb("real", [P, s.NT])
    with Stage() as ctx:
        _, _, sem = in_scope(nc, ctx)
        made = sem("const_made")
        block = ctx.enter_context(nc.Block())

        @block.gpsimd
        def _(pool):
            nc.gpsimd.memset(ident[:], 0.0)
            nc.gpsimd.memset(below[:], 1.0)
            nc.gpsimd.iota(bins[:], [[1, P]], base=0, channel_multiplier=0, allow_small_or_imprecise_dtypes=True)
            nc.gpsimd.iota(lane[:], [[0, 1]], base=0, channel_multiplier=1, allow_small_or_imprecise_dtypes=True)
            nc.gpsimd.iota(node[:], [[P, s.NT]], base=0, channel_multiplier=1, allow_small_or_imprecise_dtypes=True)
            nc.gpsimd.iota(node_i[:], [[P, s.NT]], base=0, channel_multiplier=1)
            nc.gpsimd.memset(ones16[:], 1.0)
            pool.drain()
            nc.gpsimd.affine_select(out=ident[:], in_=ident[:], compare_op=ALU.not_equal, fill=1.0, base=0,
                                    pattern=[[-1, P]], channel_multiplier=1)
            nc.gpsimd.affine_select(out=below[:], in_=below[:], compare_op=ALU.is_gt, fill=0.0, base=0,
                                    pattern=[[1, P]], channel_multiplier=-1)
            pool.drain()
            nc.gpsimd.tensor_copy(below16[:], below[:])
            nc.gpsimd.tensor_scalar(real[:], node[:], float(s.N), None, ALU.is_lt).then_inc(made, 1)

        @block.vector
        def _(dve):
            dve.wait_ge(made, 1)


class PaddedEdges:

    def __init__(self, prog, ctx):
        s = prog.s
        self.prog = prog
        sb, _, sem = in_scope(prog.nc, ctx)
        prog.edges = {k: prog.dram(f"{k}_padded", [s.EP], I32) for k in ("src", "dst", "edge_type_64")}
        self.pads = sb("pad_edges", [1, 3, s.EP - s.E], I32)
        self.made, self.copied = sem("pad_made"), sem("pad_copied")

    def vector(self, dve):
        fill = {"src": 0, "dst": self.prog.s.NP + P * 8, "edge_type_64": 0}
        for j, k in enumerate(self.prog.edges):
            self.prog.nc.vector.memset(self.pads[:, j, :], fill[k]).then_inc(self.made, 1)

    def sync(self, sp):
        s, edges = self.prog.s, self.prog.edges
        cut = 50
        for k in edges:
            sp.dma_start(edges[k][0:s.E].rearrange("(a b) -> a b", a=cut),
                         self.prog.ins[k].rearrange("(a b) -> a b", a=cut)).then_inc(self.copied, 16)
        sp.wait_ge(self.made, 3)
        for j, k in enumerate(edges):
            sp.dma_start(edges[k][s.E:s.EP].rearrange("(a b) -> a b", a=1), self.pads[:, j, :]).then_inc(self.copied, 16)

    def sync_end(self, sp):
        sp.wait_ge(self.copied, 16 * 6)


def project(prog, ctx, tag, tiles, tiles_ready, w, width, used):
    nc, s = prog.nc, prog.s
    sb, psum, sem = in_scope(nc, ctx)
    halves = -(-width // 512)
    turned = psum(f"{tag}_turned", [P, 2, 512])
    out = psum(f"{tag}_out", [P, 2, halves * 512])
    cols = sb(f"{tag}_cols", [P, 2, s.DK * P])
    turned_done, cols_ready, done = sem(f"{tag}_turned_done"), sem(f"{tag}_cols_ready"), sem(f"{tag}_done")

    def before(k):
        return 1 if k == 0 else 2

    def turn(pe, i, k):
        n = i * s.U + k
        pe.wait_ge(tiles_ready, n + 1)
        if not (isinstance(i, int) and n < 2):
            pe.wait_ge(cols_ready, n - before(k) + 1)
        for c in range(s.DK):
            m = nc.tensor.transpose(turned[:, k % 2, c * P:(c + 1) * P], tiles[:, k, c * P:(c + 1) * P], prog.ident[:])
        m.then_inc(turned_done, 1)

    def multiply(pe, i, k):
        n = i * s.U + k
        pe.wait_ge(cols_ready, n + 1)
        if not (isinstance(i, int) and n < 2):
            used(pe, n - before(k) + 1)
        for h in range(halves):
            a, b = h * 512, min(width, h * 512 + 512)
            for c in range(s.DK):
                m = nc.tensor.matmul(out[:, k % 2, a:b], cols[:, k % 2, c * P:(c + 1) * P], w[:, c, a:b],
                                     start=c == 0, stop=c == s.DK - 1)
        m.then_inc(done, 1)

    def copy_cols(act, i, k):
        n = i * s.U + k
        act.wait_ge(turned_done, n + 1)
        if not (isinstance(i, int) and n < 2):
            act.wait_ge(done, n - before(k) + 1)
        nc.scalar.activation(cols[:, k % 2, :], turned[:, k % 2, 0:s.DK * P], ACT.Copy).then_inc(cols_ready, 1)

    def run_pe(pe, i):
        for k in range(s.U):
            turn(pe, i, k)
            if k:
                multiply(pe, i, k - 1)
        multiply(pe, i, s.U - 1)

    return out, done, turned_done, run_pe, copy_cols


def rounds(eng, s, body):
    body(0)
    with eng.Fori(1, s.IT) as i:
        body(i)


class LayerNorm:

    def __init__(self, prog, ctx, tag):
        sb, _, sem = in_scope(prog.nc, ctx)
        self.nc, self.s = prog.nc, prog.s
        self.stats, self.agg = sb(f"{tag}_stats", [P, self.s.U, 6]), sb(f"{tag}_agg", [P, self.s.U, 2])
        self.inverse, self.rstd = sb(f"{tag}_inverse", [P, self.s.U]), sb(f"{tag}_rstd", [P, self.s.U])
        self.var_ready, self.rstd_ready = sem(f"{tag}_var_ready"), sem(f"{tag}_rstd_ready")

    def moments(self, k, src):
        self.nc.vector.bn_stats(self.stats[:, k, :], src)

    def vector(self, dve, i, src, dst, ready, free=None, moments=True, before=None):
        nc, s = self.nc, self.s
        if moments:
            for k in range(s.U):
                self.moments(k, src(k))
            dve.drain()
        for k in range(s.U):
            nc.vector.bn_aggr(self.agg[:, k, :], self.stats[:, k, :])
        dve.drain()
        nc.vector.tensor_scalar(self.inverse[:], self.agg[:, :, 1], 1e-5, None, ALU.add)
        dve.drain()
        nc.vector.reciprocal(self.inverse[:], self.inverse[:]).then_inc(self.var_ready, 1)
        dve.wait_ge(self.rstd_ready, i + 1)
        if before:
            before()
        for k in range(s.U):
            if free is not None and not isinstance(i, int):
                dve.wait_ge(free, (i - 1) * s.U + k + 1)
            nc.vector.tensor_scalar(dst(k), src(k), self.agg[:, k, 0:1], self.rstd[:, k:k + 1],
                                    ALU.subtract, ALU.mult).then_inc(ready, 1)

    def vector_end(self, dve):
        dve.drain()
        self.nc.vector.memset(self.inverse[:], 1.0).then_inc(self.var_ready, 1)

    def root(self, act, i):
        act.wait_ge(self.var_ready, i + 1)
        self.nc.scalar.activation(self.rstd[:], self.inverse[:], ACT.Sqrt).then_inc(self.rstd_ready, 1)


def tile_of(buf, n):
    return buf[:, n, :] if isinstance(n, int) else buf[:, bass.ds(n, 1), :].rearrange("p a f -> p (a f)")


def row(ap):
    return ap.rearrange("(a b) -> a b", a=1)


def tile_rows(table, i, s):
    return table.rearrange("(t p) f -> p t f", p=P)[:, bass.ds(i * s.U, s.U), :]


def turn_lists(prog, keep, tag, lists, dt=U32):
    nc = prog.nc
    sbk, _, _ = in_scope(nc, keep)
    m = len(lists)
    cols = sbk(f"{tag}_cols", [P, m, P], dt)
    with Stage() as ctx:
        sb, psum, sem = in_scope(nc, ctx)
        rows = sb(f"{tag}_rows", [P, m, P], I32)
        rows_f = sb(f"{tag}_rows_f", [P, m, P])
        turned = psum(f"{tag}_turned", [P, m, P])
        rows_in, cast, turn_done, ready = sem(f"{tag}_in"), sem(f"{tag}_cast"), sem(f"{tag}_turn"), sem(f"{tag}_ready")
        block = ctx.enter_context(nc.Block())

        @block.sync
        def _(sp):
            for j, l in enumerate(lists):
                sp.dma_start(rows[0:l.shape[0], j, :], l).then_inc(rows_in, 16)

        @block.vector
        def _(dve):
            nc.vector.memset(rows_f[:], 0.0)
            dve.drain()
            dve.wait_ge(rows_in, 16 * m)
            for j, l in enumerate(lists):
                nc.vector.tensor_copy(rows_f[0:l.shape[0], j, :], rows[0:l.shape[0], j, :])
            dve.drain()
            nc.vector.memset(rows[0:1, 0, 0:1], 0).then_inc(cast, 1)
            dve.wait_ge(turn_done, 1)
            nc.vector.tensor_copy(cols[:], turned[:]).then_inc(ready, 1)
            dve.wait_ge(ready, 1)

        @block.tensor
        def _(pe):
            pe.wait_ge(cast, 1)
            for j in range(m):
                t = nc.tensor.transpose(turned[:, j, :], rows_f[:, j, :], prog.ident[:])
            t.then_inc(turn_done, 1)
    return cols


def l0_tables(prog, keep):
    nc, s, ins = prog.nc, prog.s, prog.ins
    H, HD, D = s.H, s.HD, s.D
    W1 = D + 2 * H
    prog.xt_table = xt_table = prog.dram("xt_table", [s.NP, D + H])
    prog.al_table = al_table = prog.dram("al_table", [s.NP, H])
    prog.x = xs = in_scope(nc, keep)[0]("x_now", [P, s.NT, D])
    with Stage() as ctx:
        sb, psum, sem = in_scope(nc, ctx)
        edges = PaddedEdges(prog, ctx)
        cleared, tail_in = sem("a_cleared"), sem("a_tail_in")
        xn = sb("a_xn", [P, s.U, D])
        w = sb("a_w", [P, s.DK, W1])
        attn = sb("a_attn", [P, 2, D])
        prod = sb("a_prod", [P, 2, s.DK, D])
        rows = sb("a_rows", [P, s.U, W1])
        norm = LayerNorm(prog, ctx, "a")
        x_in, w_in, w_ready, xn_ready, rows_ready, stored = (
            sem("a_x_in"), sem("a_w_in"), sem("a_w_ready"), sem("a_xn_ready"), sem("a_rows_ready"), sem("a_stored"))
        out, done, turned, run_pe, copy_cols = project(prog, ctx, "a", xn, xn_ready, w, W1,
                                                       lambda pe, m: pe.wait_ge(rows_ready, m))
        block = ctx.enter_context(nc.Block())

        @block.sync
        def _(sp):
            sp.dma_start(w[:, :, 0:D], ins["L0_gnn_weight"].rearrange("(c p) f -> p c f", p=P)).then_inc(w_in, 16)
            for j, k in enumerate(("L0_gnn_attn_r", "L0_gnn_attn_l")):
                sp.dma_start(attn[:, j, :], row(ins[k].rearrange("h d -> (h d)")).to_broadcast([P, D])).then_inc(w_in, 16)
            def load(i):
                if not isinstance(i, int) or i:
                    sp.wait_ge(x_in, i * 16)
                n = s.U if i is not last else s.U - 1
                sp.dma_start(xs[:, bass.ds(i * s.U, n), :],
                             ins["x"][bass.ds(i * s.U * P, n * P), :].rearrange("(t p) f -> p t f", p=P)).then_inc(x_in, 16)

            last = s.IT - 1
            load(0)
            sp.wait_ge(cleared, 1)
            sp.dma_start(xs[0:s.LAST, s.NT - 1, :], ins["x"][(s.NT - 1) * P:s.N, :]).then_inc(tail_in, 16)
            with sp.Fori(1, last) as i:
                load(i)
            load(last)
            edges.sync(sp)

            def store(i):
                sp.wait_ge(rows_ready, (i + 1) * s.U)
                sp.dma_start(tile_rows(xt_table, i, s), rows[:, :, 0:D + H]).then_inc(stored, 16)
                sp.dma_start(tile_rows(al_table, i, s), rows[:, :, D + H:W1]).then_inc(stored, 16)

            with sp.Fori(0, s.IT) as i:
                store(i)
            sp.wait_ge(stored, 32 * s.IT)
            edges.sync_end(sp)

        @block.vector
        def _(dve):
            nc.vector.memset(xs[:, s.NT - 1, :], 0.0).then_inc(cleared, 1)
            edges.vector(dve)
            dve.wait_ge(w_in, 48)
            dve.wait_ge(tail_in, 16)
            for j in range(2):
                for c in range(s.DK):
                    nc.vector.tensor_tensor(prod[:, j, c, :], w[:, c, 0:D], attn[:, j, :], ALU.mult)
            dve.drain()
            for j in range(2):
                for c in range(s.DK):
                    nc.vector.tensor_reduce(w[:, c, D + j * H:D + j * H + H],
                                            prod[:, j, c, :].rearrange("p (h d) -> p h d", h=H), AX.X, ALU.add)
            dve.drain()
            nc.vector.tensor_copy(attn[0:1, 0, 0:1], w[0:1, 0, 0:1]).then_inc(w_ready, 1)

            def body(i):
                if not isinstance(i, int):
                    dve.drain()
                dve.wait_ge(x_in, (i + 1) * 16)
                norm.vector(dve, i, lambda k: tile_of(xs, i * s.U + k), lambda k: xn[:, k, :], xn_ready, turned)

            rounds(dve, s, body)
            norm.vector_end(dve)

        @block.tensor
        def _(pe):
            pe.wait_ge(w_ready, 1)
            rounds(pe, s, lambda i: run_pe(pe, i))

        @block.scalar
        def _(act):
            def keep(i, k):
                n = i * s.U + k
                act.wait_ge(done, n + 1)
                if k == 0 and not isinstance(i, int):
                    act.wait_ge(stored, i * 32)
                nc.scalar.activation(rows[:, k, :], out[:, k % 2, 0:W1], ACT.Copy).then_inc(rows_ready, 1)

            def body(i):
                for k in range(s.U):
                    copy_cols(act, i, k)
                    if k:
                        keep(i, k - 1)
                    if k == s.U // 2:
                        norm.root(act, i + 1)
                keep(i, s.U - 1)

            norm.root(act, 0)
            rounds(act, s, body)


def cols_of(buf, i, s):
    return buf[:, bass.ds(i * s.U, s.U)]


def gather(nc, out, table, index, rows):
    return nc.gpsimd.indirect_dma_start(out=out, out_offset=None, in_=table,
                                        in_offset=bass.IndirectOffsetOnAxis(ap=index, axis=0),
                                        bounds_check=rows - 1, oob_is_err=False)


def scatter(nc, table, index, data, rows):
    return nc.gpsimd.indirect_dma_start(out=table, out_offset=bass.IndirectOffsetOnAxis(ap=index, axis=0),
                                        in_=data, in_offset=None, bounds_check=rows - 1, oob_is_err=False)


def l0_attend(prog, keep):
    nc, s, ins = prog.nc, prog.s, prog.ins
    H, HD, D, U = s.H, s.HD, s.D, s.U
    sbk, _, _ = in_scope(nc, keep)
    xs = prog.x
    prog.logits = logits = sbk("logits", [P, s.NT, s.X])
    prog.xn_table = xn_table = prog.dram("xn_table", [s.NP, D])
    with Stage() as ctx:
        sb, psum, sem = in_scope(nc, ctx)
        ends = turn_lists(prog, ctx, "ends", [prog.edges[k][0:s.NP].rearrange("(t p) -> t p", p=P)
                                              for k in ("dst", "src")])
        ends_now = sb("b_ends_now", [P, 2, U], U32)
        xt = sb("b_xt", [P, U, D + H])
        al = sb("b_al", [P, U, H])
        z = sb("b_z", [P, U, H])
        zs = sb("b_zs", [P, U, H])
        top = sb("b_top", [P, U])
        ez = sb("b_ez", [P, U, H])
        total = sb("b_total", [P, U])
        prod = sb("b_prod", [P, U, D])
        tmp = sb("b_tmp", [P, U, HD])
        xn = sb("b_xn", [P, U, D])
        w = sb("b_w", [P, s.DK, s.X])
        bias = sb("b_bias", [P, 2, s.X])
        norm = LayerNorm(prog, ctx, "b")
        w_in = sem("b_w_in")
        rows_in = [sem(f"b_rows_in{k}") for k in range(U)]
        shifted, exp_done, rows_used = sem("b_shifted"), sem("b_exp_done"), sem("b_rows_used")
        xn_ready, kept, stored, ended = sem("b_xn_ready"), sem("b_kept"), sem("b_stored"), sem("b_ended")
        out, done, turned, run_pe, copy_cols = project(prog, ctx, "b", xn, xn_ready, w, s.X,
                                                       lambda pe, m: pe.wait_ge(kept, m))
        block = ctx.enter_context(nc.Block())

        @block.sync
        def _(sp):
            sp.dma_start(w[:], ins["L0_ffn_Wg"].rearrange("(c p) f -> p c f", p=P)).then_inc(w_in, 16)
            for j, k in enumerate(("L0_ffn_bg", "L0_ffn_bias")):
                sp.dma_start(bias[:, j, :], row(ins[k]).to_broadcast([P, s.X])).then_inc(w_in, 16)

            with sp.Fori(0, s.IT) as i:
                sp.wait_ge(xn_ready, (i + 1) * U)
                sp.dma_start(tile_rows(xn_table, i, s), xn[:]).then_inc(stored, 16)

            sp.wait_ge(stored, 16 * s.IT)

        @block.gpsimd
        def _(pool):
            def body(i):
                if not isinstance(i, int):
                    pool.wait_ge(rows_used, i)
                for j in range(2):
                    nc.gpsimd.tensor_copy(ends_now[:, j, :], ends[:, j, bass.ds(i * U, U)])
                pool.drain()
                for k in range(U):
                    gather(nc, xt[:, k, :], prog.xt_table, ends_now[:, 0, k:k + 1], s.NP).then_inc(rows_in[k], 16)
                    gather(nc, al[:, k, :], prog.al_table, ends_now[:, 1, k:k + 1], s.NP).then_inc(rows_in[k], 16)

            rounds(pool, s, body)

        @block.vector
        def _(dve):
            def body(i):
                if not isinstance(i, int):
                    dve.drain()
                for k in range(U):
                    dve.wait_ge(rows_in[k], (i + 1) * 32)
                nc.vector.tensor_tensor(z[:], xt[:, :, D:D + H], al[:], ALU.add)
                dve.drain()
                nc.vector.scalar_tensor_tensor(out=zs[:], in0=z[:], scalar=0.01, in1=z[:], op0=ALU.mult, op1=ALU.max)
                dve.drain()
                nc.vector.tensor_reduce(top[:], zs[:], AX.X, ALU.max)
                dve.drain()
                nc.vector.tensor_tensor(zs[:], zs[:], columns(top, [P, U, H]), ALU.subtract).then_inc(shifted, 1)
                dve.wait_ge(exp_done, i + 1)
                nc.vector.tensor_reduce(total[:], ez[:], AX.X, ALU.add)
                dve.drain()
                nc.vector.reciprocal(total[:], total[:])
                dve.drain()
                nc.vector.tensor_tensor(ez[:], ez[:], columns(total, [P, U, H]), ALU.mult)
                dve.drain()
                nc.vector.tensor_tensor(prod[:].rearrange("p u (h d) -> p u h d", h=H),
                                        xt[:, :, 0:D].rearrange("p u (h d) -> p u h d", h=H),
                                        ez[:].unsqueeze(3).to_broadcast([P, U, H, HD]), ALU.mult).then_inc(rows_used, 1)
                dve.drain()
                nc.vector.tensor_reduce(tmp[:], prod[:].rearrange("p u (h d) -> p u d h", h=H), AX.X, ALU.add)
                dve.drain()
                now = xs[:, bass.ds(i * U, U), :].rearrange("p u (h d) -> p u h d", h=H)
                nc.vector.tensor_tensor(now, now, tmp[:].unsqueeze(2).to_broadcast([P, U, H, HD]), ALU.add)
                dve.drain()

                def stored_xn():
                    if not isinstance(i, int):
                        dve.wait_ge(stored, i * 16)

                norm.vector(dve, i, lambda k: tile_of(xs, i * U + k), lambda k: xn[:, k, :], xn_ready, turned,
                            before=stored_xn)

            rounds(dve, s, body)
            norm.vector_end(dve)
            dve.wait_ge(w_in, 48)
            dve.wait_ge(kept, s.NT)
            for j in range(2):
                nc.vector.tensor_tensor(logits[:], logits[:], bias[:, j, :].unsqueeze(1).to_broadcast([P, s.NT, s.X]), ALU.add)
                dve.drain()
            nc.vector.memset(top[:], 0.0).then_inc(ended, 1)

        @block.tensor
        def _(pe):
            pe.wait_ge(w_in, 48)
            rounds(pe, s, lambda i: run_pe(pe, i))

        @block.scalar
        def _(act):
            def expo(i):
                act.wait_ge(shifted, i + 1)
                nc.scalar.activation(ez[:], zs[:], ACT.Exp).then_inc(exp_done, 1)

            def keep_logits(i, k):
                n = i * U + k
                act.wait_ge(done, n + 1)
                nc.scalar.activation(tile_of(logits, n), out[:, k % 2, 0:s.X], ACT.Copy).then_inc(kept, 1)

            def body(i):
                expo(i)
                norm.root(act, i)
                for k in range(U):
                    copy_cols(act, i, k)
                    if k:
                        keep_logits(i, k - 1)
                keep_logits(i, U - 1)

            rounds(act, s, body)


class EdgesAhead:

    def __init__(self, prog, ctx):
        nc, s = prog.nc, prog.s
        self.nc, self.s, self.prog = nc, s, prog
        sb, psum, sem = in_scope(nc, ctx)
        self.WW = s.WIN + s.B
        self.rows = s.EC // s.B
        self.CB = CB = 13
        self.steps = s.EC // CB
        assert s.EC % CB == 0 and self.steps % 2 == 0 and s.NP < 1 << 16 and s.RELS < 1 << 16
        prog.windows = prog.dram("edge_windows", [s.NB, 2 * self.WW], U16)
        self.lists = sb("e_lists", [P, 2, s.EC + self.WW], I32)
        self.wide = sb("e_wide", [P, self.rows, 2, self.WW], U16)
        self.dst = sb("e_dst", [P, s.EC], I32)
        self.part = sb("e_part", [P, 2, s.EC], I32)
        self.digits = sb("e_digits", [P, 2, s.EC], BF16)
        self.bins16 = sb("e_bins16", [P, P], BF16)
        self.hot_hi = sb("e_hot_hi", [P, 2, CB, s.NT], BF16)
        self.hot_lo = sb("e_hot_lo", [P, 2, CB, P], BF16)
        self.hist = psum("e_hist", [P, 512])
        self.lists_in, self.ready, self.stored, self.dst_in = sem("e_lists_in"), sem("e_ready"), sem("e_stored"), sem("e_dst_in")
        self.cleared, self.hot_ready, self.used, self.counted = (sem("e_cleared"), sem("e_hot_ready"), sem("e_used"),
                                                                 sem("e_counted"))

    def pairs(self, eng, body):
        for j in range(2):
            body(0, j)
        with eng.Fori(1, self.steps // 2) as i:
            for j in range(2):
                body(i, j)

    def sync(self, sp):
        s, edges = self.s, self.prog.edges
        EC, WW = s.EC, self.WW
        sp.dma_start(self.dst[:], edges["dst"].rearrange("(p c) -> p c", p=P)).then_inc(self.dst_in, 16)
        sp.wait_ge(self.cleared, 1)
        for j, k in enumerate(("src", "edge_type_64")):
            sp.dma_start(self.lists[:, j, 0:EC], edges[k].rearrange("(p c) -> p c", p=P)).then_inc(self.lists_in, 16)
            sp.dma_start(self.lists[0:P - 1, j, EC:EC + WW],
                         edges[k][EC:s.EP].rearrange("(p c) -> p c", c=EC)[:, 0:WW]).then_inc(self.lists_in, 16)
        sp.wait_ge(self.ready, 2 * WW // s.B)
        sp.dma_start(self.prog.windows.rearrange("(p r) f -> p (r f)", p=P),
                     self.wide[:].rearrange("p r k w -> p (r k w)")).then_inc(self.stored, 16)
        sp.wait_ge(self.stored, 16)

    def clear(self):
        v = self.nc.vector
        v.memset(self.lists[:], 0).then_inc(self.cleared, 1)
        v.tensor_copy(self.bins16[:], self.prog.bins[:])

    def scalar(self, act):
        act.wait_ge(self.lists_in, 64)
        for k in range(2):
            for j in range(0, self.WW, self.s.B):
                self.nc.scalar.activation(self.wide[:, :, k, j:j + self.s.B],
                                          self.lists[:, k, j:j + self.s.EC].rearrange("p (r b) -> p r b", b=self.s.B),
                                          ACT.Copy).then_inc(self.ready, 1)

    def vector(self, dve):
        s, v = self.s, self.nc.vector
        dve.wait_ge(self.dst_in, 16)
        v.tensor_scalar(self.part[:, 0, :], self.dst[:], 7, None, ALU.arith_shift_right)
        v.tensor_scalar(self.part[:, 1, :], self.dst[:], P - 1, None, ALU.bitwise_and)
        dve.drain()
        v.tensor_copy(self.digits[:], self.part[:])
        dve.drain()

        def body(i, j):
            g = i * 2 + j
            if not isinstance(i, int):
                dve.wait_ge(self.used, g - 1)
            for hot, d, n in ((self.hot_hi, 0, s.NT), (self.hot_lo, 1, P)):
                m = v.tensor_tensor(hot[:, j], self.bins16[:, 0:n].unsqueeze(1).to_broadcast([P, self.CB, n]),
                                    self.digits[:, d, bass.ds(g * self.CB, self.CB)].unsqueeze(2)
                                    .to_broadcast([P, self.CB, n]), ALU.is_equal)
            m.then_inc(self.hot_ready, 1)

        self.pairs(dve, body)
        dve.wait_ge(self.used, self.steps)
        v.memset(self.prog.edge_count[:], 0.0)
        dve.drain()
        v.tensor_copy(self.prog.edge_count[0:s.NT, :], self.hist[0:s.NT, 0:P]).then_inc(self.counted, 1)

    def tensor(self, pe):
        def body(i, j):
            g = i * 2 + j
            pe.wait_ge(self.hot_ready, g + 1)
            for c in range(self.CB):
                first = isinstance(i, int) and j == 0 and c == 0
                m = self.nc.tensor.matmul(self.hist[0:self.s.NT, 0:P], self.hot_hi[:, j, c, :], self.hot_lo[:, j, c, :],
                                          start=first, stop=True, skip_group_check=True)
            m.then_inc(self.used, 1)

        self.pairs(pe, body)


def route(prog, keep, tag, experts, groups, beside=None):
    nc, s = prog.nc, prog.s
    X, NT, U, GT = s.X, s.NT, s.U, s.GT
    sbk, _, _ = in_scope(nc, keep)
    weight = [sbk(f"{tag}_weight{j}", [P, NT]) for j in range(experts)]
    slot = [sbk(f"{tag}_slot{j}", [P, NT], I32) for j in range(experts)]
    of_group = sbk(f"{tag}_of_group", [1, P], I32)
    last_pair = sbk(f"{tag}_last_pair", [1, 1], I32)
    slots = groups * GT
    halves = groups * GT // P
    slot_node = prog.dram(f"{tag}_slot_node", [slots, 1], I32)
    with Stage() as ctx:
        sb, psum, sem = in_scope(nc, ctx)
        L = sb(f"{tag}_L", [P, NT, X])
        eq = sb(f"{tag}_eq", [P, NT, X])
        hot = [sb(f"{tag}_hot{j}", [P, X, NT]) for j in range(experts)]
        hot16 = sb(f"{tag}_hot16", [P, X, NT], BF16)
        best = [sb(f"{tag}_best{j}", [P, NT]) for j in range(2)]
        which = sb(f"{tag}_which", [P, NT])
        ex = sb(f"{tag}_ex", [P, NT])
        edge = sb(f"{tag}_edge", [P, X, NT])
        upto = sb(f"{tag}_upto", [P, X, NT])
        place = sb(f"{tag}_place", [P, X, NT])
        tot_i = sb(f"{tag}_tot_i", [P, X], I32)
        ng = sb(f"{tag}_ng", [P, X])
        endg = sb(f"{tag}_endg", [P, X])
        base = sb(f"{tag}_base", [P, X])
        pos = sb(f"{tag}_pos", [P, NT])
        keepm = sb(f"{tag}_keepm", [P, NT])
        scat = [sb(f"{tag}_scat{j}", [P, NT], U32) for j in range(experts)]
        now = sb(f"{tag}_now", [P, experts, U], U32)
        now_node = sb(f"{tag}_now_node", [P, U], I32)
        zeros = sb(f"{tag}_zeros", [P, slots // P], I32)
        gcmp = sb(f"{tag}_gcmp", [1, P, X])
        gex = sb(f"{tag}_gex", [1, P])
        tiles_ps = psum(f"{tag}_tiles_ps", [P, 512])
        below_ps = psum(f"{tag}_below_ps", [P, 512])
        hot_ready, counted, exp_in, exp_done = (sem(f"{tag}_hot_ready"), sem(f"{tag}_counted"), sem(f"{tag}_exp_in"),
                                                sem(f"{tag}_exp_done"))
        placed, zeroed, zero_ready, scattered = (sem(f"{tag}_placed"), sem(f"{tag}_zeroed"), sem(f"{tag}_zero_ready"),
                                                 sem(f"{tag}_scattered"))
        other = beside(prog, ctx) if beside else None
        block = ctx.enter_context(nc.Block())
        bins8 = prog.bins[:, 0:X].unsqueeze(1).to_broadcast([P, NT, X])

        @block.sync
        def _(sp):
            sp.wait_ge(zero_ready, 1)
            sp.dma_start(slot_node.rearrange("(p c) a -> p (c a)", p=P), zeros[:]).then_inc(zeroed, 16)
            if other:
                other.sync(sp)

        @block.tensor
        def _(pe):
            pe.wait_ge(hot_ready, 1)
            flat = hot16[:].rearrange("p e t -> p (e t)")
            nc.tensor.matmul(tiles_ps[:, 0:X * NT], prog.ones16[:], flat, start=True, stop=True)
            nc.tensor.matmul(below_ps[:, 0:X * NT], prog.below16[:], flat, start=True, stop=True).then_inc(counted, 1)
            if other:
                other.tensor(pe)

        @block.scalar
        def _(act):
            act.wait_ge(exp_in, 1)
            if experts == 2:
                nc.scalar.activation(pos[:], best[1][:], ACT.Exp).then_inc(exp_done, 1)
            else:
                nc.scalar.activation(eq[:], L[:], ACT.Exp).then_inc(exp_done, 1)
            if other:
                other.scalar(act)

        @block.vector
        def _(dve):
            v = nc.vector

            def step(ins):
                dve.drain()
                return ins

            def by_tile(t):
                return t[:].rearrange("p e t -> p t e")

            def per_expert(t):
                return t[:, :].unsqueeze(2).to_broadcast([P, X, NT])

            v.memset(zeros[:], 0).then_inc(zero_ready, 1)
            if other:
                other.clear()
            v.memset(edge[:], 1.0)
            v.tensor_copy(L[:], prog.logits[:])
            step(None)
            v.memset(edge[:, :, 0:1], 0.0)
            for j in range(experts):
                step(v.tensor_reduce(best[j][:], L[:], AX.X, ALU.max))
                step(v.tensor_tensor(eq[:], L[:], columns(best[j], [P, NT, X]), ALU.not_equal))
                step(v.scalar_tensor_tensor(out=eq[:], in0=eq[:], scalar=float(X), in1=bins8, op0=ALU.mult, op1=ALU.add))
                step(v.tensor_reduce(which[:], eq[:], AX.X, ALU.min))
                step(v.tensor_tensor(eq[:], bins8, columns(which, [P, NT, X]), ALU.is_equal))
                step(v.tensor_tensor(by_tile(hot[j]), eq[:], columns(prog.real, [P, NT, X]), ALU.mult))
                if experts == 2 and j == 0:
                    step(v.scalar_tensor_tensor(out=L[:], in0=eq[:], scalar=-3e38, in1=L[:], op0=ALU.mult, op1=ALU.add))
            if experts == 2:
                step(v.tensor_tensor(hot16[:], hot[0][:], hot[1][:], ALU.add))
            else:
                step(v.tensor_copy(hot16[:], hot[0][:]))
            v.memset(now_node[:], 0).then_inc(hot_ready, 1)
            if experts == 2:
                v.tensor_tensor(best[1][:], best[1][:], best[0][:], ALU.subtract).then_inc(exp_in, 1)
                dve.wait_ge(exp_done, 1)
                step(v.tensor_scalar(ex[:], pos[:], 1.0, None, ALU.add))
                step(v.reciprocal(weight[0][:], ex[:]))
                step(v.tensor_tensor(weight[1][:], pos[:], weight[0][:], ALU.mult))
            else:
                v.tensor_tensor(L[:], L[:], columns(best[0], [P, NT, X]), ALU.subtract).then_inc(exp_in, 1)
                dve.wait_ge(exp_done, 1)
                step(v.tensor_reduce(ex[:], eq[:], AX.X, ALU.add))
                step(v.reciprocal(weight[0][:], ex[:]))
            dve.wait_ge(counted, 1)
            flat = lambda t: t[:].rearrange("p e t -> p (e t)")
            step(v.tensor_tensor_scan(flat(upto), flat(edge), tiles_ps[:, 0:X * NT], 0.0, ALU.mult, ALU.add))
            step(v.tensor_tensor(flat(place), flat(upto), tiles_ps[:, 0:X * NT], ALU.subtract))
            step(v.tensor_tensor(flat(place), flat(place), below_ps[:, 0:X * NT], ALU.add))
            most = float(s.NP if experts == 2 else s.CAP)
            step(v.tensor_scalar(tot_i[:], upto[:, :, NT - 1], most, float(GT - 1), ALU.min, ALU.add))
            step(v.tensor_scalar(tot_i[:], tot_i[:], GT.bit_length() - 1, None, ALU.arith_shift_right))
            step(v.tensor_copy(ng[:], tot_i[:]))
            step(v.tensor_tensor_scan(endg[:], ng[:], ng[:], 0.0, ALU.add, ALU.bypass))
            step(v.tensor_scalar(last_pair[:], endg[0:1, X - 1:X], -1.0, None, ALU.add))
            step(v.tensor_scalar(last_pair[:], last_pair[:], 1, None, ALU.arith_shift_right))
            step(v.tensor_tensor(base[:], endg[:], ng[:], ALU.subtract))
            step(v.tensor_scalar(base[:], base[:], float(GT), None, ALU.mult))
            if experts == 2:
                step(v.tensor_tensor(place[:], place[:], per_expert(base), ALU.add))
            for j in range(experts):
                step(v.tensor_tensor(upto[:], hot[j][:], place[:], ALU.mult))
                step(v.tensor_reduce(pos[:], by_tile(upto), AX.X, ALU.add))
                if experts == 2:
                    step(v.tensor_copy(slot[j][:], pos[:]))
                    step(v.tensor_scalar(ex[:], prog.real[:], -float(SKIP), float(SKIP), ALU.mult, ALU.add))
                    step(v.tensor_tensor(scat[j][:], ex[:], pos[:], ALU.add))
                else:
                    step(v.tensor_scalar(keepm[:], pos[:], float(s.CAP), None, ALU.is_lt))
                    step(v.tensor_tensor(weight[0][:], weight[0][:], keepm[:], ALU.mult))
                    step(v.tensor_tensor(keepm[:], keepm[:], prog.real[:], ALU.mult))
                    step(v.tensor_scalar(pos[:], pos[:], float(s.CAP - 1), None, ALU.min))
                    step(v.tensor_tensor(upto[:], hot[j][:], per_expert(base), ALU.mult))
                    step(v.tensor_reduce(ex[:], by_tile(upto), AX.X, ALU.add))
                    step(v.tensor_tensor(pos[:], pos[:], ex[:], ALU.add))
                    step(v.tensor_copy(slot[j][:], pos[:]))
                    step(v.tensor_scalar(ex[:], keepm[:], -float(SKIP), float(SKIP), ALU.mult, ALU.add))
                    step(v.tensor_tensor(scat[j][:], ex[:], pos[:], ALU.add))
            step(v.tensor_tensor(gcmp[:], prog.bins[0:1, :].unsqueeze(2).to_broadcast([1, P, X]),
                                 endg[0:1, :].unsqueeze(1).to_broadcast([1, P, X]), ALU.is_ge))
            step(v.tensor_reduce(gex[:], gcmp[:], AX.X, ALU.add))
            v.tensor_scalar(of_group[:], gex[:], float(X - 1), None, ALU.min).then_inc(placed, 1)
            if other:
                other.vector(dve)

        @block.gpsimd
        def _(pool):
            pool.wait_ge(placed, 1)
            pool.wait_ge(zeroed, 16)

            def body(i):
                if not isinstance(i, int):
                    pool.wait_ge(scattered, i * 16 * U * experts)
                for j in range(experts):
                    nc.gpsimd.tensor_copy(now[:, j, :], cols_of(scat[j], i, s))
                nc.gpsimd.tensor_copy(now_node[:], cols_of(prog.node_i, i, s))
                pool.drain()
                for k in range(U):
                    for j in range(experts):
                        scatter(nc, slot_node, now[:, j, k:k + 1], now_node[:, k:k + 1], slots).then_inc(scattered, 16)

            rounds(pool, s, body)
            pool.wait_ge(scattered, 16 * U * experts * s.IT)
    return weight, slot, slot_node, of_group, last_pair


def mlp(prog, tag, table, slot_node, of_group, last_pair, groups, F, w1, b1, w2, b2):
    nc, s = prog.nc, prog.s
    D, DK, GT, X = s.D, s.DK, s.GT, s.X
    FC = F // P
    SUB = GT // P
    sub_all = groups * SUB
    y_table = prog.dram(f"{tag}_y", [groups * GT, D])
    with Stage() as ctx:
        sb, psum, sem = in_scope(nc, ctx)
        node_rows = sb(f"{tag}_node_rows", [P, P], I32)
        node_f = sb(f"{tag}_node_f", [P, P])
        nodes = sb(f"{tag}_nodes", [P, P], U32)
        b1_rows = sb(f"{tag}_b1_rows", [P, P])
        b1_cols = sb(f"{tag}_b1_cols", [P, P])
        nodes_now = sb(f"{tag}_nodes_now", [P, 2, SUB], U32)
        xg = sb(f"{tag}_xg", [P, 2, SUB, D])
        xT = sb(f"{tag}_xT", [P, 2, DK * GT])
        w1s = sb(f"{tag}_w1s", [P, 2, DK, F])
        w2s = sb(f"{tag}_w2s", [P, 2, FC, D])
        b2s = sb(f"{tag}_b2s", [P, 2, D])
        hT = sb(f"{tag}_hT", [P, 2, FC, GT])
        ys = sb(f"{tag}_ys", [P, 2, SUB, D])
        turned = psum(f"{tag}_turned", [P, 2, 512])
        hid = psum(f"{tag}_hid", [P, 4, 512])
        yp = psum(f"{tag}_yp", [P, 2, 512])
        lists_in, lists_f, lists_T, lists_ready = (sem(f"{tag}_lists_in"), sem(f"{tag}_lists_f"), sem(f"{tag}_lists_T"),
                                                   sem(f"{tag}_lists_ready"))
        w_in = [sem(f"{tag}_w_in{j}") for j in range(2)]
        x_in = [sem(f"{tag}_x_in{j}") for j in range(2)]
        y_out = [sem(f"{tag}_y_out{j}") for j in range(2)]
        turn_done, xT_ready, hid_done, h_ready = (sem(f"{tag}_turn_done"), sem(f"{tag}_xT_ready"), sem(f"{tag}_hid_done"),
                                                  sem(f"{tag}_h_ready"))
        y_done, y_ready, cleared = sem(f"{tag}_y_done"), sem(f"{tag}_y_ready"), sem(f"{tag}_cleared")
        block = ctx.enter_context(nc.Block())

        def pairs(eng, body):
            for j in range(2):
                body(0, j)
            last = eng.value_load(last_pair[0:1, 0:1], min_val=0, max_val=groups // 2 - 1)
            with eng.If(last > 0):
                with eng.Fori(1, last + 1) as i:
                    for j in range(2):
                        body(i, j)
            return last

        def later(i):
            return not isinstance(i, int)

        @block.sync
        def _(sp):
            sp.dma_start(node_rows[0:sub_all, :], slot_node.rearrange("(c p) a -> c (p a)", p=P)).then_inc(lists_in, 16)
            sp.wait_ge(cleared, 1)
            sp.dma_start(b1_rows[0:X * FC, :], b1.rearrange("e (c p) -> (e c) p", p=P)).then_inc(lists_in, 16)

            def store(i, j):
                sp.dma_start(y_table[bass.ds((i * 2 + j) * GT, GT), :].rearrange("(c p) f -> p c f", p=P),
                             ys[:, j]).then_inc(y_out[j], 16)

            def body(i, j):
                e = sp.value_load(of_group[0:1, bass.ds(i * 2 + j, 1)], min_val=0, max_val=X - 1)
                if later(i):
                    sp.wait_ge(y_ready, i * 2 + j - 1)
                    store(i - 1, j)
                sp.dma_start(w1s[:, j], w1[bass.ds(e, 1)].rearrange("a (c p) f -> p (a c) f", p=P)).then_inc(w_in[j], 16)
                sp.dma_start(w2s[:, j], w2[bass.ds(e, 1)].rearrange("a (c p) f -> p (a c) f", p=P)).then_inc(w_in[j], 16)
                sp.dma_start(b2s[:, j], b2[bass.ds(e, 1), :].to_broadcast([P, D])).then_inc(w_in[j], 16)

            last = pairs(sp, body)
            for j in range(2):
                sp.wait_ge(y_ready, last * 2 + j + 1)
                store(last, j)
            with sp.If(last < groups // 2 - 1):
                with sp.Fori(last + 1, groups // 2) as i:
                    for j in range(2):
                        store(i, j)
            for j in range(2):
                sp.wait_ge(y_out[j], 16 * (groups // 2))

        @block.gpsimd
        def _(pool):
            pool.wait_ge(lists_ready, 1)

            def body(i, j):
                if later(i):
                    pool.wait_ge(turn_done, i * 2 + j - 1)
                nc.gpsimd.tensor_copy(nodes_now[:, j, :], nodes[:, bass.ds((i * 2 + j) * SUB, SUB)])
                pool.drain()
                for c in range(SUB):
                    gather(nc, xg[:, j, c, :], table, nodes_now[:, j, c:c + 1], s.NP).then_inc(x_in[j], 16)

            pairs(pool, body)

        @block.tensor
        def _(pe):
            pe.wait_ge(lists_f, 1)
            nc.tensor.transpose(turned[:, 0, 0:P], node_f[:], prog.ident[:])
            nc.tensor.transpose(turned[:, 1, 0:P], b1_rows[:], prog.ident[:]).then_inc(lists_T, 1)
            pe.wait_ge(lists_ready, 1)

            def turn(i, j):
                pe.wait_ge(x_in[j], (i + 1) * 16 * SUB)
                if later(i):
                    pe.wait_ge(xT_ready, i * 2 + j - 1)
                for c in range(DK):
                    for t in range(SUB):
                        m = nc.tensor.transpose(turned[:, j, c * GT + t * P:c * GT + (t + 1) * P],
                                                xg[:, j, t, c * P:(c + 1) * P], prog.ident[:])
                m.then_inc(turn_done, 1)

            def first(i, j):
                g = i * 2 + j
                pe.wait_ge(xT_ready, g + 1)
                pe.wait_ge(w_in[j], (i + 1) * 48)
                for f in range(FC):
                    if later(i) or j * FC + f >= 4:
                        pe.wait_ge(h_ready, g * FC + f - 3)
                    for c in range(DK):
                        m = nc.tensor.matmul(hid[:, f % 4, 0:GT], w1s[:, j, c, f * P:(f + 1) * P],
                                             xT[:, j, c * GT:(c + 1) * GT], start=c == 0, stop=c == DK - 1)
                    m.then_inc(hid_done, 1)

            def second(i, j):
                g = i * 2 + j
                pe.wait_ge(h_ready, (g + 1) * FC)
                for t in range(SUB):
                    if later(i) or j * SUB + t >= 2:
                        pe.wait_ge(y_ready, g)
                    for f in range(FC):
                        m = nc.tensor.matmul(yp[:, t, 0:D], hT[:, j, f, t * P:(t + 1) * P], w2s[:, j, f, :],
                                             start=f == 0, stop=f == FC - 1)
                    m.then_inc(y_done, 1)

            def body(i, j):
                turn(i, j)
                if later(i) or j:
                    second(*((i, 0) if j else (i - 1, 1)))
                first(i, j)

            last = pairs(pe, body)
            second(last, 1)

        @block.scalar
        def _(act):
            act.wait_ge(lists_ready, 1)

            def body(i, j):
                g = i * 2 + j
                e = act.value_load(of_group[0:1, bass.ds(g, 1)], min_val=0, max_val=X - 1)
                act.wait_ge(turn_done, g + 1)
                if later(i):
                    act.wait_ge(hid_done, (g - 1) * FC)
                nc.scalar.activation(xT[:, j, :], turned[:, j, :], ACT.Copy).then_inc(xT_ready, 1)
                if later(i):
                    act.wait_ge(y_done, (g - 1) * SUB)
                for f in range(FC):
                    act.wait_ge(hid_done, g * FC + f + 1)
                    nc.scalar.activation(hT[:, j, f, :], hid[:, f % 4, 0:GT], ACT.Relu,
                                         bias=b1_cols[:, bass.ds(e * FC + f, 1)]).then_inc(h_ready, 1)

            pairs(act, body)

        @block.vector
        def _(dve):
            nc.vector.memset(node_f[:], 0.0)
            nc.vector.memset(b1_rows[:], 0.0).then_inc(cleared, 1)
            dve.drain()
            dve.wait_ge(lists_in, 32)
            nc.vector.tensor_copy(node_f[0:sub_all, :], node_rows[0:sub_all, :]).then_inc(lists_f, 1)
            dve.wait_ge(lists_T, 1)
            nc.vector.tensor_copy(nodes[:], turned[:, 0, 0:P])
            nc.vector.tensor_copy(b1_cols[:], turned[:, 1, 0:P])
            dve.drain()
            nc.vector.memset(node_f[:], 0.0).then_inc(lists_ready, 1)

            def body(i, j):
                g = i * 2 + j
                dve.wait_ge(w_in[j], (i + 1) * 48)
                if later(i):
                    dve.wait_ge(y_out[j], i * 16)
                for t in range(SUB):
                    dve.wait_ge(y_done, g * SUB + t + 1)
                    m = nc.vector.tensor_tensor(ys[:, j, t, :], yp[:, t, 0:D], b2s[:, j, :], ALU.add)
                m.then_inc(y_ready, 1)

            pairs(dve, body)
    return y_table


def l1_tables(prog, weight, slot, y_table):
    nc, s, ins = prog.nc, prog.s, prog.ins
    H, HD, D, U = s.H, s.HD, s.D, s.U
    HV = HD + 1
    KV = D + H * HV
    xs = prog.x
    prog.q_table = q_table = prog.dram("q_table", [s.NP, D])
    prog.kv_table = kv_table = prog.dram("kv_table", [s.NP, KV])
    prog.nx_table = nx_table = prog.dram("nx_table", [s.NP, 2 * D])
    scale = HD ** -0.5
    with Stage() as ctx:
        sb, psum, sem = in_scope(nc, ctx)
        slot_now = sb("d_slot_now", [P, 2, U], U32)
        y = sb("d_y", [P, 2, U, D])
        xn = sb("d_xn", [P, U, D])
        enh = sb("d_enh", [P, U, D])
        w = sb("d_w", [P, s.DK, 3 * D])
        bias = sb("d_bias", [P, 3 * D])
        query = sb("d_query", [P, D])
        rows = sb("d_rows", [P, U, D + KV])
        norm = LayerNorm(prog, ctx, "d")
        y_in = [sem(f"d_y_in{k}") for k in range(U)]
        w_in, w_ready, summed = sem("d_w_in"), sem("d_w_ready"), sem("d_summed")
        xn_ready, enh_ready, rows_ready, stored = sem("d_xn_ready"), sem("d_enh_ready"), sem("d_rows_ready"), sem("d_stored")
        nx_stored = sem("d_nx_stored")
        out, done, turned, run_pe, copy_cols = project(prog, ctx, "d", enh, enh_ready, w, 3 * D,
                                                       lambda pe, m: pe.wait_ge(rows_ready, m))
        block = ctx.enter_context(nc.Block())

        @block.sync
        def _(sp):
            for j, k in enumerate(("q", "k", "v")):
                sp.dma_start(w[:, :, j * D:(j + 1) * D], ins[f"L1_gnn_W{k}"].rearrange("(c p) f -> p c f", p=P)).then_inc(w_in, 16)
                sp.dma_start(bias[:, j * D:(j + 1) * D], row(ins[f"L1_gnn_b{k}"]).to_broadcast([P, D])).then_inc(w_in, 16)
            sp.dma_start(query[:], row(ins["L1_gnn_query_emb"]).to_broadcast([P, D])).then_inc(w_in, 16)

            def body(i):
                sp.wait_ge(xn_ready, (i + 1) * U)
                nx = tile_rows(nx_table, i, s)
                sp.dma_start(nx[:, :, 0:D], xn[:]).then_inc(nx_stored, 16)
                sp.dma_start(nx[:, :, D:2 * D], xs[:, bass.ds(i * U, U), :]).then_inc(nx_stored, 16)
                sp.wait_ge(rows_ready, (i + 1) * U)
                sp.dma_start(tile_rows(q_table, i, s), rows[:, :, 0:D]).then_inc(stored, 16)
                sp.dma_start(tile_rows(kv_table, i, s), rows[:, :, D:D + KV]).then_inc(stored, 16)

            rounds(sp, s, body)
            sp.wait_ge(stored, 32 * s.IT)
            sp.wait_ge(nx_stored, 32 * s.IT)

        @block.gpsimd
        def _(pool):
            def body(i):
                if not isinstance(i, int):
                    pool.wait_ge(summed, i)
                for j in range(2):
                    nc.gpsimd.tensor_copy(slot_now[:, j, :], cols_of(slot[j], i, s).bitcast(U32))
                pool.drain()
                for k in range(U):
                    for j in range(2):
                        gather(nc, y[:, j, k, :], y_table, slot_now[:, j, k:k + 1], s.GA * s.GT).then_inc(y_in[k], 16)

            rounds(pool, s, body)

        @block.vector
        def _(dve):
            nc.vector.memset(rows[:], 1.0)
            dve.drain()
            dve.wait_ge(w_in, 16 * 7)
            nc.vector.tensor_scalar(w[:, :, 0:D], w[:, :, 0:D], scale, None, ALU.mult)
            nc.vector.tensor_scalar(bias[:, 0:D], bias[:, 0:D], scale, None, ALU.mult)
            nc.vector.tensor_scalar(query[:], query[:], 0.1, None, ALU.mult)
            dve.drain()
            nc.vector.memset(enh[:], 0.0).then_inc(w_ready, 1)
            dve.wait_ge(w_ready, 1)

            def add_expert(i, k, j):
                n = i * U + k
                x = tile_of(xs, n)
                wt = weight[j][:, n:n + 1] if isinstance(n, int) else weight[j][:, bass.ds(n, 1)]
                return nc.vector.scalar_tensor_tensor(out=x, in0=y[:, j, k, :], scalar=wt, in1=x, op0=ALU.mult, op1=ALU.add)

            def first_round():
                for k in range(U):
                    dve.wait_ge(y_in[k], 32)
                for k in range(U):
                    add_expert(0, k, 0)
                dve.drain()
                for k in range(U):
                    m = add_expert(0, k, 1)
                m.then_inc(summed, 1)
                dve.drain()
                for k in range(U):
                    norm.moments(k, tile_of(xs, k))

            def body(i, last=False):
                def stored_nx():
                    if not isinstance(i, int) or i:
                        dve.wait_ge(nx_stored, i * 32)

                dve.drain()
                norm.vector(dve, i, lambda k: tile_of(xs, i * U + k), lambda k: xn[:, k, :], xn_ready, moments=False,
                            before=stored_nx)
                dve.drain()
                for k in range(U):
                    if not isinstance(i, int) or i:
                        dve.wait_ge(turned, (i - 1) * U + k + 1)
                    nc.vector.tensor_tensor(enh[:, k, :], xn[:, k, :], query[:], ALU.add).then_inc(enh_ready, 1)
                if not isinstance(i, int) or i:
                    dve.wait_ge(stored, i * 32)
                for k in range(U):
                    if not last:
                        if k:
                            dve.drain()
                            norm.moments(k - 1, tile_of(xs, (i + 1) * U + k - 1))
                        dve.wait_ge(y_in[k], (i + 2) * 32)
                        add_expert(i + 1, k, 0)
                    dve.wait_ge(done, i * U + k + 1)
                    nc.vector.tensor_tensor(rows[:, k, 0:2 * D], out[:, k % 2, 0:2 * D], bias[:, 0:2 * D], ALU.add)
                    nc.vector.tensor_tensor(rows[:, k, 2 * D:D + KV].rearrange("p (h d) -> p h d", h=H)[:, :, 0:HD],
                                            out[:, k % 2, 2 * D:3 * D].rearrange("p (h d) -> p h d", h=H),
                                            bias[:, 2 * D:3 * D].rearrange("p (h d) -> p h d", h=H), ALU.add).then_inc(rows_ready, 1)
                    if not last:
                        dve.drain()
                        m = add_expert(i + 1, k, 1)
                if not last:
                    m.then_inc(summed, 1)
                    dve.drain()
                    norm.moments(U - 1, tile_of(xs, (i + 1) * U + U - 1))

            first_round()
            body(0)
            with dve.Fori(1, s.IT - 1) as i:
                body(i)
            body(s.IT - 1, True)
            norm.vector_end(dve)

        @block.tensor
        def _(pe):
            pe.wait_ge(w_ready, 1)
            rounds(pe, s, lambda i: run_pe(pe, i))

        @block.scalar
        def _(act):
            def body(i):
                norm.root(act, i)
                for k in range(U):
                    copy_cols(act, i, k)

            rounds(act, s, body)


def node_order(prog, keep):
    nc, s = prog.nc, prog.s
    NT, U, B = s.NT, s.U, s.B
    sbk, _, _ = in_scope(nc, keep)
    prog.sorted_node = sbk("sorted_node", [P, NT + 1], U32)
    prog.sorted_node_f = sbk("sorted_node_f", [P, NT + 1])
    prog.sorted_row = sbk("sorted_row", [P, NT + 1], U32)
    prog.sorted_shift = sbk("sorted_shift", [P, B, NT + 1])
    prog.sorted_deg = sbk("sorted_deg", [P, NT + 1])
    prog.trips = trips = sbk("trips", [1, P], I32)
    table = prog.dram("sorted_table", [s.NP, 4])
    with Stage() as ctx:
        sb, psum, sem = in_scope(nc, ctx)
        stay = ctx.enter_context(Stage())
        count = prog.edge_count
        col = sb("n_col", [P, 3, P])
        with Stage() as inner:
            sb1, psum1, sem1 = in_scope(nc, inner)
            upto = sb1("n_upto", [P, P])
            first = sb1("n_first", [P, P])
            work_i = sb1("n_work_i", [P, 2, P], I32)
            blk = sb1("n_blk", [P, 3, P])
            ps_base = psum1("n_ps_base", [P, 512])
            ps_turn = psum1("n_ps_turn", [P, 3, P])
            scanned, based, ready, turn_done, done = (sem1("n_scanned"), sem1("n_based"), sem1("n_ready"),
                                                      sem1("n_turn_done"), sem1("n_end"))
            block = inner.enter_context(nc.Block())

            @block.vector
            def _(dve):
                v = nc.vector

                def step(ins):
                    dve.drain()

                step(v.tensor_tensor_scan(upto[:], count[:], count[:], 0.0, ALU.add, ALU.bypass))
                step(v.tensor_tensor(first[:], upto[:], count[:], ALU.subtract))
                v.memset(work_i[:], 0).then_inc(scanned, 1)
                dve.wait_ge(based, 1)
                step(v.tensor_scalar(first[:], first[:], ps_base[:, 0:1], None, ALU.add))
                v.tensor_copy(work_i[:, 0, :], first[:])
                step(v.tensor_copy(work_i[:, 1, :], first[:]))
                v.tensor_scalar(work_i[:, 0, :], work_i[:, 0, :], B.bit_length() - 1, None, ALU.arith_shift_right)
                step(v.tensor_scalar(work_i[:, 1, :], work_i[:, 1, :], B - 1, None, ALU.bitwise_and))
                step(v.tensor_copy(blk[:, 0:2, :], work_i[:]))
                v.tensor_copy(blk[:, 2, :], count[:]).then_inc(ready, 1)
                dve.wait_ge(turn_done, 1)
                v.tensor_copy(col[:], ps_turn[:]).then_inc(done, 1)

            @block.tensor
            def _(pe):
                pe.wait_ge(scanned, 1)
                nc.tensor.matmul(ps_base[:, 0:1], prog.below[:], upto[:, P - 1:P], start=True, stop=True).then_inc(based, 1)
                pe.wait_ge(ready, 1)
                for j in range(3):
                    m = nc.tensor.transpose(ps_turn[:, j, :], blk[:, j, :], prog.ident[:])
                m.then_inc(turn_done, 1)

        with Stage() as inner:
            sb1, psum1, sem1 = in_scope(nc, inner)
            key = sb1("n_key", [P, NT])
            blocks_i = sb1("n_blocks_i", [P, NT], I32)
            hot = sb1("n_hot", [P, P, NT], BF16)
            tiles = sb1("n_tiles", [P, P, NT])
            place = sb1("n_place", [P, P, NT])
            pos = sb1("n_pos", [P, NT])
            pos_u = sb1("n_pos_u", [P, NT], U32)
            data = sb1("n_data", [P, NT, 4])
            now = sb1("n_now", [P, U], U32)
            now_data = sb1("n_now_data", [P, U, 4])
            got = sb1("n_got", [P, NT, 4])
            square = sb1("n_square", [P, P])
            most = sb1("n_most", [P, P])
            trip_f = sb1("n_trip_f", [1, 3, P])
            trip_i = sb1("n_trip_i", [1, 2, P], I32)
            ps = psum1("n_ps", [P, 2, 2, 512])
            ps_sq = psum1("n_ps_sq", [P, 2, P])
            hot_ready, counted, taken, ready, scattered, got_in = (sem1("n_hot_r"), sem1("n_cnt"), sem1("n_taken"),
                                                                   sem1("n_ready2"), sem1("n_scattered"), sem1("n_got_in"))
            sq_ready, sq_done, trips_ready = sem1("n_sq_ready"), sem1("n_sq_done"), sem1("n_trips_ready")
            W = P * NT
            cuts = [(a, min(512, W - a)) for a in range(0, W, 512)]
            block = inner.enter_context(nc.Block())

            def flat(t):
                return t[:].rearrange("p b t -> p (b t)")

            @block.vector
            def _(dve):
                v = nc.vector

                def step(ins):
                    dve.drain()

                step(v.tensor_scalar(blocks_i[:], col[:, 2, 0:NT], float(B - 1), None, ALU.add))
                step(v.tensor_scalar(blocks_i[:], blocks_i[:], B.bit_length() - 1, None, ALU.arith_shift_right))
                step(v.tensor_scalar(key[:], blocks_i[:], float(P - 1), -1.0, ALU.min, ALU.mult))
                step(v.tensor_scalar(key[:], key[:], float(P - 1), None, ALU.add))
                v.tensor_tensor(hot[:], prog.bins[:].unsqueeze(2).to_broadcast([P, P, NT]),
                                key[:].unsqueeze(1).to_broadcast([P, P, NT]), ALU.is_equal).then_inc(hot_ready, 1)
                for n, (a, w) in enumerate(cuts):
                    dve.wait_ge(counted, n + 1)
                    v.tensor_copy(flat(tiles)[:, a:a + w], ps[:, n % 2, 0, 0:w])
                    v.tensor_copy(flat(place)[:, a:a + w], ps[:, n % 2, 1, 0:w]).then_inc(taken, 1)
                dve.drain()
                step(v.tensor_tensor(flat(place), flat(place), flat(tiles), ALU.subtract))
                step(v.tensor_tensor_scan(flat(tiles), flat(tiles), flat(tiles), 0.0, ALU.add, ALU.bypass))
                step(v.tensor_tensor(flat(place), flat(place), flat(tiles), ALU.add))
                step(v.tensor_tensor(flat(place), flat(place), flat(hot), ALU.mult))
                step(v.tensor_reduce(pos[:], place[:].rearrange("p b t -> p t b"), AX.X, ALU.add))
                step(v.tensor_copy(pos_u[:], pos[:]))
                v.tensor_copy(data[:, :, 0], prog.node[:])
                v.tensor_copy(data[:, :, 1], col[:, 0, 0:NT])
                v.tensor_copy(data[:, :, 2], col[:, 1, 0:NT])
                step(v.tensor_copy(data[:, :, 3], col[:, 2, 0:NT]))
                v.memset(square[:], 0.0).then_inc(ready, 1)
                dve.wait_ge(got_in, 16)
                dve.drain()
                v.memset(prog.sorted_node[:, NT:NT + 1], 0)
                v.tensor_copy(prog.sorted_node[:, 0:NT], got[:, :, 0])
                v.memset(prog.sorted_node_f[:, NT:NT + 1], 0.0)
                v.tensor_copy(prog.sorted_node_f[:, 0:NT], got[:, :, 0])
                v.memset(prog.sorted_row[:, NT:NT + 1], 0)
                v.tensor_copy(prog.sorted_row[:, 0:NT], got[:, :, 1])
                v.memset(prog.sorted_deg[:, NT:NT + 1], 0.0)
                v.tensor_copy(prog.sorted_deg[:, 0:NT], got[:, :, 3])
                v.memset(prog.sorted_shift[:, :, NT:NT + 1], 0.0)
                for j in range(B):
                    v.tensor_scalar(prog.sorted_shift[:, j, 0:NT], got[:, :, 2], float(j), None, ALU.is_equal)
                v.tensor_copy(square[:, 0:NT], got[:, :, 3])
                v.memset(most[:], 0.0).then_inc(sq_ready, 1)
                dve.wait_ge(sq_done, 1)
                dve.drain()
                v.tensor_reduce(most[:, 0:1], ps_sq[:, 0, :], AX.X, ALU.max).then_inc(sq_ready, 1)
                dve.wait_ge(sq_done, 2)
                shift = B.bit_length() - 1
                step(v.tensor_scalar(trip_i[:, 0, :], ps_sq[0:1, 1, :], float(B - 1), None, ALU.add))
                step(v.tensor_scalar(trip_i[:, 0, :], trip_i[:, 0, :], shift, None, ALU.arith_shift_right))
                step(v.tensor_scalar(trip_i[:, 0, :], trip_i[:, 0, :], 2, None, ALU.max))
                step(v.tensor_scalar(trip_i[:, 1, :], trip_i[:, 0, :], s.CH - 1, None, ALU.bitwise_and))
                step(v.tensor_scalar(trip_f[:, 1, :], trip_i[:, 1, :], 1.0, None, ALU.is_equal))
                step(v.tensor_tensor(trip_f[:, 0, :], trip_f[:, 1, :], trip_i[:, 0, :], ALU.add))
                step(v.tensor_scalar(trips[:], trip_f[:, 0, :], -1.0, None, ALU.add))
                v.memset(square[:], 0.0).then_inc(trips_ready, 1)

            @block.tensor
            def _(pe):
                pe.wait_ge(hot_ready, 1)
                for n, (a, w) in enumerate(cuts):
                    if n >= 2:
                        pe.wait_ge(taken, n - 1)
                    nc.tensor.matmul(ps[:, n % 2, 0, 0:w], prog.ones16[:], flat(hot)[:, a:a + w], start=True, stop=True)
                    nc.tensor.matmul(ps[:, n % 2, 1, 0:w], prog.below16[:], flat(hot)[:, a:a + w],
                                     start=True, stop=True).then_inc(counted, 1)
                pe.wait_ge(sq_ready, 1)
                nc.tensor.transpose(ps_sq[:, 0, :], square[:], prog.ident[:]).then_inc(sq_done, 1)
                pe.wait_ge(sq_ready, 2)
                nc.tensor.transpose(ps_sq[:, 1, :], most[:], prog.ident[:]).then_inc(sq_done, 1)

            @block.gpsimd
            def _(pool):
                pool.wait_ge(ready, 1)

                def body(i):
                    if not isinstance(i, int):
                        pool.wait_ge(scattered, i * 16 * U)
                    nc.gpsimd.tensor_copy(now[:], cols_of(pos_u, i, s))
                    nc.gpsimd.tensor_copy(now_data[:], data[:, bass.ds(i * U, U), :])
                    pool.drain()
                    for k in range(U):
                        scatter(nc, table, now[:, k:k + 1], now_data[:, k, :], s.NP).then_inc(scattered, 16)

                rounds(pool, s, body)
                pool.wait_ge(scattered, 16 * s.NT)
                pool.dma_start(got[:], table.rearrange("(t p) f -> p t f", p=P)).then_inc(got_in, 16)


def l1_attend(prog, keep):
    nc, s, ins = prog.nc, prog.s, prog.ins
    H, HD, D, B, NT, CH, WIN, R = s.H, s.HD, s.D, s.B, s.NT, s.CH, s.WIN, s.RELS
    HV = HD + 1
    KV = D + H * HV
    trips = prog.trips
    sbk, _, _ = in_scope(nc, keep)
    prog.attended = attended = sbk("attended", [P, NT, H * HV])
    with Stage() as ctx:
        sb, psum, sem = in_scope(nc, ctx)
        row_at = sb("g_row_at", [P, 1], U32)
        eight = sb("g_eight", [P, 1], U32)
        node_at = sb("g_node_at", [P, 1], U32)
        idle = sb("g_idle", [P, 1], U32)
        win = sb("g_win", [P, 2, WIN + B], U16)
        left = sb("g_left", [P, 1])
        pick = sb("g_pick", [P, B, 2, WIN])
        picked = sb("g_picked", [P, 2, WIN])
        away = sb("g_away", [P, 2, WIN])
        source = sb("g_source", [P, 2, WIN], U32)
        kind = sb("g_kind", [P, 2, WIN])
        hot = sb("g_hot", [P, B, R], BF16)
        hot_T = sb("g_hot_T", [P, B * R // P, P], BF16)
        rel_f = sb("g_rel_f", [P, 2, P])
        rel_3 = sb("g_rel_3", [P, 3, P], BF16)
        ident16 = sb("g_ident16", [P, P], BF16)
        kv_at = sb("g_kv_at", [P, 2, B], U32)
        kv = sb("g_kv", [P, 2, B, KV])
        q_in = sb("g_q_in", [P, D])
        q_row = sb("g_q", [P, D])
        kr = sb("g_kr", [P, B, D])
        prod = sb("g_prod", [P, B, H, HD + 1])
        sc = sb("g_sc", [P, B + 1, H])
        top = sb("g_top", [P, H])
        dif = sb("g_dif", [P, B + 1, H])
        pr = sb("g_pr", [P, B + 1, H])
        pv = sb("g_pv", [P, B + 1, H * HV])
        acc = psum("g_acc", [P, 512])
        rel_ps = psum("g_rel_ps", [P, 512])
        hot_ps = psum("g_hot_ps", [P, B * R // P, P], BF16)
        kv_in = [sem(f"g_kv_in{j}") for j in range(2)]
        win_in, node_in, cleared, rel_in = sem("g_win_in"), sem("g_node_in"), sem("g_cleared"), sem("g_rel_in")
        decoded, q_ready, hot_ready, turned, hot_copied = (sem("g_decoded"), sem("g_q_ready"), sem("g_hot_ready"),
                                                           sem("g_turned"), sem("g_hot_copied"))
        rel_ready, dif_ready, exp_done = sem("g_rel_ready"), sem("g_dif_ready"), sem("g_exp_done")
        kr_done = sem("g_kr_done")
        scaled, mask_ready, at_ready = sem("g_scaled"), sem("g_mask_ready"), sem("g_at_ready")
        pv_ready = sem("g_pv_ready")
        prod_done = sem("g_prod_done")
        summed = sem("g_summed")
        kept = sem("g_kept")
        block = ctx.enter_context(nc.Block())

        def by_parity(eng, g, body):
            with eng.If(g % 2 == 0):
                body(0)
            with eng.Else():
                body(1)

        def none(*_):
            pass

        def tiles(tag, eng, begin_tile=none, begin_chunk=none, step=none, end_tile=none):
            steps_done = eng.alloc_register(f"g_steps_done_{tag}")
            chunks_done = eng.alloc_register(f"g_chunks_done_{tag}")
            eng.reg_mov(steps_done, 0)
            eng.reg_mov(chunks_done, 0)
            with eng.Fori(0, NT) as t:
                g0 = eng.snap(steps_done, min_val=0, max_val=s.NB)
                q0 = eng.snap(chunks_done, min_val=0, max_val=s.NB)
                but_one = eng.value_load(trips[0:1, bass.ds(t, 1)], min_val=1, max_val=s.NB)
                full = eng.snap(but_one // CH)
                tail = eng.snap(but_one % CH)
                begin_tile(t, g0)

                def chunk(g, q, steps_but_one, last):
                    begin_chunk(q, t, last)
                    with eng.Fori(0, steps_but_one) as i:
                        step(g + i, i.with_bounds(min_val=0, max_val=CH - 2), q, False)
                    step(g + steps_but_one, steps_but_one, q, True)

                with eng.If(full > 0):
                    with eng.Fori(0, full) as c:
                        chunk(g0 + c * CH, q0 + c, CH - 1, False)
                g_last = eng.snap(g0 + full * CH)
                chunk(g_last, q0 + full, tail, True)
                end_tile(t, g_last + tail + 1)
                eng.reg_mov(steps_done, g_last + tail + 1)
                eng.reg_mov(chunks_done, q0 + full + 1)

        @block.sync
        def _(sp):
            sp.wait_ge(cleared, 1)
            for j in range(2):
                sp.dma_start(rel_f[j * R:(j + 1) * R, 0, j * HD:(j + 1) * HD], ins["L1_gnn_rel_w"][:, :]).then_inc(rel_in, 16)

        @block.gpsimd
        def _(pool):
            def load_node(t):
                nc.gpsimd.tensor_copy(node_at[:], prog.sorted_node[:, bass.ds(t, 1)])
                pool.drain()
                gather(nc, q_in[:], prog.q_table, node_at[:], s.NP).then_inc(node_in, 16)

            def get_window():
                gather(nc, win[:].rearrange("p k w -> p (k w)"), prog.windows, row_at[:], s.NB).then_inc(win_in, 16)

            nc.gpsimd.memset(eight[:], CH)
            pool.wait_ge(cleared, 1)
            nc.gpsimd.tensor_copy(row_at[:], prog.sorted_row[:, 0:1])
            load_node(0)
            get_window()

            def begin_chunk(q, t, last):
                pool.wait_ge(decoded, q + 1)
                if last:
                    nc.gpsimd.tensor_copy(row_at[:], prog.sorted_row[:, bass.ds(t + 1, 1)])
                else:
                    nc.gpsimd.tensor_tensor(row_at[:], row_at[:], eight[:], ALU.add)
                pool.drain()
                get_window()

            def step(g, i, q, last):
                def rows(j):
                    pool.wait_ge(kr_done, g + 1)
                    nc.gpsimd.tensor_copy(kv_at[:, j, :], source[:].rearrange("p a w -> p (a w)")
                                          [:, bass.ds((q % 2) * WIN + i * B, B)]).then_inc(at_ready, 1)
                    pool.wait_ge(at_ready, g + 1)
                    pool.wait_ge(pv_ready, g + 1)
                    nc.gpsimd.tensor_tensor(idle[:], eight[:], eight[:], ALU.add)
                    for b in range(B):
                        gather(nc, kv[:, j, b, :], prog.kv_table, kv_at[:, j, b:b + 1], s.NP).then_inc(kv_in[j], 16)

                by_parity(pool, g, rows)

            def end_tile(t, g):
                pool.wait_ge(q_ready, t + 1)
                load_node(t + 1)

            tiles("pool", pool, begin_chunk=begin_chunk, step=step, end_tile=end_tile)
            pool.wait_ge(node_in, (NT + 1) * 16)

        @block.vector
        def _(dve):
            v = nc.vector
            v.memset(kv[:], 0.0)
            v.memset(top[:], 0.0).then_inc(pv_ready, 2)
            v.memset(left[:], 0.0).then_inc(kr_done, 2)
            v.memset(q_row[:], 0.0)
            v.memset(rel_f[:], 0.0)
            v.memset(pv[:], 0.0).then_inc(prod_done, 1)
            v.tensor_copy(ident16[:], prog.ident[:])
            dve.drain()
            v.memset(pick[:], 0.0).then_inc(cleared, 1)
            dve.wait_ge(rel_in, 32)
            v.tensor_scalar(rel_f[:, 0, :], rel_f[:, 0, :], 0.2, None, ALU.mult)
            dve.drain()
            for j in range(3):
                v.tensor_copy(rel_3[:, j, :], rel_f[:, j % 2, :])
                dve.drain()
                v.tensor_tensor(rel_f[:, 1 - j % 2, :], rel_f[:, j % 2, :], rel_3[:, j, :], ALU.subtract)
                dve.drain()
            v.memset(top[:], 0.0).then_inc(cleared, 1)

            def decode(q, t, fresh):
                par = q % 2
                v.tensor_copy(left[:], prog.sorted_deg[:, bass.ds(t, 1)]) if fresh else \
                    v.tensor_scalar(left[:], left[:], -float(WIN), None, ALU.add)
                dve.wait_ge(win_in, (q + 1) * 16)
                for j in range(B):
                    v.tensor_scalar(pick[:, j], win[:, :, j:j + WIN], prog.sorted_shift[:, j, bass.ds(t, 1)], None, ALU.mult)
                dve.drain()
                v.tensor_scalar(away[:].rearrange("p a w -> p (a w)")[:, bass.ds(par * WIN, WIN)], prog.bins[:, 0:WIN],
                                left[:], 2.0 * s.NP, ALU.is_ge, ALU.mult)
                v.tensor_reduce(picked[:], pick[:].rearrange("p b k w -> p k w b"), AX.X, ALU.add)
                dve.drain()
                v.tensor_copy(kind[:].rearrange("p a w -> p (a w)")[:, bass.ds(par * WIN, WIN)], picked[:, 1, :])
                v.tensor_tensor(source[:].rearrange("p a w -> p (a w)")[:, bass.ds(par * WIN, WIN)], picked[:, 0, :],
                                away[:].rearrange("p a w -> p (a w)")[:, bass.ds(par * WIN, WIN)], ALU.add).then_inc(decoded, 1)
                dve.drain()

            def one_hot(i, q):
                v.tensor_tensor(hot[:], prog.bins[:, 0:R].unsqueeze(1).to_broadcast([P, B, R]),
                                kind[:].rearrange("p a w -> p (a w)")[:, bass.ds((q % 2) * WIN + i * B, B)].unsqueeze(2)
                                .to_broadcast([P, B, R]), ALU.is_equal).then_inc(hot_ready, 1)

            decode(0, 0, True)
            one_hot(0, 0)

            def begin_tile(t, g):
                dve.drain()
                dve.wait_ge(q_ready, t + 1)
                v.memset(sc[:, B, :], -1e30)

            def begin_chunk(q, t, last):
                decode(q + 1, t + 1 if last else t, last)

            def step(g, i, q, last):
                def work(j):
                    dve.wait_ge(kv_in[j], (g + 2) // 2 * (16 * B))
                    dve.wait_ge(rel_ready, g + 1)
                    v.tensor_tensor(kr[:].rearrange("p b (h d) -> p b h d", h=H),
                                    kv[:, j, :, 0:D].rearrange("p b (h d) -> p b h d", h=H),
                                    rel_ps[:, 0:B * HD].rearrange("p (b d) -> p b d", b=B).unsqueeze(2)
                                    .to_broadcast([P, B, H, HD]), ALU.add).then_inc(kr_done, 1)
                    dve.drain()
                    v.tensor_tensor(prod[:, :, :, 0:HD], kr[:].rearrange("p b (h d) -> p b h d", h=H),
                                    q_row[:].rearrange("p (h d) -> p h d", h=H).unsqueeze(1)
                                    .to_broadcast([P, B, H, HD]), ALU.mult).then_inc(prod_done, 1)
                    dve.drain()
                    dve.wait_ge(mask_ready, g + 1)
                    v.tensor_reduce(sc[:, 0:B, :], prod[:], AX.X, ALU.add)
                    dve.drain()
                    v.tensor_reduce(top[:], sc[:].rearrange("p b h -> p h b"), AX.X, ALU.max)
                    dve.drain()
                    v.tensor_tensor(dif[:], sc[:], top[:].unsqueeze(1).to_broadcast([P, B + 1, H]),
                                    ALU.subtract).then_inc(dif_ready, 1)
                    dve.wait_ge(turned, g + 1)
                    one_hot(0 if last else i + 1, q + 1 if last else q)
                    dve.wait_ge(summed, g + 1)
                    dve.wait_ge(exp_done, g + 1)
                    v.tensor_copy(sc[:, B, :], top[:])
                    v.tensor_tensor(pv[:, 0:B, :].rearrange("p b (h d) -> p b h d", h=H),
                                    kv[:, j, :, D:KV].rearrange("p b (h d) -> p b h d", h=H),
                                    pr[:, 0:B, :].unsqueeze(3).to_broadcast([P, B, H, HV]), ALU.mult).then_inc(pv_ready, 1)

                by_parity(dve, g, work)

            tiles("dve", dve, begin_tile, begin_chunk, step)

        @block.tensor
        def _(pe):
            PAIRS = B * R // P

            def turn(g):
                pe.wait_ge(hot_ready, g + 1)
                for c in range(PAIRS):
                    m = nc.tensor.transpose(hot_ps[:, c, :], hot[:].rearrange("p b r -> p (b r)")[:, c * P:(c + 1) * P],
                                            ident16[:])
                m.then_inc(turned, 1)

            def relations(g):
                pe.wait_ge(hot_copied, g + 1)
                for c in range(PAIRS):
                    for part in range(3):
                        m = nc.tensor.matmul(rel_ps[:, c * P:(c + 1) * P], hot_T[:, c, :], rel_3[:, part, :],
                                             start=part == 0, stop=part == 2)
                m.then_inc(rel_ready, 1)

            def add_up():
                for b in range(B + 1):
                    m = nc.tensor.matmul(acc[:, 0:H * HV], prog.ident[:], pv[:, b, :], start=b == 0, stop=b == B)
                m.then_inc(summed, 1)

            pe.wait_ge(cleared, 2)
            add_up()
            turn(0)
            relations(0)

            def step(g, i, q, last):
                turn(g + 1)
                pe.wait_ge(kr_done, g + 3)
                relations(g + 1)
                pe.wait_ge(scaled, g + 1)
                pe.wait_ge(pv_ready, g + 3)
                add_up()

            def begin_tile(t, g):
                pe.wait_ge(kept, t + 1)

            tiles("pe", pe, begin_tile, step=step)

        @block.scalar
        def _(act):
            def copy_hot(g):
                act.wait_ge(turned, g + 1)
                nc.scalar.activation(hot_T[:], hot_ps[:], ACT.Copy).then_inc(hot_copied, 1)

            def write_mask(i, q):
                nc.scalar.activation(prod[:, :, :, HD], away[:].rearrange("p a w -> p (a w)")
                                     [:, bass.ds((q % 2) * WIN + i * B, B)].unsqueeze(2).to_broadcast([P, B, H]),
                                     ACT.Copy, scale=-1e26).then_inc(mask_ready, 1)

            def load_q(t, g):
                act.wait_ge(node_in, (t + 1) * 16)
                act.wait_ge(prod_done, g + 1)
                nc.scalar.activation(q_row[:], q_in[:], ACT.Copy).then_inc(q_ready, 1)

            act.wait_ge(cleared, 1)
            nc.scalar.activation(pr[:], prog.bins[:, 0:(B + 1) * H].rearrange("p (b h) -> p b h", b=B + 1),
                                 ACT.Exp, scale=0.0).then_inc(kept, 1)
            act.wait_ge(decoded, 1)
            write_mask(0, 0)
            copy_hot(0)
            load_q(0, 0)

            def step(g, i, q, last):
                act.wait_ge(dif_ready, g + 1)
                nc.scalar.activation(pr[:], dif[:], ACT.Exp).then_inc(exp_done, 1)
                write_mask(0 if last else i + 1, q + 1 if last else q)
                act.wait_ge(rel_ready, g + 1)
                copy_hot(g + 1)
                act.wait_ge(summed, g + 1)
                act.wait_ge(exp_done, g + 1)
                for hd in range(H):
                    m = nc.scalar.activation(pv[:, B, hd * HV:(hd + 1) * HV], acc[:, hd * HV:(hd + 1) * HV], ACT.Copy,
                                             scale=pr[:, B, hd:hd + 1])
                m.then_inc(scaled, 1)
                act.drain()

            def end_tile(t, g):
                load_q(t + 1, g)
                act.wait_ge(summed, g + 1)
                nc.scalar.activation(tile_of(attended, t), acc[:, 0:H * HV], ACT.Copy).then_inc(kept, 1)

            tiles("act", act, step=step, end_tile=end_tile)


def l1_out(prog):
    nc, s, ins = prog.nc, prog.s, prog.ins
    H, HD, D, U = s.H, s.HD, s.D, s.U
    HV = HD + 1
    KV = D + H * HV
    prog.x3_table = x3_table = prog.dram("x3_table", [s.NP, D])
    with Stage() as ctx:
        sb, psum, sem = in_scope(nc, ctx)
        kv_at = sb("f_kv_at", [P, U], U32)
        nx_at = sb("f_nx_at", [P, U], U32)
        put_at = sb("f_put_at", [P, U], U32)
        idle = sb("f_idle", [P, 1], U32)
        nx = sb("f_nx", [P, U, 2 * D])
        kv = sb("f_kv", [P, U, KV])
        has = sb("f_has", [P, s.NT])
        hasnt = sb("f_hasnt", [P, s.NT])
        inv = sb("f_inv", [P, U, H])
        msg = sb("f_msg", [P, U, D])
        own = sb("f_own", [P, U, D])
        y = sb("f_y", [P, U, D])
        yn = sb("f_yn", [P, U, D])
        x3 = sb("f_x3", [P, U, D])
        w = sb("f_w", [P, s.DK, D])
        par = sb("f_par", [P, 3, D])
        norm = LayerNorm(prog, ctx, "f")
        kv_in = [sem(f"f_kv_in{k}") for k in range(U)]
        nx_in = [sem(f"f_nx_in{k}") for k in range(U)]
        nx_used = sem("f_nx_used")
        w_in, msg_ready, y_ready, yn_ready = sem("f_w_in"), sem("f_msg_ready"), sem("f_y_ready"), sem("f_yn_ready")
        x3_ready, stored = sem("f_x3_ready"), sem("f_stored")
        out, done, turned, run_pe, copy_cols = project(prog, ctx, "f", msg, msg_ready, w, D,
                                                       lambda pe, m: pe.wait_ge(y_ready, m))
        block = ctx.enter_context(nc.Block())

        @block.sync
        def _(sp):
            sp.dma_start(w[:], ins["L1_gnn_Wo"].rearrange("(c p) f -> p c f", p=P)).then_inc(w_in, 16)
            for j, k in enumerate(("bo", "gamma", "beta")):
                sp.dma_start(par[:, j, :], row(ins[f"L1_gnn_{k}"]).to_broadcast([P, D])).then_inc(w_in, 16)

        @block.gpsimd
        def _(pool):
            def hold():
                nc.gpsimd.tensor_tensor(idle[:], prog.sorted_node[:, 0:1], prog.sorted_node[:, 0:1], ALU.add)

            def load(table, buf, at, done, i):
                nc.gpsimd.tensor_copy(at[:], cols_of(prog.sorted_node, i, s))
                pool.drain()
                for k in range(U):
                    gather(nc, buf[:, k, :], table, at[:, k:k + 1], s.NP).then_inc(done[k], 16)

            def put(i):
                pool.wait_ge(x3_ready, i + 1)
                if not isinstance(i, int):
                    pool.wait_ge(stored, i * 16 * U)
                hold()
                nc.gpsimd.tensor_copy(put_at[:], cols_of(prog.sorted_node, i, s))
                pool.drain()
                for k in range(U):
                    scatter(nc, x3_table, put_at[:, k:k + 1], x3[:, k, :], s.NP).then_inc(stored, 16)

            def body(i):
                pool.wait_ge(msg_ready, (i + 1) * U)
                hold()
                load(prog.kv_table, kv, kv_at, kv_in, i + 1)
                pool.wait_ge(nx_used, i + 1)
                hold()
                load(prog.nx_table, nx, nx_at, nx_in, i + 1)
                put(i)

            load(prog.kv_table, kv, kv_at, kv_in, 0)
            load(prog.nx_table, nx, nx_at, nx_in, 0)
            body(0)
            with pool.Fori(1, s.IT - 1) as i:
                body(i)
            last = s.IT - 1
            pool.wait_ge(stored, last * 16 * U)
            put(last)
            pool.wait_ge(stored, 16 * s.NT)

        @block.vector
        def _(dve):
            v = nc.vector
            v.tensor_scalar(has[:], prog.sorted_deg[:, 0:s.NT], 0.0, None, ALU.is_gt)
            v.tensor_scalar(hasnt[:], prog.sorted_deg[:, 0:s.NT], 0.0, None, ALU.is_equal)
            dve.drain()
            dve.wait_ge(w_in, 64)

            def heads(t):
                return t.rearrange("p (h d) -> p h d", h=H)

            def body(i):
                if not isinstance(i, int):
                    dve.drain()
                now = prog.attended[:, bass.ds(i * U, U), :].rearrange("p u (h d) -> p u h d", h=H)
                v.tensor_scalar(inv[:], now[:, :, :, HD], 1e-30, None, ALU.max)
                dve.drain()
                v.reciprocal(inv[:], inv[:])
                dve.drain()
                v.tensor_tensor(inv[:], inv[:], has[:, bass.ds(i * U, U)].unsqueeze(2).to_broadcast([P, U, H]), ALU.mult)
                dve.drain()
                v.tensor_tensor(own[:].rearrange("p u (h d) -> p u h d", h=H), now[:, :, :, 0:HD],
                                inv[:].unsqueeze(3).to_broadcast([P, U, H, HD]), ALU.mult)
                dve.drain()
                for k in range(U):
                    dve.wait_ge(kv_in[k], (i + 1) * 16)
                for k in range(U):
                    if not isinstance(i, int):
                        dve.wait_ge(turned, (i - 1) * U + k + 1)
                    v.scalar_tensor_tensor(out=heads(msg[:, k, :]), in0=heads(kv[:, k, D:KV])[:, :, 0:HD],
                                           scalar=hasnt[:, bass.ds(i * U + k, 1)], in1=heads(own[:, k, :]),
                                           op0=ALU.mult, op1=ALU.add).then_inc(msg_ready, 1)
                dve.drain()
                for k in range(U):
                    dve.wait_ge(nx_in[k], (i + 1) * 16)
                v.tensor_tensor(own[:], nx[:, :, 0:D], par[:, 0, :].unsqueeze(1).to_broadcast([P, U, D]), ALU.add)
                dve.drain()
                for k in range(U):
                    dve.wait_ge(done, i * U + k + 1)
                    v.tensor_tensor(y[:, k, :], out[:, k % 2, 0:D], own[:, k, :], ALU.add).then_inc(y_ready, 1)
                dve.drain()
                norm.vector(dve, i, lambda k: y[:, k, :], lambda k: yn[:, k, :], yn_ready)
                dve.drain()
                v.tensor_tensor(yn[:], yn[:], par[:, 1, :].unsqueeze(1).to_broadcast([P, U, D]), ALU.mult)
                v.tensor_tensor(own[:], nx[:, :, D:2 * D], par[:, 2, :].unsqueeze(1).to_broadcast([P, U, D]),
                                ALU.add).then_inc(nx_used, 1)
                dve.drain()
                if not isinstance(i, int):
                    dve.wait_ge(stored, i * 16 * U)
                v.tensor_tensor(x3[:], yn[:], own[:], ALU.add).then_inc(x3_ready, 1)

            rounds(dve, s, body)

        @block.tensor
        def _(pe):
            pe.wait_ge(w_in, 64)
            rounds(pe, s, lambda i: run_pe(pe, i))

        @block.scalar
        def _(act):
            def body(i):
                for k in range(U):
                    copy_cols(act, i, k)
                norm.root(act, i)

            rounds(act, s, body)


def l1_gate(prog):
    nc, s, ins = prog.nc, prog.s, prog.ins
    D, U = s.D, s.U
    xs, logits = prog.x, prog.logits
    with Stage() as ctx:
        sb, psum, sem = in_scope(nc, ctx)
        xn = sb("h_xn", [P, U, D])
        w = sb("h_w", [P, s.DK, s.X])
        bias = sb("h_bias", [P, s.X])
        norm = LayerNorm(prog, ctx, "h")
        x_in, w_in, xn_ready, kept, stored = sem("h_x_in"), sem("h_w_in"), sem("h_xn_ready"), sem("h_kept"), sem("h_stored")
        out, done, turned, run_pe, copy_cols = project(prog, ctx, "h", xn, xn_ready, w, s.X,
                                                       lambda pe, m: pe.wait_ge(kept, m))
        block = ctx.enter_context(nc.Block())

        @block.sync
        def _(sp):
            sp.dma_start(w[:], ins["L1_ffn_gate_w"].rearrange("(c p) f -> p c f", p=P)).then_inc(w_in, 16)
            sp.dma_start(bias[:], row(ins["L1_ffn_gate_b"]).to_broadcast([P, s.X])).then_inc(w_in, 16)

            def load(i):
                sp.dma_start(xs[:, bass.ds(i * U, U), :], tile_rows(prog.x3_table, i, s)).then_inc(x_in, 16)

            def store(i):
                sp.wait_ge(xn_ready, (i + 1) * U)
                sp.dma_start(tile_rows(prog.xn_table, i, s), xn[:]).then_inc(stored, 16)

            load(0)
            with sp.Fori(0, s.IT - 1) as i:
                sp.wait_ge(x_in, (i + 1) * 16)
                load(i + 1)
                store(i)
            store(s.IT - 1)
            sp.wait_ge(stored, 16 * s.IT)

        @block.vector
        def _(dve):
            def body(i):
                def stored_xn():
                    if not isinstance(i, int):
                        dve.wait_ge(stored, i * 16)

                if not isinstance(i, int):
                    dve.drain()
                dve.wait_ge(x_in, (i + 1) * 16)
                norm.vector(dve, i, lambda k: tile_of(xs, i * U + k), lambda k: xn[:, k, :], xn_ready, turned,
                            before=stored_xn)

            rounds(dve, s, body)
            norm.vector_end(dve)
            dve.wait_ge(w_in, 32)
            dve.wait_ge(kept, s.NT)
            nc.vector.tensor_tensor(logits[:], logits[:], bias[:].unsqueeze(1).to_broadcast([P, s.NT, s.X]), ALU.add)

        @block.tensor
        def _(pe):
            pe.wait_ge(w_in, 32)
            rounds(pe, s, lambda i: run_pe(pe, i))

        @block.scalar
        def _(act):
            def keep_logits(i, k):
                n = i * U + k
                act.wait_ge(done, n + 1)
                nc.scalar.activation(tile_of(logits, n), out[:, k % 2, 0:s.X], ACT.Copy).then_inc(kept, 1)

            def body(i):
                norm.root(act, i)
                for k in range(U):
                    copy_cols(act, i, k)
                    if k:
                        keep_logits(i, k - 1)
                keep_logits(i, U - 1)

            rounds(act, s, body)


def l1_combine(prog, weight, slot, y_table):
    nc, s = prog.nc, prog.s
    D, U = s.D, s.U
    xs = prog.x
    BIG = 3.4028235e38
    with Stage() as ctx:
        sb, psum, sem = in_scope(nc, ctx)
        at = sb("o_at", [P, U], U32)
        y = sb("o_y", [P, U, D])
        z = sb("o_z", [P, U, D])
        mask = sb("o_mask", [P, 3, U, D], mybir.dt.uint8)
        const = sb("o_const", [P, 3, D])
        y_in = [sem(f"o_y_in{k}") for k in range(U)]
        used, ready, stored = sem("o_used"), sem("o_ready"), sem("o_stored")
        block = ctx.enter_context(nc.Block())

        @block.gpsimd
        def _(pool):
            def body(i):
                if not isinstance(i, int):
                    pool.wait_ge(used, i)
                nc.gpsimd.tensor_copy(at[:], cols_of(slot[0], i, s).bitcast(U32))
                pool.drain()
                for k in range(U):
                    gather(nc, y[:, k, :], y_table, at[:, k:k + 1], s.GB * s.GT).then_inc(y_in[k], 16)

            rounds(pool, s, body)

        @block.vector
        def _(dve):
            v = nc.vector
            for j, c in enumerate((0.0, 1e4, -1e4)):
                v.memset(const[:, j, :], c)
            dve.drain()

            def body(i):
                if not isinstance(i, int):
                    dve.drain()
                now = xs[:, bass.ds(i * U, U), :]
                for k in range(U):
                    dve.wait_ge(y_in[k], (i + 1) * 16)
                v.tensor_tensor(z[:], y[:], weight[0][:, bass.ds(i * U, U)].unsqueeze(2).to_broadcast([P, U, D]),
                                ALU.mult).then_inc(used, 1)
                dve.drain()
                v.tensor_tensor(mask[:, 0], z[:], z[:], ALU.not_equal)
                v.tensor_scalar(mask[:, 1], z[:], BIG, None, ALU.is_gt)
                v.tensor_scalar(mask[:, 2], z[:], -BIG, None, ALU.is_lt)
                dve.drain()
                for j in range(3):
                    v.copy_predicated(z[:], mask[:, j], const[:, j, :].unsqueeze(1).to_broadcast([P, U, D]))
                    dve.drain()
                v.tensor_tensor(now, now, z[:], ALU.add).then_inc(ready, 1)

            rounds(dve, s, body)

        @block.sync
        def _(sp):
            full = s.IT - 1
            with sp.Fori(0, full) as i:
                sp.wait_ge(ready, i + 1)
                sp.dma_start(prog.out[0:full * U * P, :].rearrange("(t p) f -> p t f", p=P)[:, bass.ds(i * U, U), :],
                             xs[:, bass.ds(i * U, U), :]).then_inc(stored, 16)
            sp.wait_ge(ready, s.IT)
            rest = prog.out[full * U * P:s.N, :]
            whole = (U - 1) * P
            sp.dma_start(rest[0:whole, :].rearrange("(t p) f -> p t f", p=P), xs[:, full * U:s.NT - 1, :]).then_inc(stored, 16)
            sp.dma_start(rest[whole:whole + s.LAST, :], xs[0:s.LAST, s.NT - 1, :]).then_inc(stored, 16)
            sp.wait_ge(stored, 16 * (full + 2))


_OUT = (6250, 256)


def build(nc, ins, out):
    prog = Program(nc, ins, out)
    with Stage() as keep:
        constants(prog, keep)
        prog.edge_count = in_scope(nc, keep)[0]("edge_count", [P, P])
        l0_tables(prog, keep)
        l0_attend(prog, keep)
        with Stage() as layer:
            weight, slot, slot_node, of_group, last_pair = route(prog, layer, "r0", 2, prog.s.GA, EdgesAhead)
            y = mlp(prog, "m0", prog.xn_table, slot_node, of_group, last_pair, prog.s.GA, prog.s.FA,
                    ins["L0_ffn_W1"], ins["L0_ffn_b1"], ins["L0_ffn_W2"], ins["L0_ffn_b2"])
            l1_tables(prog, weight, slot, y)
        with Stage() as layer:
            node_order(prog, layer)
            l1_attend(prog, layer)
            l1_out(prog)
        l1_gate(prog)
        weight, slot, slot_node, of_group, last_pair = route(prog, keep, "r1", 1, prog.s.GB)
        y = mlp(prog, "m1", prog.xn_table, slot_node, of_group, last_pair, prog.s.GB, prog.s.FB,
                ins["L1_ffn_w1"], ins["L1_ffn_b1"], ins["L1_ffn_w2"], ins["L1_ffn_b2"])
        l1_combine(prog, weight, slot, y)


def kernel(**inputs):
    import numpy as np
    import concourse.bacc as bacc
    from concourse import mybir as mb
    from concourse.bass_utils import run_bass_kernel_spmd as run

    nc = bacc.Bacc("TRN2", target_bir_lowering=False, num_devices=1)
    arrays, ins = {}, {}
    for name, a in inputs.items():
        a = np.ascontiguousarray(a)
        arrays[f"in_{name}"] = a
        ins[name] = nc.dram_tensor(f"in_{name}", a.shape, mb.dt.from_np(a.dtype), kind="ExternalInput").ap()
    out = nc.dram_tensor("out_0", _OUT, mb.dt.float32, kind="ExternalOutput").ap()
    build(nc, ins, out)
    return run(nc, [arrays], core_ids=[0]).results[0]["out_0"]
```
